# Optimizing a Trainium2 kernel written in Bass

```python
import numpy as np
import jax
import jax.numpy as jnp

def _softmax(x, axis=-1):
    return jax.nn.softmax(x, axis=axis)

def _gelu(x):
    return jax.nn.gelu(x, approximate=True)

def _silu(x):
    return jax.nn.silu(x)

def _sigmoid(x):
    return jax.nn.sigmoid(x)

def _layernorm(x, axis=-1, eps=1e-05):
    m = jnp.mean(x, axis=axis, keepdims=True)
    v = jnp.var(x, axis=axis, keepdims=True)
    return (x - m) / jnp.sqrt(v + eps)

def _scatter_add(tgt, idx, src, axis=0):
    return tgt.at[idx].add(src)

def _segment_sum(src, seg, n):
    return jax.ops.segment_sum(src, seg, n)
kernel_name = 'mk_seq_preln_d1_jaxref_r4_96f8ed'

def setup_inputs(seed: int=0):
    np.random.seed(seed)
    _w = jnp.asarray

    def _L0_attn_setup():
        import jax, jax.numpy as jnp
        import numpy as np
        B, T, D = (2, 512, 256)
        H = 16
        HD = D // H
        WINDOW = 128
        N_GLOBAL = 1
        SCALE = 1.0 / np.sqrt(HD)

        def _attend_mask(T):
            idx = jnp.arange(T)
            dist = jnp.abs(idx[:, None] - idx[None, :])
            attend = dist <= WINDOW
            glb = idx < N_GLOBAL
            attend = attend | glb[:, None] | glb[None, :]
            return attend
        key = jax.random.key(seed)
        ks = jax.random.split(key, 5)
        scale_w = 1.0 / np.sqrt(D)
        return {'x': jax.random.normal(ks[0], (B, T, D), dtype=jnp.float32), 'Wq': jax.random.normal(ks[1], (D, D), dtype=jnp.float32) * scale_w, 'Wk': jax.random.normal(ks[2], (D, D), dtype=jnp.float32) * scale_w, 'Wv': jax.random.normal(ks[3], (D, D), dtype=jnp.float32) * scale_w, 'Wo': jax.random.normal(ks[4], (D, D), dtype=jnp.float32) * scale_w}
    _L0_attn_in = _L0_attn_setup()

    def _L0_ffn_setup():
        import jax, jax.numpy as jnp
        import numpy as np

        def _bitlinear(x, w_latent):
            scale = jax.lax.stop_gradient(jnp.clip(jnp.mean(jnp.abs(w_latent), axis=1, keepdims=True), 1e-05, None))
            tern = jnp.clip(jnp.round(w_latent / scale), -1.0, 1.0)
            w = w_latent + jax.lax.stop_gradient(tern - w_latent)
            return x @ (w * scale).T
        key = jax.random.key(seed)
        ks = jax.random.split(key, 6)
        dim, hidden, rank = (256, 1024, 16)
        B, S = (4, 1024)
        x = jax.random.normal(ks[0], (B, S, dim), dtype=jnp.float32)
        w_fc = 0.02 * jax.random.normal(ks[1], (hidden, dim), dtype=jnp.float32)
        w_proj = 0.02 * jax.random.normal(ks[2], (dim, hidden), dtype=jnp.float32)
        u = 0.02 * jax.random.normal(ks[3], (hidden, rank), dtype=jnp.float32)
        v = 0.02 * jax.random.normal(ks[4], (rank, dim), dtype=jnp.float32)
        fast_b = jax.random.normal(ks[5], (rank, rank), dtype=jnp.float32)
        gate = jnp.float32(0.05)
        return {'x': x, 'fast_b': fast_b, 'w_fc': w_fc, 'w_proj': w_proj, 'u': u, 'v': v, 'gate': gate}
    _L0_ffn_in = _L0_ffn_setup()
    _d = {'L0_attn_x': _L0_attn_in['x'], 'L0_attn_Wq': _L0_attn_in['Wq'], 'L0_attn_Wk': _L0_attn_in['Wk'], 'L0_attn_Wv': _L0_attn_in['Wv'], 'L0_attn_Wo': _L0_attn_in['Wo'], 'L0_ffn_fast_b': _L0_ffn_in['fast_b'], 'L0_ffn_w_fc': _L0_ffn_in['w_fc'], 'L0_ffn_w_proj': _L0_ffn_in['w_proj'], 'L0_ffn_u': _L0_ffn_in['u'], 'L0_ffn_v': _L0_ffn_in['v'], 'L0_ffn_gate': _L0_ffn_in['gate']}
    _x0 = _d['L0_attn_x']
    _d['L0_attn_x'] = jax.random.normal(jax.random.fold_in(jax.random.key(seed), 1), (4, 2048, 256), dtype=_x0.dtype)
    del _x0
    return _d

def reference(L0_attn_x, L0_attn_Wq, L0_attn_Wk, L0_attn_Wv, L0_attn_Wo, L0_ffn_fast_b, L0_ffn_w_fc, L0_ffn_w_proj, L0_ffn_u, L0_ffn_v, L0_ffn_gate):

    def _L0_attn_ref(x, Wq, Wk, Wv, Wo):
        import jax, jax.numpy as jnp
        import numpy as np
        B, T, D = (2, 512, 256)
        H = 16
        HD = D // H
        WINDOW = 128
        N_GLOBAL = 1
        SCALE = 1.0 / np.sqrt(HD)

        def _attend_mask(T):
            idx = jnp.arange(T)
            dist = jnp.abs(idx[:, None] - idx[None, :])
            attend = dist <= WINDOW
            glb = idx < N_GLOBAL
            attend = attend | glb[:, None] | glb[None, :]
            return attend
        Bb, Tt, Dd = x.shape
        q = (x @ Wq.T).reshape(Bb, Tt, H, HD).transpose(0, 2, 1, 3)
        k = (x @ Wk.T).reshape(Bb, Tt, H, HD).transpose(0, 2, 1, 3)
        v = (x @ Wv.T).reshape(Bb, Tt, H, HD).transpose(0, 2, 1, 3)
        attend = _attend_mask(Tt)
        logits = jnp.einsum('bhqd,bhkd->bhqk', q, k) * SCALE
        logits = jnp.where(attend[None, None, :, :], logits, -jnp.inf)
        weights = jax.nn.softmax(logits, axis=-1)
        weights = jnp.nan_to_num(weights)
        out = jnp.einsum('bhqk,bhkd->bhqd', weights, v)
        out = out.transpose(0, 2, 1, 3).reshape(Bb, Tt, Dd)
        return out @ Wo.T

    def _L0_ffn_ref(x, fast_b, w_fc, w_proj, u, v, gate):
        import jax, jax.numpy as jnp
        import numpy as np

        def _bitlinear(x, w_latent):
            scale = jax.lax.stop_gradient(jnp.clip(jnp.mean(jnp.abs(w_latent), axis=1, keepdims=True), 1e-05, None))
            tern = jnp.clip(jnp.round(w_latent / scale), -1.0, 1.0)
            w = w_latent + jax.lax.stop_gradient(tern - w_latent)
            return x @ (w * scale).T
        h = _bitlinear(x, w_fc) + gate * (x @ v.T @ fast_b.T @ u.T)
        r = jnp.maximum(h, 0.0)
        return _bitlinear(r * r, w_proj)
    x = L0_attn_x
    x = x + _L0_attn_ref(_layernorm(x, axis=-1), L0_attn_Wq, L0_attn_Wk, L0_attn_Wv, L0_attn_Wo)
    x = x + _L0_ffn_ref(_layernorm(x, axis=-1), L0_ffn_fast_b, L0_ffn_w_fc, L0_ffn_w_proj, L0_ffn_u, L0_ffn_v, L0_ffn_gate)
    return x

_drawn_inputs = setup_inputs


def setup_inputs(seed=0):
    import zlib

    import numpy as np

    out = dict(_drawn_inputs(seed))
    spreads = {}
    factors = {'L0_ffn_fast_b': 8.0, 'L0_ffn_u': 8.0, 'L0_ffn_v': 8.0}
    for name, (base, spread) in spreads.items():
        noise = np.random.default_rng([zlib.crc32(name.encode()), seed]).standard_normal(out[name].shape)
        drawn = base * np.exp(spread * noise) if base else spread * noise
        out[name] = jnp.asarray(drawn.astype(out[name].dtype))
    for name, factor in factors.items():
        out[name] = (out[name] * factor).astype(out[name].dtype)
    return out
```

```python
from contextlib import ExitStack

import numpy as np

import concourse.bass as bass
from concourse import mybir

ACT = mybir.ActivationFunctionType
ALU = mybir.AluOpType
AX = mybir.AxisListType
F32 = mybir.dt.float32
F32R = mybir.dt.float32r
BF16 = mybir.dt.bfloat16

P = 128
B, T, D = 4, 2048, 256
H, HD = 16, 16
HID = 1024
RANK = 16
N = B * T
KT = D // P
GT = 512
TB = GT // P
G = N // GT
GB = T // GT
VW = HD + 1
VROW = H * VW
EPS = 1e-5
QSCALE = 1.0 / float(np.sqrt(HD))
NEG = -3.0e38
ROUND = 4
DMA = 16
HIGH, MID, LOW = 0, 1, 2
K_SLOTS = (HIGH, MID, LOW, HIGH, MID, HIGH)
Q_SLOTS = (HIGH, HIGH, HIGH, MID, MID, LOW)
SLOT_ROWS = len(K_SLOTS) * HD
SHIFT_ROWS = 3
NQ = 4
UPG = H // NQ
UNITS = G * UPG
UPB = GB * UPG
WIN = GT + 2 * P


class Group:

    def __init__(self, i, k):
        self.g = i * ROUND + k
        self.par, self.half = k % 2, i * (ROUND // 2) + k // 2
        self.ring, self.turn = k % 4, i * (ROUND // 4) + k // 4


def wait(eng, sem, value):
    if isinstance(value, int) and value <= 0:
        return
    eng.wait_ge(sem, value)


class Turn:

    def __init__(self, eng, sem, name, start, step=1):
        self.eng, self.sem, self.step = eng, sem, step
        self.value = eng.alloc_register(name)
        self.looped = False
        eng.reg_mov(self.value, start)

    def wait(self, value):
        self.looped = self.looped or not isinstance(value, int)
        if self.looped and isinstance(value, int):
            self.eng.wait_ge(self.sem, value)
        else:
            self.eng.wait_ge(self.sem, self.value)
            self.eng.reg_add(self.value, self.value, self.step)


def sweep(eng, body, lags):
    def fixed(it):
        return lambda lag: Group(0, it - lag) if 0 <= it - lag < G else None

    first = -(-lags // ROUND)
    for it in range(first * ROUND):
        body(fixed(it))
    with eng.Fori(first, G // ROUND) as i:
        for p in range(ROUND):
            body(lambda lag, p=p: Group(i, p - lag))
    for it in range(G, G + lags):
        body(fixed(it))


def identity(pool, tile, sem):
    pool.memset(tile, 1.0).then_inc(sem, 1)
    pool.wait_ge(sem, 1)
    pool.affine_select(out=tile, in_=tile, compare_op=ALU.is_equal, fill=0.0, base=0,
                       pattern=[[-1, P]], channel_multiplier=1).then_inc(sem, 1)


class Norm:

    STEPS = 9

    def __init__(self, nc, ctx, name):
        def sb(n, shape):
            return ctx.enter_context(nc.sbuf_tensor(f"{name}_{n}", shape, F32))
        self.name = name
        self.stats = sb("stats", [P, TB, 6])
        self.mv = sb("meanvar", [P, 2, TB, 2])
        self.ve = sb("var_eps", [P, 2, TB])
        self.sd = sb("stddev", [P, 2, TB])
        self.r0 = sb("rstd_first", [P, TB])
        self.t0 = sb("newton", [P, TB])
        self.rs = sb("rstd", [P, TB])
        self.s_step = ctx.enter_context(nc.semaphore(f"{name}_step"))
        self.s_sd = ctx.enter_context(nc.semaphore(f"{name}_sd"))
        self.s_back = ctx.enter_context(nc.semaphore(f"{name}_back"))

    def begin(self, v):
        self.stats_turn = Turn(v, self.s_step, f"{self.name}_stats_turn", 1, 3)

    def front(self, v, x, q):
        par, base = q.par, q.g * 3
        for t in range(TB):
            ins = v.bn_stats(self.stats[:, t, :], x[:, t, :])
        ins.then_inc(self.s_step, 1)
        self.stats_turn.wait(base + 1)
        for t in range(TB):
            ins = v.bn_aggr(self.mv[:, par, t, :], self.stats[:, t, :])
        ins.then_inc(self.s_step, 1)
        v.wait_ge(self.s_step, base + 2)
        v.tensor_scalar(self.ve[:, par, :], self.mv[:, par, :, 1], EPS, None, ALU.add).then_inc(self.s_step, 1)

    def root(self, a, q):
        a.wait_ge(self.s_step, q.g * 3 + 3)
        a.activation(self.sd[:, q.par, :], self.ve[:, q.par, :], ACT.Sqrt).then_inc(self.s_sd, 1)

    def back(self, v, x, xn, q):
        par, base = q.par, q.g * 6
        v.wait_ge(self.s_sd, q.g + 1)
        v.reciprocal(self.r0[:], self.sd[:, par, :]).then_inc(self.s_back, 1)
        v.wait_ge(self.s_back, base + 1)
        v.tensor_tensor(self.t0[:], self.ve[:, par, :], self.r0[:], ALU.mult).then_inc(self.s_back, 1)
        v.wait_ge(self.s_back, base + 2)
        v.tensor_tensor(self.t0[:], self.t0[:], self.r0[:], ALU.mult).then_inc(self.s_back, 1)
        v.wait_ge(self.s_back, base + 3)
        v.tensor_scalar(self.t0[:], self.t0[:], -0.5, 1.5, ALU.mult, ALU.add).then_inc(self.s_back, 1)
        v.wait_ge(self.s_back, base + 4)
        v.tensor_tensor(self.rs[:], self.t0[:], self.r0[:], ALU.mult).then_inc(self.s_back, 1)
        v.wait_ge(self.s_back, base + 5)
        for t in range(TB):
            ins = v.tensor_scalar(xn[:, t, :], x[:, t, :], self.mv[:, par, t, 0:1], self.rs[:, t:t + 1],
                                  ALU.subtract, ALU.mult)
        ins.then_inc(self.s_back, 1)

    def done(self, q):
        return q.g * 6 + 6


def three_pass(pe, out, lhs_hi, lhs_lo, rhs_hi, rhs_lo):
    n = len(lhs_hi)
    for k in range(n):
        pe.matmul(out, lhs_hi[k], rhs_hi[k], start=(k == 0), stop=False)
        pe.matmul(out, lhs_hi[k], rhs_lo[k], start=False, stop=False)
        ins = pe.matmul(out, lhs_lo[k], rhs_hi[k], start=False, stop=(k == n - 1))
    return ins


def stage_project(nc, x, weights, qk_dram, kf_dram, va_dram):
    with ExitStack() as ctx:
        def sb(name, shape, dt=F32):
            return ctx.enter_context(nc.sbuf_tensor(f"p_{name}", shape, dt))

        def sem(name):
            return ctx.enter_context(nc.semaphore(f"p_{name}"))

        ident = sb("ident", [P, P])
        w_in = sb("w_in", [P, 3, KT, D])
        wt_hi = sb("wt_hi", [P, 3, KT, D], F32R)
        wt_lo = sb("wt_lo", [P, 3, KT, D], F32R)
        xb = sb("x", [P, 2, TB, D])
        xn = sb("xn", [P, 2, TB, D])
        xt_hi = sb("xt_hi", [P, 2, KT, GT], F32R)
        xt_lo = sb("xt_lo", [P, 2, KT, GT], F32R)
        parts = sb("parts", [P, 2, 2 * KT, 3, GT], BF16)
        rest = sb("rest", [P, 2 * KT, GT])
        kf = sb("kf", [P, 2, KT, GT])
        va = sb("va", [P, 2, TB, H, VW])
        banks = [ctx.enter_context(nc.psum_tensor(f"p_bank{i}", [P, GT], F32)) for i in range(8)]
        t_bank, qk_bank, v_bank = banks[0:2], banks[2:6], banks[6:8]
        norm = Norm(nc, ctx, "n1")

        s_w, s_id, s_ones = sem("weights_in"), sem("ident"), sem("ones")
        s_wt, s_whi, s_wlo = sem("w_turned"), sem("w_hi"), sem("w_lo")
        s_x = [sem("x_in0"), sem("x_in1")]
        s_t, s_hi, s_lo = sem("turned"), sem("xt_hi"), sem("xt_lo")
        s_qk, s_v = sem("qk"), sem("v")
        s_kf, s_high, s_rest, s_mid, s_low, s_vout = (
            sem("kf"), sem("high"), sem("rest"), sem("mid"), sem("low"), sem("v_out"))
        s_out = [sem("out0"), sem("out1")]
        STORES = 8

        x_v = x.rearrange("b (g t p) d -> (b g) p t d", t=TB, p=P)
        block = ctx.enter_context(nc.Block())

        @block.sync
        def _(sp):
            for w in range(3):
                sp.dma_start(w_in[:, w], weights[w].rearrange("(m p) k -> p m k", p=P)).then_inc(s_w, DMA)

            def body(at):
                if q := at(0):
                    wait(sp, norm.s_back, (q.g - 2) * 6 + 6)
                    sp.dma_start(xb[:, q.par], x_v[bass.ds(q.g, 1)].rearrange("a p t d -> (a p) t d")
                                 ).then_inc(s_x[q.par], DMA)
                if q := at(2):
                    sp.wait_ge(s_kf, q.g * 2 + 2)
                    sp.wait_ge(s_low, q.g * 4 + 4)
                    cols = bass.ds(q.g * GT, GT)
                    for s in range(2):
                        for part in range(3):
                            sp.dma_start(qk_dram[s, part, :, cols].rearrange("(m p) t -> p m t", p=P),
                                         parts[:, q.par, KT * s:KT * s + KT, part, :]).then_inc(s_out[q.par], DMA)
                    sp.dma_start(kf_dram[:, cols].rearrange("(m p) t -> p m t", p=P),
                                 kf[:, q.par]).then_inc(s_out[q.par], DMA)
                    sp.wait_ge(s_vout, q.g * 2 + 2)
                    sp.dma_start(va_dram[cols, :].rearrange("(t p) n -> p t n", p=P),
                                 va[:, q.par].rearrange("p t h e -> p t (h e)")).then_inc(s_out[q.par], DMA)

            sweep(sp, body, 2)
            for par in range(2):
                sp.wait_ge(s_out[par], DMA * STORES * (G // 2))

        @block.gpsimd
        def _(pool):
            pool.memset(va[:, :, :, :, HD:VW], 1.0).then_inc(s_ones, 1)
            identity(pool, ident[:], s_id)

            def body(at):
                if q := at(2):
                    for u in range(2 * KT):
                        pool.wait_ge(s_mid, q.g * 4 + u + 1)
                        pool.tensor_tensor(parts[:, q.par, u, LOW, :], rest[:, u, :],
                                           parts[:, q.par, u, MID, :], ALU.subtract).then_inc(s_low, 1)

            sweep(pool, body, 2)

        @block.tensor
        def _(pe):
            pe.wait_ge(s_id, 2)
            for w in range(3):
                pe.wait_ge(s_w, 3 * DMA)
                for k in range(KT):
                    for m in range(KT):
                        ins = pe.transpose(banks[w][:, k * D + m * P:k * D + m * P + P],
                                           w_in[:, w, m, k * P:k * P + P], ident[:])
                ins.then_inc(s_wt, 1)
            pe.wait_ge(s_wlo, 3)

            def body(at):
                if q := at(1):
                    pe.wait_ge(norm.s_back, norm.done(q))
                    for k in range(KT):
                        wait(pe, s_lo, (q.g - 1) * KT + k + 1)
                        for t in range(TB):
                            ins = pe.transpose(t_bank[k][:, t * P:t * P + P],
                                               xn[:, q.par, t, k * P:k * P + P], ident[:])
                        ins.then_inc(s_t, 1)
                if q := at(2):
                    pe.wait_ge(s_lo, q.g * KT + KT)
                    xh = [xt_hi[:, q.par, k, :] for k in range(KT)]
                    xl = [xt_lo[:, q.par, k, :] for k in range(KT)]
                    for u in range(2 * KT):
                        w, m = u // KT, (u % KT) * P
                        wait(pe, s_rest, (q.g - 1) * 4 + u + 1)
                        three_pass(pe, qk_bank[u][:], [wt_hi[:, w, k, m:m + P] for k in range(KT)],
                                   [wt_lo[:, w, k, m:m + P] for k in range(KT)], xh, xl).then_inc(s_qk, 1)
                    for c in range(2):
                        wait(pe, s_vout, (q.g - 1) * 2 + c + 1)
                        for t in range(2):
                            cut = slice((2 * c + t) * P, (2 * c + t + 1) * P)
                            ins = three_pass(pe, v_bank[c][:, t * D:t * D + D], [a[:, cut] for a in xh],
                                             [a[:, cut] for a in xl], [wt_hi[:, 2, k, :] for k in range(KT)],
                                             [wt_lo[:, 2, k, :] for k in range(KT)])
                        ins.then_inc(s_v, 1)

            sweep(pe, body, 2)

        @block.scalar
        def _(act):
            for w in range(3):
                act.wait_ge(s_wt, w + 1)
                act.activation(wt_hi[:, w].rearrange("p k n -> p (k n)"), banks[w][:], ACT.Copy).then_inc(s_whi, 1)

            def mid(q, u):
                act.wait_ge(s_rest, q.g * 4 + u + 1)
                act.activation(parts[:, q.par, u, MID, :], rest[:, u, :], ACT.Copy).then_inc(s_mid, 1)

            def body(at):
                if q := at(0):
                    norm.root(act, q)
                if q := at(1):
                    wait(act, s_v, (q.g - 2) * 2 + 2)
                    for k in range(KT):
                        act.wait_ge(s_t, q.g * KT + k + 1)
                        act.activation(xt_hi[:, q.par, k, :], t_bank[k][:], ACT.Copy).then_inc(s_hi, 1)
                if q := at(2):
                    wait(act, s_out[q.par], q.half * DMA * STORES)
                    for u in range(2 * KT):
                        act.wait_ge(s_qk, q.g * 4 + u + 1)
                        if u >= KT:
                            act.activation(kf[:, q.par, u - KT, :], qk_bank[u][:], ACT.Copy).then_inc(s_kf, 1)
                        act.activation(parts[:, q.par, u, HIGH, :], qk_bank[u][:], ACT.Copy,
                                       scale=QSCALE if u < KT else 1.0).then_inc(s_high, 1)
                        if u:
                            mid(q, u - 1)
                    mid(q, 2 * KT - 1)
                    if isinstance(q.g, int) and q.g == 0:
                        act.wait_ge(s_ones, 1)
                    for c in range(2):
                        act.wait_ge(s_v, q.g * 2 + c + 1)
                        for t in range(2):
                            ins = act.activation(va[:, q.par, 2 * c + t, :, 0:HD],
                                                 v_bank[c][:, t * D:t * D + D].rearrange("p (h e) -> p h e", h=H),
                                                 ACT.Copy)
                        ins.then_inc(s_vout, 1)

            sweep(act, body, 2)

        @block.vector
        def _(dve):
            norm.begin(dve)
            for w in range(3):
                dve.wait_ge(s_whi, w + 1)
                dve.tensor_tensor(wt_lo[:, w].rearrange("p k n -> p (k n)"), banks[w][:],
                                  wt_hi[:, w].bitcast(F32).rearrange("p k n -> p (k n)"),
                                  ALU.subtract).then_inc(s_wlo, 1)

            def body(at):
                if q := at(1):
                    wait(dve, s_t, (q.g - 2) * KT + KT)
                    norm.back(dve, xb[:, q.par], xn[:, q.par], q)
                if q := at(0):
                    dve.wait_ge(s_x[q.par], (q.half + 1) * DMA)
                    norm.front(dve, xb[:, q.par], q)
                if q := at(1):
                    for k in range(KT):
                        dve.wait_ge(s_hi, q.g * KT + k + 1)
                        dve.tensor_tensor(xt_lo[:, q.par, k, :], t_bank[k][:], xt_hi[:, q.par, k, :].bitcast(F32),
                                          ALU.subtract).then_inc(s_lo, 1)
                if q := at(2):
                    for u in range(2 * KT):
                        dve.wait_ge(s_high, q.g * 4 + u + 1)
                        wait(dve, s_low, (q.g - 1) * 4 + u + 1)
                        dve.scalar_tensor_tensor(out=rest[:, u, :], in0=qk_bank[u][:],
                                                 scalar=QSCALE if u < KT else 1.0,
                                                 in1=parts[:, q.par, u, HIGH, :],
                                                 op0=ALU.mult, op1=ALU.subtract).then_inc(s_rest, 1)

            sweep(dve, body, 2)


class Unit:

    def __init__(self, b, i):
        self.i, self.gi, self.hq = i, i // UPG, i % UPG
        self.n = b * UPB + i
        self.g = b * GB + self.gi
        self.batch = b
        self.gpar = self.gi % 2
        self.ghalf = b * (GB // 2) + self.gi // 2
        self.upar = i % 2
        self.uhalf = b * (UPB // 2) + i // 2


def march(eng, body, lags):
    def step(b, i):
        def at(lag):
            j = i - lag
            if j >= 0:
                return Unit(b, j) if not isinstance(b, int) or b < B else None
            if isinstance(b, int) and b == 0:
                return None
            return Unit(b - 1, j + UPB)
        return at

    for i in range(UPB):
        body(step(0, i))
    with eng.Fori(1, B) as b:
        for i in range(UPB):
            body(step(b, i))
    for i in range(lags):
        body(step(B, i))


SCORE_TILES = ((0, 0, 1, 0, 3), (0, 3, -1, 0, 1),
               (1, 0, 0, 0, 2), (1, 2, 3, 2, 2),
               (2, 0, 4, 3, 1), (2, 1, 2, 1, 3))
HEAD_COLS = 3 * GT
CUT_LOW = ((0, 1), (6, 1), (8, 2))
CUT_HIGH = ((2, 2), (5, 1), (11, 1))
SUM_ORDER = (1, 2, 0, 3, -1, 4)
CHUNK = 2 * GT
CHUNKS = NQ * HEAD_COLS // CHUNK
TILES = NQ * TB
TURN_OF_TILE = tuple(j + 1 if j < 2 else j + 2 for j in range(TILES))
TURN_OF_M, TURN_OF_S = 0, 3

L_KEY0, L_MAX, L_SHIFT, L_SCORE, L_SUM, L_OUT = 2, 3, 4, 5, 6, 7


def in_group(gi, kb):
    return not (gi == 0 and kb == -1) and not (gi == GB - 1 and kb == TB)


def stage_attend(nc, qk_dram, va_dram, o_dram):
    with ExitStack() as ctx:
        def sb(name, shape, dt=F32):
            return ctx.enter_context(nc.sbuf_tensor(f"a_{name}", shape, dt))

        def sem(name):
            return ctx.enter_context(nc.semaphore(f"a_{name}"))

        rows = SLOT_ROWS + SHIFT_ROWS
        kw = [[sb(f"k{g}{q}", [P, NQ, WIN], BF16) for q in range(UPG)] for g in range(2)]
        qw = [[sb(f"q{g}{q}", [P, NQ, GT], BF16) for q in range(UPG)] for g in range(2)]
        vw = sb("v", [P, 2, TB + 2, VROW])
        v0 = sb("v0", [P, VROW])
        k0 = sb("k0", [P, H], BF16)
        ident = sb("ident", [P, P])
        band = sb("band", [P, 3 * P + 1], BF16)
        gate0 = sb("gate0", [P, NQ, TB])
        masked = sb("masked", [P, TILES, 3 * P + 1])
        mx = sb("max", [P, UPG, P])
        d0 = sb("d0", [P, 2, TILES])
        p0 = sb("p0", [P, UPG, NQ, TB])
        neg = sb("neg_rest", [TILES, 2, P])
        shift = sb("shift", [TILES, 2, SHIFT_ROWS, P], BF16)
        pe_w = sb("weights", [P, 2, NQ * HEAD_COLS])
        sums = sb("sums", [P, 2, GT])
        t0 = sb("key0_part", [P, UPG, TB, NQ, HD])
        den = sb("den", [P, 2, TB, NQ])
        rden = sb("rden", [P, 2, TB, NQ])
        num = sb("num", [P, 2, TB, NQ, HD])
        ob = sb("o", [P, 2, TB, D])
        score = [ctx.enter_context(nc.psum_tensor(f"a_score{i}", [P, CHUNK], F32)) for i in range(2)]
        sum_bank = [ctx.enter_context(nc.psum_tensor(f"a_sum{i}", [P, GT], F32)) for i in range(2)]
        turn = [ctx.enter_context(nc.psum_tensor(f"a_turn{i}", [P, GT], F32)) for i in range(2)]

        s_init, s_pool = sem("init"), sem("pool_init")
        s_load = [[sem(f"qk_in{g}{q}") for q in range(UPG)] for g in range(2)]
        s_v, s_v0 = [sem("v_in0"), sem("v_in1")], sem("v0_in")
        s_row = [sem("row0"), sem("row1")]
        s_k0 = sem("k0")
        s_tile, s_tile_read = sem("tile"), sem("tile_read")
        s_m, s_m_read, s_s, s_s_read = sem("m"), sem("m_read"), sem("s"), sem("s_read")
        s_den = sem("den")
        s_d0, s_p0 = sem("d0"), sem("p0")
        s_shift = sem("shift")
        s_score, s_exp, s_cut = sem("score"), sem("exp"), sem("cut")
        s_sum, s_sumout = sem("sum"), sem("sum_out")
        s_t0, s_gate = sem("t0"), sem("gate")
        s_num, s_o = sem("num"), sem("o")
        s_out = [sem("out0"), sem("out1")]
        LOADS = 2 * len(K_SLOTS)
        block = ctx.enter_context(nc.Block())

        def window(gi):
            return (1 if gi == 0 else 0), (TB + 1 if gi == GB - 1 else TB + 2)

        @block.sync
        def _(sp):
            def body(at):
                if u := at(0):
                    wait(sp, s_score, (u.n - 2 * UPG) * CHUNKS + CHUNKS)
                    lo, hi = window(u.gi)
                    h0 = u.hq * NQ
                    keys = bass.ds(u.g * GT + (lo - 1) * P, (hi - lo) * P)
                    queries = bass.ds(u.g * GT, GT)
                    for s in range(len(K_SLOTS)):
                        r = slice(s * HD, s * HD + HD)
                        sp.dma_start(kw[u.gpar][u.hq][r, :, lo * P:hi * P],
                                     qk_dram[1, K_SLOTS[s], h0 * HD:(h0 + NQ) * HD, keys]
                                     .rearrange("(h d) t -> d h t", d=HD)).then_inc(s_load[u.gpar][u.hq], DMA)
                        sp.dma_start(qw[u.gpar][u.hq][r, :, :],
                                     qk_dram[0, Q_SLOTS[s], h0 * HD:(h0 + NQ) * HD, queries]
                                     .rearrange("(h d) t -> d h t", d=HD)).then_inc(s_load[u.gpar][u.hq], DMA)
                if (u := at(L_MAX)) and u.hq == 0:
                    wait(sp, s_sum, (u.n - UPG * 2) + UPG)
                    lo, hi = window(u.gi)
                    sp.dma_start(vw[:, u.gpar, lo:hi, :],
                                 va_dram[bass.ds(u.g * GT + (lo - 1) * P, (hi - lo) * P), :]
                                 .rearrange("(w p) n -> p w n", p=P)).then_inc(s_v[u.gpar], DMA)
                if (u := at(L_SCORE)) and u.i == 0:
                    wait(sp, s_t0, u.n)
                    sp.dma_start(v0[:], va_dram[bass.ds(u.batch * T, 1), :].to_broadcast((P, VROW))
                                 ).then_inc(s_v0, DMA)
                if u := at(L_SHIFT):
                    sp.wait_ge(s_shift, u.n * 4 + 4)
                    for part in range(SHIFT_ROWS):
                        row = qw[u.gpar][u.hq][SLOT_ROWS + part:SLOT_ROWS + part + 1, :, :]
                        sp.dma_start(row.rearrange("s h (t q) -> s (h t) q", q=P),
                                     shift[:, u.upar, part, :]).then_inc(s_row[u.upar], DMA)
                if (u := at(L_OUT)) and u.hq == UPG - 1:
                    sp.wait_ge(s_o, u.n + 1)
                    sp.dma_start(o_dram[bass.ds(u.g * GT, GT), :].rearrange("(t p) d -> p t d", p=P),
                                 ob[:, u.gpar]).then_inc(s_out[u.gpar], DMA)

            march(sp, body, L_OUT)
            for par in range(2):
                sp.wait_ge(s_out[par], DMA * (G // 2))

        @block.gpsimd
        def _(pool):
            identity(pool, ident[:], s_pool)
            pool.memset(band[:], 0.0).then_inc(s_pool, 1)
            pool.wait_ge(s_pool, 3)
            pool.affine_select(out=band[:, 0:P], in_=band[:, 0:P], compare_op=ALU.is_ge, fill=NEG, base=0,
                               pattern=[[1, P]], channel_multiplier=-1)
            pool.affine_select(out=band[:, 2 * P:3 * P], in_=band[:, 2 * P:3 * P], compare_op=ALU.is_ge,
                               fill=NEG, base=0, pattern=[[-1, P]], channel_multiplier=1)
            pool.memset(gate0[:], 1.0).then_inc(s_pool, 1)
            pool.wait_ge(s_pool, 4)
            pool.affine_select(out=gate0[:], in_=gate0[:], compare_op=ALU.is_gt, fill=0.0, base=-P,
                               pattern=[[0, NQ], [P, TB]], channel_multiplier=1).then_inc(s_pool, 1)

            exp_turn = Turn(pool, s_exp, "exp_turn", CHUNKS, CHUNKS)

            def body(at):
                if u := at(L_SCORE):
                    pool.wait_ge(s_p0, u.n + 1)
                    if u.gi == 0:
                        pool.tensor_tensor(p0[:, u.hq], p0[:, u.hq], gate0[:], ALU.mult).then_inc(s_gate, 1)
                        pool.wait_ge(s_gate, u.batch * UPG + u.hq + 1)
                    if u.i == 0:
                        pool.wait_ge(s_v0, (u.batch + 1) * DMA)
                    wait(pool, s_num, u.n - 3)
                    values = v0[:, u.hq * NQ * VW:(u.hq + 1) * NQ * VW].rearrange("p (h e) -> p h e", h=NQ)
                    pool.tensor_tensor(
                        t0[:, u.hq], values[:, :, 0:HD].unsqueeze(1).broadcast_to([P, TB, NQ, HD]),
                        p0[:, u.hq].rearrange("p h t -> p t h").unsqueeze(3).broadcast_to([P, TB, NQ, HD]),
                        ALU.mult).then_inc(s_t0, 1)
                    w = pe_w[:, u.upar].rearrange("p (h c q) -> p h c q", h=NQ, q=P)
                    exp_turn.wait(u.n * CHUNKS + CHUNKS)
                    for runs, sign in ((CUT_LOW, 1), (CUT_HIGH, -1)):
                        for c, m in runs:
                            cut = w[:, :, c:c + m, :]
                            ins = pool.affine_select(out=cut, in_=cut, compare_op=ALU.is_ge, fill=0.0, base=0,
                                                     pattern=[[0, NQ], [0, m], [sign, P]], channel_multiplier=-sign)
                    ins.then_inc(s_cut, 1)
                if u := at(L_OUT):
                    pool.wait_ge(s_num, u.n + 1)
                    if u.hq == 0:
                        wait(pool, s_out[u.gpar], u.ghalf * DMA)
                    o = ob[:, u.gpar].rearrange("p t (h e) -> p t h e", e=HD)[:, :, u.hq * NQ:(u.hq + 1) * NQ, :]
                    pool.tensor_tensor(o, num[:, u.upar], rden[:, u.upar].unsqueeze(3).broadcast_to([P, TB, NQ, HD]),
                                       ALU.mult).then_inc(s_o, 1)

            march(pool, body, L_OUT)

        @block.tensor
        def _(pe):
            pe.wait_ge(s_init, 5)
            pe.wait_ge(s_pool, 2)

            def body(at):
                um, ux, us, up, uo = at(L_SHIFT), at(L_MAX), at(L_SCORE), at(L_SUM), at(L_OUT)

                def bank_read(turn_no):
                    if turn_no < 2:
                        if um:
                            pe.wait_ge(s_tile_read, um.n * TILES + TILES - 1 + turn_no)
                    elif turn_no == TURN_OF_M + 2:
                        if um:
                            pe.wait_ge(s_m_read, um.n + 1)
                    elif turn_no == TURN_OF_S + 2 and uo:
                        pe.wait_ge(s_s_read, uo.n + 1)
                    elif ux:
                        tile = max(j for j in range(TILES) if TURN_OF_TILE[j] in (turn_no - 2, turn_no - 4))
                        pe.wait_ge(s_tile_read, ux.n * TILES + tile + 1)
                    elif um:
                        pe.wait_ge(s_tile_read, UNITS * TILES)
                    else:
                        pe.wait_ge(s_s_read, uo.n)

                def maxima_turned():
                    if um:
                        pe.wait_ge(s_d0, um.n + 1)
                        bank_read(TURN_OF_M)
                        pe.transpose(turn[TURN_OF_M % 2][:, 0:P], mx[:, um.hq, :], ident[:]).then_inc(s_m, 1)

                def sums_turned():
                    if uo:
                        pe.wait_ge(s_sumout, uo.n + 1)
                        bank_read(TURN_OF_S)
                        for t in range(TB):
                            ins = pe.transpose(turn[TURN_OF_S % 2][:, t * P:t * P + P],
                                               sums[:, uo.upar, t * P:t * P + P], ident[:])
                        ins.then_inc(s_s, 1)

                def max_tile(j):
                    if not ux:
                        return
                    k = TURN_OF_TILE[j]
                    h, t = j // TB, j % TB
                    if j == 0:
                        pe.wait_ge(s_load[ux.gpar][ux.hq], (ux.ghalf + 1) * LOADS * DMA)
                        if ux.gi == 0:
                            pe.wait_ge(s_k0, ux.batch * UPG + ux.hq + 1)
                    bank_read(k)
                    lo = P if ux.gi == 0 and t == 0 else 0
                    hi = 2 * P if ux.gi == GB - 1 and t == TB - 1 else 3 * P
                    q, kk = qw[ux.gpar][ux.hq], kw[ux.gpar][ux.hq]
                    lhs = q[0:SLOT_ROWS, h, t * P:t * P + P]
                    pe.matmul(turn[k % 2][:, lo:hi], lhs, kk[0:SLOT_ROWS, h, t * P + lo:t * P + hi],
                              start=True, stop=True)
                    key = ux.hq * NQ + h
                    pe.matmul(turn[k % 2][:, hi:hi + 1], lhs, k0[0:SLOT_ROWS, key:key + 1],
                              start=True, stop=True).then_inc(s_tile, 1)

                def score_bank(n):
                    if not us:
                        return
                    c = n // 2
                    if n == 0:
                        pe.wait_ge(s_row[us.upar], (us.uhalf + 1) * DMA * SHIFT_ROWS)
                    if n % 2 == 0:
                        wait(pe, s_exp, us.n * CHUNKS + c - 1)
                    j, third = n // 3, n % 3
                    q, kk = qw[us.gpar][us.hq], kw[us.gpar][us.hq]
                    tiles = [x for x in SCORE_TILES if x[0] == third and in_group(us.gi, x[2])]
                    for _, col, kb, qb, m in tiles:
                        ins = pe.matmul(
                            score[c % 2][:, (n % 2) * GT + col * P:(n % 2) * GT + (col + m) * P],
                            kk[0:rows, j, (kb + 1) * P:(kb + 2) * P], q[0:rows, j, qb * P:(qb + m) * P],
                            start=True, stop=True)
                    if n % 2 == 1:
                        ins.then_inc(s_score, 1)

                def sum_block(o):
                    if not up:
                        return
                    kb = SUM_ORDER[o]
                    if o == 0:
                        pe.wait_ge(s_cut, up.n + 1)
                        wait(pe, s_sumout, up.n - 1)
                        if up.hq == 0:
                            pe.wait_ge(s_v[up.gpar], (up.ghalf + 1) * DMA)
                    last = [x for x in SUM_ORDER if in_group(up.gi, x)][-1]
                    if in_group(up.gi, kb):
                        third, col, _, qb, m = [x for x in SCORE_TILES if x[2] == kb][0]
                        for j in range(NQ):
                            c0 = j * HEAD_COLS + third * GT + col * P
                            h = up.hq * NQ + j
                            ins = pe.matmul(sum_bank[up.upar][32 * j:32 * j + VW, qb * P:(qb + m) * P],
                                            vw[:, up.gpar, kb + 1, h * VW:h * VW + VW],
                                            pe_w[:, up.upar, c0:c0 + m * P], start=(o == 0), stop=(kb == last),
                                            skip_group_check=True)
                        if kb == last:
                            ins.then_inc(s_sum, 1)

                maxima_turned()
                j = 0
                for o in range(6):
                    for half in range(2):
                        score_bank(2 * o + half)
                        if j < TILES:
                            max_tile(j)
                            j += 1
                    if o == 0:
                        sums_turned()
                    sum_block(o)
                    if o < 4:
                        max_tile(j)
                        j += 1
                assert j == TILES

            march(pe, body, L_OUT)

        @block.scalar
        def _(act):
            def body(at):
                if u := at(L_OUT):
                    act.wait_ge(s_sum, u.n + 1)
                    wait(act, s_s, u.n - 1)
                    act.activation(sums[:, u.upar, :], sum_bank[u.upar][:], ACT.Copy).then_inc(s_sumout, 1)
                us, ud = at(L_SCORE), at(L_SHIFT)
                for c in range(CHUNKS):
                    if us:
                        act.wait_ge(s_score, us.n * CHUNKS + c + 1)
                        if c == 0:
                            wait(act, s_sum, us.n - 1)
                        act.activation(pe_w[:, us.upar, c * CHUNK:(c + 1) * CHUNK], score[c % 2][:], ACT.Exp
                                       ).then_inc(s_exp, 1)
                    if ud and c == 0:
                        act.wait_ge(s_d0, ud.n + 1)
                        wait(act, s_num, ud.n - 3)
                        act.activation(p0[:, ud.hq].rearrange("p h t -> p (h t)"), d0[:, ud.upar, :], ACT.Exp
                                       ).then_inc(s_p0, 1)

            march(act, body, L_OUT)

        @block.vector
        def _(dve):
            dve.memset(score[0][:], 0.0).then_inc(s_init, 1)
            dve.memset(score[1][:], 0.0).then_inc(s_init, 1)
            dve.memset(sum_bank[0][:], 0.0).then_inc(s_init, 1)
            dve.memset(sum_bank[1][:], 0.0).then_inc(s_init, 1)
            for g in range(2):
                for q in range(UPG):
                    dve.memset(kw[g][q][SLOT_ROWS:rows, :, :], 1.0)
            dve.memset(mx[:], 0.0).then_inc(s_init, 1)
            dve.wait_ge(s_init, 5)
            dve.wait_ge(s_pool, 5)
            tile_turn = Turn(dve, s_tile, "tile_turn", 1)

            def body(at):
                um, ux, uo = at(L_SHIFT), at(L_MAX), at(L_OUT)
                if (u := at(L_KEY0)) and u.gi == 0:
                    wait(dve, s_tile_read, (u.n - UPG) * TILES + TILES)
                    dve.wait_ge(s_load[0][u.hq], (u.ghalf + 1) * LOADS * DMA)
                    dve.tensor_copy(k0[0:SLOT_ROWS, u.hq * NQ:u.hq * NQ + NQ],
                                    kw[0][u.hq][0:SLOT_ROWS, :, P]).then_inc(s_k0, 1)
                if um:
                    t_in = turn[TURN_OF_M % 2][0:TILES, 0:P]
                    high, mid, low = (shift[:, um.upar, part, :] for part in (HIGH, MID, LOW))
                    dve.wait_ge(s_m, um.n + 1)
                    wait(dve, s_row[um.upar], um.uhalf * DMA * SHIFT_ROWS)
                    dve.tensor_scalar(high, t_in, -1.0, None, ALU.mult).then_inc(s_shift, 1)
                    dve.wait_ge(s_shift, um.n * 4 + 1)
                    dve.scalar_tensor_tensor(out=neg[:, 0, :], in0=t_in, scalar=-1.0, in1=high,
                                             op0=ALU.mult, op1=ALU.subtract).then_inc(s_m_read, 1)
                    dve.wait_ge(s_m_read, um.n + 1)
                    dve.tensor_copy(mid, neg[:, 0, :]).then_inc(s_shift, 1)
                    dve.wait_ge(s_shift, um.n * 4 + 2)
                    dve.tensor_tensor(neg[:, 1, :], neg[:, 0, :], mid, ALU.subtract).then_inc(s_shift, 1)
                    dve.wait_ge(s_shift, um.n * 4 + 3)
                    dve.tensor_copy(low, neg[:, 1, :]).then_inc(s_shift, 1)
                for j in range(TILES):
                    if ux:
                        bank = turn[TURN_OF_TILE[j] % 2]
                        h, t = j // TB, j % TB
                        lo = P if ux.gi == 0 and t == 0 else 0
                        hi = 2 * P if ux.gi == GB - 1 and t == TB - 1 else 3 * P
                        first = 3 * P - (hi - lo)
                        tile_turn.wait(ux.n * TILES + j + 1)
                        dve.tensor_tensor_reduce(
                            out=masked[:, j, first:3 * P + 1], in0=bank[:, lo:hi + 1],
                            in1=band[:, lo:hi + 1], scale=1.0, scalar=NEG, op0=ALU.add, op1=ALU.max,
                            accum_out=mx[:, ux.hq, j:j + 1]).then_inc(s_tile_read, 1)
                    if j == 1 and uo:
                        turned = turn[TURN_OF_S % 2][:].rearrange("p (t h e) -> p t h e", t=TB, h=NQ)
                        dve.wait_ge(s_s, uo.n + 1)
                        dve.wait_ge(s_t0, uo.n + 1)
                        wait(dve, s_o, uo.n - 1)
                        dve.tensor_tensor(den[:, uo.upar], turned[:, :, :, HD],
                                          p0[:, uo.hq].rearrange("p h t -> p t h"), ALU.add).then_inc(s_den, 1)
                        dve.tensor_tensor(num[:, uo.upar], turned[:, :, :, 0:HD], t0[:, uo.hq], ALU.add
                                          ).then_inc(s_s_read, 1)
                        dve.wait_ge(s_den, uo.n + 1)
                        dve.reciprocal(rden[:, uo.upar], den[:, uo.upar]).then_inc(s_num, 1)
                if ux:
                    dve.wait_ge(s_tile_read, ux.n * TILES + TILES)
                    wait(dve, s_p0, ux.n - 1)
                    dve.tensor_tensor(d0[:, ux.upar, :], masked[:, :, 3 * P], mx[:, ux.hq, 0:TILES], ALU.subtract
                                      ).then_inc(s_d0, 1)

            march(dve, body, L_OUT)


def block_mask(pool, tile, groups, size, base, sem):
    start = sem[1]
    pool.memset(tile, 1.0).then_inc(sem[0], 1)
    pool.wait_ge(sem[0], start + 1)
    pool.affine_select(out=tile, in_=tile, compare_op=ALU.is_ge, fill=0.0, base=base,
                       pattern=[[-size, groups]], channel_multiplier=1).then_inc(sem[0], 1)
    pool.wait_ge(sem[0], start + 2)
    pool.affine_select(out=tile, in_=tile, compare_op=ALU.is_ge, fill=0.0, base=size - 1 - base,
                       pattern=[[size, groups]], channel_multiplier=-1).then_inc(sem[0], 1)
    sem[1] = start + 3


def stage_row_zero(nc, qk_dram, kf_dram, va_dram, o_dram):
    CH = T // GT
    NB = T // P
    QR = 32
    RUN = 32
    with ExitStack() as ctx:
        def sb(name, shape, dt=F32):
            return ctx.enter_context(nc.sbuf_tensor(f"z_{name}", shape, dt))

        def sem(name):
            return ctx.enter_context(nc.semaphore(f"z_{name}"))

        qp_run = sb("q_parts", [P, 3, KT, B, RUN], BF16)
        qp = qp_run[:, :, :, :, 0]
        q0 = sb("q", [P, KT, B])
        head_of = sb("head_of", [P, KT, H])
        qd = sb("q_diag", [P, KT, B, QR])
        kf = sb("k", [P, B, KT, T])
        va = sb("v", [P, B, NB, VROW])
        ident = sb("ident", [P, P])
        own = sb("own", [P, H, VW])
        seq_of = sb("seq_of", [P, B])
        nmax = sb("nmax", [P, 1])
        den = sb("den", [P, 1])
        rden = sb("rden", [P, 1])
        w = sb("w", [P, T])
        wt = sb("wt", [P, NB, P])
        picked = sb("picked", [P, H, VW])
        row = sb("row", [B, H, HD])
        scores = ctx.enter_context(nc.psum_tensor("z_scores", [P, T], F32))
        turned = ctx.enter_context(nc.psum_tensor("z_turned", [P, 2, GT], F32))
        sums = ctx.enter_context(nc.psum_tensor("z_sums", [P, GT], F32))
        total = ctx.enter_context(nc.psum_tensor("z_total", [P, GT], F32))
        s_q, s_k, s_v, s_pool = sem("q"), sem("k"), sem("v"), sem("pool")
        s_qd, s_sc, s_max, s_exp = sem("qd"), sem("sc"), sem("max"), sem("exp")
        s_turn, s_wt, s_sum, s_pick, s_tot, s_row, s_out = (
            sem("turn"), sem("wt"), sem("sum"), sem("pick"), sem("tot"), sem("row"), sem("out"))
        block = ctx.enter_context(nc.Block())

        @block.sync
        def _(sp):
            for part in range(3):
                for k in range(KT):
                    sp.dma_start(qp_run[:, part, k], qk_dram[0, part, k * P:(k + 1) * P, :]
                                 .rearrange("p (b t) -> p b t", b=B)[:, :, 0:RUN]).then_inc(s_q, DMA)
            for b in range(B):
                sp.dma_start(kf[:, b], kf_dram[:, b * T:(b + 1) * T].rearrange("(k p) t -> p k t", p=P)
                             ).then_inc(s_k, DMA)
            for b in range(B):
                sp.dma_start(va[:, b], va_dram[b * T:(b + 1) * T, :].rearrange("(n p) e -> p n e", p=P)
                             ).then_inc(s_v, DMA)
            sp.wait_ge(s_row, 1)
            sp.dma_start(o_dram[0:N:T, :], row[:].rearrange("b h e -> b (h e)")).then_inc(s_out, DMA)
            sp.wait_ge(s_out, DMA)

        @block.gpsimd
        def _(pool):
            count = [s_pool, 0]
            for k in range(KT):
                block_mask(pool, head_of[:, k, :], H, HD, k * P, count)
            block_mask(pool, seq_of[:], B, QR, 0, count)
            pool.memset(own[:], 0.0).then_inc(s_pool, 1)
            pool.wait_ge(s_pool, count[1] + 1)
            for b in range(B):
                pool.affine_select(out=own[:], in_=own[:], compare_op=ALU.not_equal, fill=1.0, base=-QR * b,
                                   pattern=[[-1, H], [0, VW]], channel_multiplier=1).then_inc(s_pool, 1)
                pool.wait_ge(s_pool, count[1] + 2 + b)
            pool.memset(ident[:], 1.0).then_inc(s_pool, 1)
            pool.wait_ge(s_pool, count[1] + 6)
            pool.affine_select(out=ident[:], in_=ident[:], compare_op=ALU.is_equal, fill=0.0, base=0,
                               pattern=[[-1, P]], channel_multiplier=1).then_inc(s_pool, 1)
            assert count[1] + 7 == 3 * (KT + 1) + 7

        POOL_DONE = 3 * (KT + 1) + 7

        @block.vector
        def _(dve):
            dve.memset(qd[:], 0.0).then_inc(s_qd, 1)
            dve.wait_ge(s_q, 3 * KT * DMA)
            dve.wait_ge(s_pool, POOL_DONE)
            dve.tensor_tensor(q0[:], qp[:, HIGH], qp[:, MID], ALU.add).then_inc(s_qd, 1)
            dve.wait_ge(s_qd, 2)
            dve.tensor_tensor(q0[:], q0[:], qp[:, LOW], ALU.add).then_inc(s_qd, 1)
            dve.wait_ge(s_qd, 3)
            for k in range(KT):
                for b in range(B):
                    dve.tensor_scalar(qd[:, k, b, 0:H], head_of[:, k, :], q0[:, k, b:b + 1], None, ALU.mult
                                      ).then_inc(s_qd, 1)
            dve.wait_ge(s_sc, 1)
            dve.tensor_reduce(nmax[:], scores[:], AX.X, ALU.max, negate=True).then_inc(s_max, 1)
            dve.wait_ge(s_exp, 1)
            dve.reciprocal(rden[:], den[:]).then_inc(s_max, 1)
            for n in range(NB // TB):
                dve.wait_ge(s_turn, n + 1)
                dve.tensor_copy(wt[:, n * TB:(n + 1) * TB, :].rearrange("p a b -> p (a b)"), turned[:, n % 2, :]
                                ).then_inc(s_wt, 1)
            dve.wait_ge(s_sum, 1)
            dve.wait_ge(s_max, 2)
            dve.scalar_tensor_tensor(out=picked[:].rearrange("p h e -> p (h e)"), in0=sums[:, 0:VROW],
                                     scalar=rden[:, 0:1], in1=own[:].rearrange("p h e -> p (h e)"),
                                     op0=ALU.mult, op1=ALU.mult).then_inc(s_pick, 1)
            dve.wait_ge(s_tot, 1)
            dve.tensor_copy(row[:], total[0:B, 0:VROW].rearrange("b (h e) -> b h e", h=H)[:, :, 0:HD]
                            ).then_inc(s_row, 1)

        @block.scalar
        def _(act):
            act.wait_ge(s_max, 1)
            act.activation(w[:], scores[:], ACT.Exp, bias=nmax[:, 0:1], accum_out=den[:, 0:1]).then_inc(s_exp, 1)

        @block.tensor
        def _(pe):
            pe.wait_ge(s_qd, 3 + KT * B)
            pe.wait_ge(s_k, B * DMA)
            for c in range(CH):
                for k in range(KT):
                    for b in range(B):
                        ins = pe.matmul(scores[QR * b:QR * b + QR, c * GT:(c + 1) * GT], qd[:, k, b, :],
                                        kf[:, b, k, c * GT:(c + 1) * GT], start=(k == 0), stop=(k == KT - 1))
            ins.then_inc(s_sc, 1)
            pe.wait_ge(s_exp, 1)
            for n in range(NB // TB):
                wait(pe, s_wt, n - 1)
                for i in range(TB):
                    c = (n * TB + i) * P
                    ins = pe.transpose(turned[:, n % 2, i * P:(i + 1) * P], w[:, c:c + P], ident[:])
                ins.then_inc(s_turn, 1)
            pe.wait_ge(s_v, B * DMA)
            pe.wait_ge(s_wt, NB // TB)
            for n in range(NB):
                for b in range(B):
                    ins = pe.matmul(sums[QR * b:QR * b + QR, 0:VROW], wt[:, n, QR * b:QR * b + QR], va[:, b, n, :],
                                    start=(n == 0), stop=(n == NB - 1))
            ins.then_inc(s_sum, 1)
            pe.wait_ge(s_pick, 1)
            pe.matmul(total[0:B, 0:VROW], seq_of[:], picked[:].rearrange("p h e -> p (h e)"),
                      start=True, stop=True).then_inc(s_tot, 1)


def stage_feed(nc, x, o_dram, wo, fast_b, w_fc, w_proj, u, v, gate, out):
    MH = HID // P
    with ExitStack() as ctx:
        def sb(name, shape, dt=F32):
            return ctx.enter_context(nc.sbuf_tensor(f"f_{name}", shape, dt))

        def sem(name):
            return ctx.enter_context(nc.semaphore(f"f_{name}"))

        ident = sb("ident", [P, P])
        wo_in, wo_t = sb("wo_in", [P, KT, D]), sb("wo_t", [P, KT, D])
        w1_in = sb("w1_in", [P, MH, D])
        w1_low = sb("w1_low", [P, MH, D])
        w1_hi, w1_lo = sb("w1_hi", [P, KT, HID], F32R), sb("w1_lo", [P, KT, HID], F32R)
        w2_in = sb("w2_in", [P, KT, HID])
        w2_tern = sb("w2_tern", [P, KT, HID])
        w2_t = sb("w2_t", [P, MH, D], F32R)
        mag1, half1, nhalf1 = sb("mag1", [P, MH]), sb("half1", [P, MH]), sb("nhalf1", [P, MH])
        mag2, half2, nhalf2 = sb("mag2", [P, KT]), sb("half2", [P, KT]), sb("nhalf2", [P, KT])
        u_in, u_t = sb("u_in", [P, MH, RANK]), sb("u_t", [P, P])
        u_m = sb("u_m", [P, MH, P])
        tile_of = sb("tile_of", [P, MH])
        fb_t = sb("fb_t", [RANK, RANK])
        fb_rep = sb("fb_rep", [RANK, MH, RANK])
        v_in = sb("v_in", [RANK, D])
        gate_c = sb("gate", [P, 1])
        low_v = sb("low_v", [P, D])
        ob, ot = sb("o", [P, 2, TB, D]), sb("o_t", [P, KT, GT])
        xb = sb("x", [P, 4, TB, D])
        xn = sb("xn", [P, TB, D])
        xt_hi, xt_lo = sb("xt_hi", [P, 2, KT, GT], F32R), sb("xt_lo", [P, 2, KT, GT], F32R)
        r = sb("relu", [P, 4, GT])
        r2 = sb("square", [P, 4, GT])
        r2_hi, r2_lo = sb("square_hi", [P, 4, GT], F32R), sb("square_lo", [P, 4, GT], F32R)
        yt = sb("y_t", [P, KT, GT])
        banks = [ctx.enter_context(nc.psum_tensor(f"f_bank{i}", [P, GT], F32)) for i in range(8)]
        t_bank, a_bank, h_bank, y_bank = banks[0:2], banks[2:4], banks[4:6], banks[6:8]
        norm = Norm(nc, ctx, "n2")

        s_in, s_pool = sem("weights_in"), sem("pool")
        s_prep, s_pt, s_pc = sem("prep"), sem("prep_turned"), sem("prep_copied")
        s_m1, s_low, s_w1, s_w1hi = sem("low_v"), sem("low"), sem("w1"), sem("w1_hi")
        s_scale, s_tern = sem("scale"), sem("ternary")
        s_o, s_x = [sem("o_in0"), sem("o_in1")], [sem(f"x_in{i}") for i in range(4)]
        s_ot, s_otc, s_a, s_x1 = sem("o_turned"), sem("o_copied"), sem("attn"), sem("x1")
        s_xt, s_hi, s_lo = sem("xn_turned"), sem("xt_hi"), sem("xt_lo")
        s_h, s_r, s_sq, s_r2hi, s_r2lo = sem("hidden"), sem("relu"), sem("square"), sem("square_hi"), sem("square_lo")
        s_y, s_yc, s_back, s_fin = sem("y"), sem("y_copied"), sem("y_back"), sem("final")
        s_out = [sem(f"out{i}") for i in range(4)]
        x_v = x.rearrange("b (g t p) d -> (b g) p t d", t=TB, p=P)
        out_v = out.rearrange("b (g t p) d -> (b g) p t d", t=TB, p=P)
        WEIGHTS = 7
        block = ctx.enter_context(nc.Block())
        LA, LX, LF, LB = 1, 2, 3, 4

        @block.sync
        def _(sp):
            for dst, src in (
                    (wo_in[:], wo.rearrange("(m p) k -> p m k", p=P)),
                    (w1_in[:], w_fc.rearrange("(m p) k -> p m k", p=P)),
                    (w2_in[:], w_proj.rearrange("(m p) k -> p m k", p=P)),
                    (u_in[:], u.rearrange("(m p) r -> p m r", p=P)),
                                        (v_in[:], v),
                    (gate_c[:], gate.rearrange("(a b) -> a b", a=1).to_broadcast((P, 1)))):
                sp.dma_start(dst, src).then_inc(s_in, DMA)
            with nc.allow_non_contiguous_dma(reason="16 by 16, turned"):
                sp.dma_start(fb_t[:], fast_b.rearrange("a b -> b a")).then_inc(s_in, DMA)

            def body(at):
                if q := at(LB):
                    sp.wait_ge(s_fin, q.g * KT + KT)
                    sp.dma_start(out_v[bass.ds(q.g, 1)].rearrange("a p t d -> (a p) t d"), xb[:, q.ring]
                                 ).then_inc(s_out[q.ring], DMA)
                if q := at(0):
                    wait(sp, s_ot, (q.g - 2) * KT + KT)
                    sp.dma_start(ob[:, q.par], o_dram[bass.ds(q.g * GT, GT), :]
                                 .rearrange("(t p) d -> p t d", p=P)).then_inc(s_o[q.par], DMA)
                    wait(sp, s_out[q.ring], q.turn * DMA)
                    sp.dma_start(xb[:, q.ring], x_v[bass.ds(q.g, 1)].rearrange("a p t d -> (a p) t d")
                                 ).then_inc(s_x[q.ring], DMA)

            sweep(sp, body, LB)
            for i in range(4):
                sp.wait_ge(s_out[i], DMA * (G // 4))

        @block.gpsimd
        def _(pool):
            identity(pool, ident[:], s_pool)
            block_mask(pool, tile_of[:], MH, RANK, 0, [s_pool, 2])

            def body(at):
                if q := at(LF):
                    for j in range(MH):
                        pool.wait_ge(s_r, q.g * MH + j + 1)
                        wait(pool, s_r2lo, q.g * MH + j + 1 - 4)
                        pool.tensor_tensor(r2[:, j % 4, :], r[:, j % 4, :], r[:, j % 4, :], ALU.mult
                                           ).then_inc(s_sq, 1)

            sweep(pool, body, LB)

        @block.tensor
        def _(pe):
            pe.wait_ge(s_pool, 5)
            pe.wait_ge(s_in, WEIGHTS * DMA)
            for k in range(KT):
                for m in range(KT):
                    ins = pe.transpose(banks[0][:, k * D + m * P:k * D + m * P + P], wo_in[:, m, k * P:k * P + P],
                                       ident[:])
            ins.then_inc(s_pt, 1)
            pe.transpose(banks[1][:, 0:P], u_in[:].rearrange("p m r -> p (m r)"), ident[:]).then_inc(s_pt, 1)
            pe.wait_ge(s_prep, 1)
            pe.matmul(banks[2][:, 0:D], fb_rep[:].rearrange("a m b -> a (m b)"), v_in[:],
                      start=True, stop=True).then_inc(s_m1, 1)
            pe.wait_ge(s_m1, 2)
            pe.wait_ge(s_pc, 2 + MH)
            for m in range(MH):
                if m % 2 == 0:
                    wait(pe, s_w1, m - 2)
                ins = pe.matmul(banks[4 + m // 2 % 2][:, m % 2 * D:(m % 2 + 1) * D], u_m[:, m, :], low_v[:],
                                start=True, stop=True)
                if m % 2 == 1:
                    ins.then_inc(s_low, 1)
            pe.wait_ge(s_w1, MH)
            for n in range(4):
                k, c = n // 2, n % 2 * GT
                for m in range(TB):
                    ins = pe.transpose(banks[n % 2][:, m * P:m * P + P], w1_low[:, n % 2 * TB + m, k * P:k * P + P],
                                       ident[:])
                ins.then_inc(s_pt, 1)
                pe.wait_ge(s_pc, 2 + MH + n + 1)
            pe.wait_ge(s_tern, 2 * (MH + KT))
            for n in range(4):
                for i in range(2):
                    for m in range(KT):
                        ins = pe.transpose(banks[n % 2][:, i * D + m * P:i * D + m * P + P],
                                           w2_tern[:, m, (2 * n + i) * P:(2 * n + i + 1) * P], ident[:])
                ins.then_inc(s_pt, 1)
                pe.wait_ge(s_pc, 2 + MH + 4 + n + 1)

            def body(at):
                qa, qx, qf, qb = at(LA), at(LX), at(LF), at(LB)

                def back():
                    if not qb:
                        return
                    pe.wait_ge(s_yc, qb.g * KT + KT)
                    for c in range(2):
                        if qf:
                            pe.wait_ge(s_lo, qf.g * KT + c + 1)
                        wait(pe, s_fin, qb.g * KT)
                        for t in range(2):
                            for m in range(KT):
                                ins = pe.transpose(t_bank[c][:, t * D + m * P:t * D + m * P + P],
                                                   yt[:, m, (2 * c + t) * P:(2 * c + t + 1) * P], ident[:])
                        ins.then_inc(s_back, 1)

                def turn_o():
                    if not qa:
                        return
                    pe.wait_ge(s_o[qa.par], (qa.half + 1) * DMA)
                    for k in range(KT):
                        if qb:
                            pe.wait_ge(s_fin, qb.g * KT + k + 1)
                        else:
                            wait(pe, s_lo, (qa.g - 2) * KT + k + 1)
                            wait(pe, s_otc, (qa.g - 1) * KT + k + 1)
                        for t in range(TB):
                            ins = pe.transpose(t_bank[k][:, t * P:t * P + P], ob[:, qa.par, t, k * P:k * P + P],
                                               ident[:])
                        ins.then_inc(s_ot, 1)

                def turn_norm():
                    if not qx:
                        return
                    pe.wait_ge(norm.s_back, norm.done(qx))
                    for k in range(KT):
                        if qa:
                            pe.wait_ge(s_otc, qa.g * KT + k + 1)
                        elif qb:
                            pe.wait_ge(s_fin, qb.g * KT + k + 1)
                        for t in range(TB):
                            ins = pe.transpose(t_bank[k][:, t * P:t * P + P], xn[:, t, k * P:k * P + P], ident[:])
                        ins.then_inc(s_xt, 1)

                def attention_product():
                    if not qa:
                        return
                    pe.wait_ge(s_otc, qa.g * KT + KT)
                    for c in range(2):
                        wait(pe, s_x1, (qa.g - 1) * 2 + c + 1)
                        for t in range(2):
                            for k in range(KT):
                                ins = pe.matmul(a_bank[c][:, t * D:t * D + D],
                                                ot[:, k, (2 * c + t) * P:(2 * c + t + 1) * P], wo_t[:, k, :],
                                                start=(k == 0), stop=(k == KT - 1))
                        ins.then_inc(s_a, 1)

                def hidden(j):
                    if not qf:
                        return
                    if j == 0:
                        pe.wait_ge(s_lo, qf.g * KT + KT)
                    wait(pe, s_r, qf.g * MH + j - 1)
                    three_pass(pe, h_bank[j % 2][:], [w1_hi[:, k, j * P:j * P + P] for k in range(KT)],
                               [w1_lo[:, k, j * P:j * P + P] for k in range(KT)],
                               [xt_hi[:, qf.par, k, :] for k in range(KT)],
                               [xt_lo[:, qf.par, k, :] for k in range(KT)]).then_inc(s_h, 1)

                def output(j):
                    if not qf:
                        return
                    pe.wait_ge(s_r2lo, qf.g * MH + j + 1)
                    for m in range(KT):
                        if j == 0:
                            wait(pe, s_yc, (qf.g - 1) * KT + m + 1)
                        wt = w2_t[:, j, m * P:m * P + P]
                        pe.matmul(y_bank[m][:], wt, r2_hi[:, j % 4, :], start=(j == 0), stop=False)
                        ins = pe.matmul(y_bank[m][:], wt, r2_lo[:, j % 4, :], start=False, stop=(j == MH - 1))
                    ins.then_inc(s_y, 1)

                back()
                hidden(0)
                hidden(1)
                turn_o()
                for j in range(2, MH):
                    hidden(j)
                    output(j - 2)
                turn_norm()
                output(MH - 2)
                attention_product()
                output(MH - 1)

            sweep(pe, body, LB)

        @block.scalar
        def _(act):
            act.wait_ge(s_pt, 1)
            act.activation(wo_t[:].rearrange("p k n -> p (k n)"), banks[0][:], ACT.Copy).then_inc(s_pc, 1)
            act.wait_ge(s_pt, 2)
            act.activation(u_t[:], banks[1][:, 0:P], ACT.Copy).then_inc(s_pc, 1)
            act.wait_ge(s_pc, 2)
            for m in range(MH):
                act.activation(u_m[:, m, :], u_t[:], ACT.Copy, scale=tile_of[:, m:m + 1]).then_inc(s_pc, 1)
            for n in range(4):
                act.wait_ge(s_pt, 2 + n + 1)
                k, c = n // 2, n % 2 * GT
                act.activation(w1_hi[:, k, c:c + GT], banks[n % 2][:], ACT.Copy).then_inc(s_w1hi, 1)
            for n in range(4):
                act.wait_ge(s_pt, 6 + n + 1)
                act.activation(w2_t[:, 2 * n:2 * n + 2, :].rearrange("p a b -> p (a b)"), banks[n % 2][:], ACT.Copy
                               ).then_inc(s_pc, 1)

            def squares(q, j):
                wait(act, s_y, q.g * MH + j + 1 - 4)
                act.activation(r[:, j % 4, :], h_bank[j % 2][:], ACT.Relu).then_inc(s_r, 1)
                act.wait_ge(s_r, q.g * MH + j + 1)
                act.activation(r2_hi[:, j % 4, :], r[:, j % 4, :], ACT.Square).then_inc(s_r2hi, 1)

            def body(at):
                qa, qx, qf, qb = at(LA), at(LX), at(LF), at(LB)
                for j in range(MH):
                    if qf:
                        act.wait_ge(s_h, qf.g * MH + j + 1)
                        wait(act, s_sq, qf.g * MH + j + 1 - 4)
                        squares(qf, j)
                    if j == 1 and qa:
                        for k in range(KT):
                            act.wait_ge(s_ot, qa.g * KT + k + 1)
                            wait(act, s_a, (qa.g - 1) * 2 + 2)
                            act.activation(ot[:, k, :], t_bank[k][:], ACT.Copy).then_inc(s_otc, 1)
                    if j == 3 and qx:
                        norm.root(act, qx)
                if qx:
                    for k in range(KT):
                        act.wait_ge(s_xt, qx.g * KT + k + 1)
                        wait(act, s_h, (qx.g - 2) * MH + MH)
                        act.activation(xt_hi[:, qx.par, k, :], t_bank[k][:], ACT.Copy).then_inc(s_hi, 1)
                if qf:
                    act.wait_ge(s_y, qf.g * MH + MH)
                    wait(act, s_back, (qf.g - 1) * KT + KT)
                    for m in range(KT):
                        act.activation(yt[:, m, :], y_bank[m][:], ACT.Copy, scale=mag2[:, m:m + 1]).then_inc(s_yc, 1)

            sweep(act, body, LB)

        @block.vector
        def _(dve):
            norm.begin(dve)
            dve.wait_ge(s_in, WEIGHTS * DMA)
            dve.tensor_copy(fb_rep[:], fb_t[:].unsqueeze(1).broadcast_to([RANK, MH, RANK])).then_inc(s_prep, 1)
            steps = 0
            for w, mag, half, nhalf, width in ((w1_in, mag1, half1, nhalf1, D), (w2_in, mag2, half2, nhalf2, HID)):
                dve.tensor_reduce(mag[:], w[:], AX.X, ALU.add, apply_absolute_value=True).then_inc(s_scale, 1)
                dve.wait_ge(s_scale, steps + 1)
                dve.tensor_scalar(mag[:], mag[:], 1.0 / width, 1e-5, ALU.mult, ALU.max).then_inc(s_scale, 1)
                dve.wait_ge(s_scale, steps + 2)
                dve.tensor_scalar(half[:], mag[:], 0.5, None, ALU.mult)
                dve.tensor_scalar(nhalf[:], mag[:], -0.5, None, ALU.mult).then_inc(s_scale, 1)
                dve.wait_ge(s_scale, steps + 3)
                steps += 3
            for w, tern, half, nhalf, n in ((w1_in, w1_low, half1, nhalf1, MH), (w2_in, w2_tern, half2, nhalf2, KT)):
                for m in range(n):
                    dve.tensor_scalar(tern[:, m, :], w[:, m, :], nhalf[:, m:m + 1], None, ALU.is_lt).then_inc(s_tern, 1)
            dve.wait_ge(s_tern, MH + KT)
            for w, tern, half, nhalf, n in ((w1_in, w1_low, half1, nhalf1, MH), (w2_in, w2_tern, half2, nhalf2, KT)):
                for m in range(n):
                    ins = dve.scalar_tensor_tensor(out=tern[:, m, :], in0=w[:, m, :], scalar=half[:, m:m + 1],
                                                   in1=tern[:, m, :], op0=ALU.is_gt, op1=ALU.subtract)
                    ins.then_inc(s_tern, 1)
            dve.wait_ge(s_m1, 1)
            dve.tensor_scalar(low_v[:], banks[2][:, 0:D], gate_c[:, 0:1], None, ALU.mult).then_inc(s_m1, 1)
            dve.wait_ge(s_tern, 2 * (MH + KT))
            for m in range(MH):
                if m % 2 == 0:
                    dve.wait_ge(s_low, m // 2 + 1)
                dve.scalar_tensor_tensor(out=w1_low[:, m, :], in0=w1_low[:, m, :], scalar=mag1[:, m:m + 1],
                                         in1=banks[4 + m // 2 % 2][:, m % 2 * D:(m % 2 + 1) * D],
                                         op0=ALU.mult, op1=ALU.add).then_inc(s_w1, 1)
            for n in range(4):
                k, c = n // 2, n % 2 * GT
                dve.wait_ge(s_w1hi, n + 1)
                dve.tensor_tensor(w1_lo[:, k, c:c + GT], banks[n % 2][:], w1_hi[:, k, c:c + GT].bitcast(F32),
                                  ALU.subtract).then_inc(s_pc, 1)

            def low_of_squares(q, j):
                dve.wait_ge(s_r2hi, q.g * MH + j + 1)
                dve.wait_ge(s_sq, q.g * MH + j + 1)
                dve.tensor_tensor(r2_lo[:, j % 4, :], r2[:, j % 4, :], r2_hi[:, j % 4, :].bitcast(F32), ALU.subtract
                                  ).then_inc(s_r2lo, 1)

            def body(at):
                qa, qx, qf, qb = at(LA), at(LX), at(LF), at(LB)
                if qb:
                    for c in range(2):
                        dve.wait_ge(s_back, qb.g * KT + c + 1)
                        rows = xb[:, qb.ring, 2 * c:2 * c + 2, :].rearrange("p t d -> p (t d)")
                        dve.tensor_tensor(rows, t_bank[c][:], rows, ALU.add).then_inc(s_fin, 1)
                for j in range(MH):
                    if qf:
                        low_of_squares(qf, j)
                    if j == 1 and qx:
                        dve.wait_ge(s_x1, qx.g * 2 + 2)
                        norm.front(dve, xb[:, qx.ring], qx)
                    if j == 3 and qx:
                        wait(dve, s_xt, (qx.g - 1) * KT + KT)
                        norm.back(dve, xb[:, qx.ring], xn[:], qx)
                    if j == MH - 3 and qx:
                        for k in range(KT):
                            dve.wait_ge(s_hi, qx.g * KT + k + 1)
                            dve.tensor_tensor(xt_lo[:, qx.par, k, :], t_bank[k][:],
                                              xt_hi[:, qx.par, k, :].bitcast(F32), ALU.subtract).then_inc(s_lo, 1)
                if qa:
                    dve.wait_ge(s_x[qa.ring], (qa.turn + 1) * DMA)
                    for c in range(2):
                        dve.wait_ge(s_a, qa.g * 2 + c + 1)
                        rows = xb[:, qa.ring, 2 * c:2 * c + 2, :].rearrange("p t d -> p (t d)")
                        dve.tensor_tensor(rows, a_bank[c][:], rows, ALU.add).then_inc(s_x1, 1)

            sweep(dve, body, LB)


def layer(nc, x, wq, wk, wv, wo, fast_b, w_fc, w_proj, u, v, gate, out):
    qk_dram = nc.dram_tensor("qk_parts", [2, 3, D, N], BF16, kind="Internal").ap()
    kf_dram = nc.dram_tensor("k_whole", [D, N], F32, kind="Internal").ap()
    va_dram = nc.dram_tensor("v_ones", [N, VROW], F32, kind="Internal").ap()
    o_dram = nc.dram_tensor("attention", [N, D], F32, kind="Internal").ap()
    stage_project(nc, x, (wq, wk, wv), qk_dram, kf_dram, va_dram)
    stage_attend(nc, qk_dram, va_dram, o_dram)
    stage_row_zero(nc, qk_dram, kf_dram, va_dram, o_dram)
    stage_feed(nc, x, o_dram, wo, fast_b, w_fc, w_proj, u, v, gate, out)


_INS = ["x", "Wq", "Wk", "Wv", "Wo", "fast_b", "w_fc", "w_proj", "u", "v", "gate"]


def kernel(**inputs):
    import concourse.bacc as bacc
    from concourse.bass_utils import run_bass_kernel_spmd

    nc = bacc.Bacc("TRN2", target_bir_lowering=False, num_devices=1)
    arrays, args = {}, []
    for name in _INS:
        key = ("L0_attn_" if name[0] == "W" or name == "x" else "L0_ffn_") + name
        a = np.ascontiguousarray(inputs[key])
        if a.ndim == 0:
            a = a.reshape(1)
        arrays[f"in_{name}"] = a
        args.append(nc.dram_tensor(f"in_{name}", a.shape, mybir.dt.from_np(a.dtype), kind="ExternalInput").ap())
    out = nc.dram_tensor("out", (B, T, D), F32, kind="ExternalOutput").ap()
    layer(nc, *args, out)
    r = run_bass_kernel_spmd(nc, [arrays], core_ids=[0])
    return r.results[0]["out"]
```

```python
from contextlib import ExitStack

import numpy as np

import concourse.bass as bass
from concourse import mybir

ACT = mybir.ActivationFunctionType
ALU = mybir.AluOpType
AX = mybir.AxisListType
F32 = mybir.dt.float32
F32R = mybir.dt.float32r
BF16 = mybir.dt.bfloat16

P = 128
B, T, D = 4, 2048, 256
H, HD = 16, 16
HID = 1024
RANK = 16
N = B * T
KT = D // P
GT = 512
TB = GT // P
G = N // GT
GB = T // GT
VW = HD + 1
VROW = H * VW
EPS = 1e-5
QSCALE = 1.0 / float(np.sqrt(HD))
NEG = -3.0e38
ROUND = 4
DMA = 16
HIGH, MID, LOW = 0, 1, 2
PLACE = ({LOW: 0, MID: 1, HIGH: 2}, {HIGH: 0, MID: 1, LOW: 2})
SLOTS = 6
SINGLES = ((MID, HIGH, HIGH), (HIGH, MID, HIGH))
SLOT_ROWS = SLOTS * HD
SHIFT_ROWS = 3
NQ = 4
UPG = H // NQ
UNITS = G * UPG
UPB = GB * UPG
WIN = GT + 2 * P


class Group:

    def __init__(self, i, k):
        self.g = i * ROUND + k
        self.par, self.half = k % 2, i * (ROUND // 2) + k // 2
        self.ring, self.turn = k % 4, i * (ROUND // 4) + k // 4


def wait(eng, sem, value):
    if isinstance(value, int) and value <= 0:
        return
    eng.wait_ge(sem, value)


class Turn:

    def __init__(self, eng, sem, name, start, step=1):
        self.eng, self.sem, self.step = eng, sem, step
        self.value = eng.alloc_register(name)
        self.looped = False
        eng.reg_mov(self.value, start)

    def wait(self, value):
        self.looped = self.looped or not isinstance(value, int)
        if self.looped and isinstance(value, int):
            self.eng.wait_ge(self.sem, value)
        else:
            self.eng.wait_ge(self.sem, self.value)
            self.eng.reg_add(self.value, self.value, self.step)


def sweep(eng, body, lags):
    def fixed(it):
        return lambda lag: Group(0, it - lag) if 0 <= it - lag < G else None

    first = -(-lags // ROUND)
    for it in range(first * ROUND):
        body(fixed(it))
    with eng.Fori(first, G // ROUND) as i:
        for p in range(ROUND):
            body(lambda lag, p=p: Group(i, p - lag))
    for it in range(G, G + lags):
        body(fixed(it))


def identity(pool, tile, sem):
    pool.memset(tile, 1.0).then_inc(sem, 1)
    pool.wait_ge(sem, 1)
    pool.affine_select(out=tile, in_=tile, compare_op=ALU.is_equal, fill=0.0, base=0,
                       pattern=[[-1, P]], channel_multiplier=1).then_inc(sem, 1)


class Norm:

    STEPS = 9

    def __init__(self, nc, ctx, name):
        def sb(n, shape):
            return ctx.enter_context(nc.sbuf_tensor(f"{name}_{n}", shape, F32))
        self.name = name
        self.stats = sb("stats", [P, TB, 6])
        self.mv = sb("meanvar", [P, 2, TB, 2])
        self.ve = sb("var_eps", [P, 2, TB])
        self.sd = sb("stddev", [P, 2, TB])
        self.r0 = sb("rstd_first", [P, TB])
        self.t0 = sb("newton", [P, TB])
        self.rs = sb("rstd", [P, TB])
        self.s_step = ctx.enter_context(nc.semaphore(f"{name}_step"))
        self.s_sd = ctx.enter_context(nc.semaphore(f"{name}_sd"))
        self.s_back = ctx.enter_context(nc.semaphore(f"{name}_back"))

    def begin(self, v):
        self.stats_turn = Turn(v, self.s_step, f"{self.name}_stats_turn", 1, 3)

    def front(self, v, x, q):
        par, base = q.par, q.g * 3
        for t in range(TB):
            ins = v.bn_stats(self.stats[:, t, :], x[:, t, :])
        ins.then_inc(self.s_step, 1)
        self.stats_turn.wait(base + 1)
        for t in range(TB):
            ins = v.bn_aggr(self.mv[:, par, t, :], self.stats[:, t, :])
        ins.then_inc(self.s_step, 1)
        v.wait_ge(self.s_step, base + 2)
        v.tensor_scalar(self.ve[:, par, :], self.mv[:, par, :, 1], EPS, None, ALU.add).then_inc(self.s_step, 1)

    def root(self, a, q):
        a.wait_ge(self.s_step, q.g * 3 + 3)
        a.activation(self.sd[:, q.par, :], self.ve[:, q.par, :], ACT.Sqrt).then_inc(self.s_sd, 1)

    def back(self, v, x, xn, q):
        par, base = q.par, q.g * 6
        v.wait_ge(self.s_sd, q.g + 1)
        v.reciprocal(self.r0[:], self.sd[:, par, :]).then_inc(self.s_back, 1)
        v.wait_ge(self.s_back, base + 1)
        v.tensor_tensor(self.t0[:], self.ve[:, par, :], self.r0[:], ALU.mult).then_inc(self.s_back, 1)
        v.wait_ge(self.s_back, base + 2)
        v.tensor_tensor(self.t0[:], self.t0[:], self.r0[:], ALU.mult).then_inc(self.s_back, 1)
        v.wait_ge(self.s_back, base + 3)
        v.tensor_scalar(self.t0[:], self.t0[:], -0.5, 1.5, ALU.mult, ALU.add).then_inc(self.s_back, 1)
        v.wait_ge(self.s_back, base + 4)
        v.tensor_tensor(self.rs[:], self.t0[:], self.r0[:], ALU.mult).then_inc(self.s_back, 1)
        v.wait_ge(self.s_back, base + 5)
        for t in range(TB):
            ins = v.tensor_scalar(xn[:, t, :], x[:, t, :], self.mv[:, par, t, 0:1], self.rs[:, t:t + 1],
                                  ALU.subtract, ALU.mult)
        ins.then_inc(self.s_back, 1)

    def done(self, q):
        return q.g * 6 + 6


def three_pass(pe, out, lhs_hi, lhs_lo, rhs_hi, rhs_lo):
    n = len(lhs_hi)
    for k in range(n):
        pe.matmul(out, lhs_hi[k], rhs_hi[k], start=(k == 0), stop=False)
        pe.matmul(out, lhs_hi[k], rhs_lo[k], start=False, stop=False)
        ins = pe.matmul(out, lhs_lo[k], rhs_hi[k], start=False, stop=(k == n - 1))
    return ins


def stage_project(nc, x, weights, qk_dram, kf_dram, va_dram):
    with ExitStack() as ctx:
        def sb(name, shape, dt=F32):
            return ctx.enter_context(nc.sbuf_tensor(f"p_{name}", shape, dt))

        def sem(name):
            return ctx.enter_context(nc.semaphore(f"p_{name}"))

        ident = sb("ident", [P, P])
        w_in = sb("w_in", [P, 3, KT, D])
        wt_hi = sb("wt_hi", [P, 3, KT, D], F32R)
        wt_lo = sb("wt_lo", [P, 3, KT, D], F32R)
        xb = sb("x", [P, 4, TB, D])
        xn = sb("xn", [P, 2, TB, D])
        xt_hi = sb("xt_hi", [P, 2, KT, GT], F32R)
        xt_lo = sb("xt_lo", [P, 2, KT, GT], F32R)
        parts = sb("parts", [P, 2, 2 * KT, 3, GT], BF16)
        rest = sb("rest", [P, 2 * KT, GT])
        kf = sb("kf", [P, 2, KT, GT])
        va = sb("va", [P, 2, TB, H, VW])
        banks = [ctx.enter_context(nc.psum_tensor(f"p_bank{i}", [P, GT], F32)) for i in range(8)]
        t_bank, qk_bank, v_bank = banks[0:2], banks[2:6], banks[6:8]
        norm = Norm(nc, ctx, "n1")

        s_w, s_id, s_ones = sem("weights_in"), sem("ident"), sem("ones")
        s_wt, s_whi, s_wlo = sem("w_turned"), sem("w_hi"), sem("w_lo")
        s_x = [sem(f"x_in{i}") for i in range(4)]
        s_t, s_hi, s_lo = sem("turned"), sem("xt_hi"), sem("xt_lo")
        s_qk, s_v = sem("qk"), sem("v")
        s_high, s_rest, s_mid, s_low, s_vout = (
            sem("high"), sem("rest"), sem("mid"), sem("low"), sem("v_out"))
        s_out = [sem("out0"), sem("out1")]
        STORES = 2 * KT + 2

        x_v = x.rearrange("b (g t p) d -> (b g) p t d", t=TB, p=P)
        LN, LT, LP = 1, 2, 3
        block = ctx.enter_context(nc.Block())

        @block.sync
        def _(sp):
            for w in range(3):
                sp.dma_start(w_in[:, w], weights[w].rearrange("(m p) k -> p m k", p=P)).then_inc(s_w, DMA)

            def body(at):
                if q := at(0):
                    wait(sp, norm.s_back, (q.g - 4) * 6 + 6)
                    sp.dma_start(xb[:, q.ring], x_v[bass.ds(q.g, 1)].rearrange("a p t d -> (a p) t d")
                                 ).then_inc(s_x[q.ring], DMA)
                if q := at(LP):
                    cols = bass.ds(q.g * GT, GT)
                    for u in range(2 * KT):
                        k = u % KT * P
                        sp.wait_ge(s_low, q.g * 4 + u + 1)
                        sp.dma_start(qk_dram[u // KT, k:k + P, :, cols], parts[:, q.par, u]
                                     ).then_inc(s_out[q.par], DMA)
                    sp.dma_start(kf_dram[:, cols].rearrange("(m p) t -> p m t", p=P),
                                 kf[:, q.par]).then_inc(s_out[q.par], DMA)
                    sp.wait_ge(s_vout, q.g * 2 + 2)
                    sp.dma_start(va_dram[cols, :].rearrange("(t p) n -> p t n", p=P),
                                 va[:, q.par].rearrange("p t h e -> p t (h e)")).then_inc(s_out[q.par], DMA)

            sweep(sp, body, LP)
            for par in range(2):
                sp.wait_ge(s_out[par], DMA * STORES * (G // 2))

        @block.gpsimd
        def _(pool):
            pool.memset(va[:, :, :, :, HD:VW], 1.0).then_inc(s_ones, 1)
            identity(pool, ident[:], s_id)

            def body(at):
                if q := at(LP):
                    for u in range(2 * KT):
                        pool.wait_ge(s_mid, q.g * 4 + u + 1)
                        pool.tensor_tensor(parts[:, q.par, u, PLACE[u // KT][LOW], :], rest[:, u, :],
                                           parts[:, q.par, u, PLACE[u // KT][MID], :], ALU.subtract).then_inc(s_low, 1)

            sweep(pool, body, LP)

        @block.tensor
        def _(pe):
            pe.wait_ge(s_id, 2)
            for w in range(3):
                pe.wait_ge(s_w, 3 * DMA)
                for k in range(KT):
                    for m in range(KT):
                        ins = pe.transpose(banks[w][:, k * D + m * P:k * D + m * P + P],
                                           w_in[:, w, m, k * P:k * P + P], ident[:])
                ins.then_inc(s_wt, 1)
            pe.wait_ge(s_wlo, 3)

            def body(at):
                def turn():
                    if q := at(LT):
                        pe.wait_ge(norm.s_back, norm.done(q))
                        for k in range(KT):
                            wait(pe, s_lo, (q.g - 1) * KT + k + 1)
                            for t in range(TB):
                                ins = pe.transpose(t_bank[k][:, t * P:t * P + P],
                                                   xn[:, q.par, t, k * P:k * P + P], ident[:])
                            ins.then_inc(s_t, 1)

                q = at(LP)
                if q:
                    pe.wait_ge(s_lo, q.g * KT + KT)
                    xh = [xt_hi[:, q.par, k, :] for k in range(KT)]
                    xl = [xt_lo[:, q.par, k, :] for k in range(KT)]
                for u in range(2 * KT):
                    if u == KT + 1:
                        turn()
                    if q:
                        w, m = u // KT, (u % KT) * P
                        wait(pe, s_rest, (q.g - 1) * 4 + u + 1)
                        three_pass(pe, qk_bank[u][:], [wt_hi[:, w, k, m:m + P] for k in range(KT)],
                                   [wt_lo[:, w, k, m:m + P] for k in range(KT)], xh, xl).then_inc(s_qk, 1)
                if q:
                    for c in range(2):
                        wait(pe, s_vout, (q.g - 1) * 2 + c + 1)
                        for t in range(2):
                            cut = slice((2 * c + t) * P, (2 * c + t + 1) * P)
                            ins = three_pass(pe, v_bank[c][:, t * D:t * D + D], [a[:, cut] for a in xh],
                                             [a[:, cut] for a in xl], [wt_hi[:, 2, k, :] for k in range(KT)],
                                             [wt_lo[:, 2, k, :] for k in range(KT)])
                        ins.then_inc(s_v, 1)

            sweep(pe, body, LP)

        @block.scalar
        def _(act):
            for w in range(3):
                act.wait_ge(s_wt, w + 1)
                act.activation(wt_hi[:, w].rearrange("p k n -> p (k n)"), banks[w][:], ACT.Copy).then_inc(s_whi, 1)

            def mid(q, u):
                act.wait_ge(s_rest, q.g * 4 + u + 1)
                act.activation(parts[:, q.par, u, PLACE[u // KT][MID], :], rest[:, u, :], ACT.Copy).then_inc(s_mid, 1)

            def body(at):
                if q := at(LT):
                    norm.root(act, q)
                q = at(LP)
                if q:
                    wait(act, s_out[q.par], q.half * DMA * STORES)
                for u in range(2 * KT):
                    if q:
                        act.wait_ge(s_qk, q.g * 4 + u + 1)
                        if u >= KT:
                            act.activation(kf[:, q.par, u - KT, :], qk_bank[u][:], ACT.Copy)
                        act.activation(parts[:, q.par, u, PLACE[u // KT][HIGH], :], qk_bank[u][:], ACT.Copy,
                                       scale=QSCALE if u < KT else 1.0).then_inc(s_high, 1)
                    if u == KT and (t := at(LT)):
                        wait(act, s_v, (t.g - 2) * 2 + 2)
                        for k in range(KT):
                            act.wait_ge(s_t, t.g * KT + k + 1)
                            act.activation(xt_hi[:, t.par, k, :], t_bank[k][:], ACT.Copy).then_inc(s_hi, 1)
                    if q and u:
                        mid(q, u - 1)
                if q:
                    mid(q, 2 * KT - 1)
                    if isinstance(q.g, int) and q.g == 0:
                        act.wait_ge(s_ones, 1)
                    for c in range(2):
                        act.wait_ge(s_v, q.g * 2 + c + 1)
                        for t in range(2):
                            ins = act.activation(va[:, q.par, 2 * c + t, :, 0:HD],
                                                 v_bank[c][:, t * D:t * D + D].rearrange("p (h e) -> p h e", h=H),
                                                 ACT.Copy)
                        ins.then_inc(s_vout, 1)

            sweep(act, body, LP)

        @block.vector
        def _(dve):
            norm.begin(dve)
            for w in range(3):
                dve.wait_ge(s_whi, w + 1)
                dve.tensor_tensor(wt_lo[:, w].rearrange("p k n -> p (k n)"), banks[w][:],
                                  wt_hi[:, w].bitcast(F32).rearrange("p k n -> p (k n)"),
                                  ALU.subtract).then_inc(s_wlo, 1)

            def body(at):
                if q := at(LT):
                    wait(dve, s_t, (q.g - 2) * KT + KT)
                    norm.back(dve, xb[:, q.ring], xn[:, q.par], q)
                q = at(LP)
                for u in range(2 * KT):
                    if q:
                        dve.wait_ge(s_high, q.g * 4 + u + 1)
                        wait(dve, s_low, (q.g - 1) * 4 + u + 1)
                        dve.scalar_tensor_tensor(out=rest[:, u, :], in0=qk_bank[u][:],
                                                 scalar=QSCALE if u < KT else 1.0,
                                                 in1=parts[:, q.par, u, PLACE[u // KT][HIGH], :],
                                                 op0=ALU.mult, op1=ALU.subtract).then_inc(s_rest, 1)
                    if u == KT and (t := at(LT)):
                        for k in range(KT):
                            dve.wait_ge(s_hi, t.g * KT + k + 1)
                            dve.tensor_tensor(xt_lo[:, t.par, k, :], t_bank[k][:],
                                              xt_hi[:, t.par, k, :].bitcast(F32), ALU.subtract).then_inc(s_lo, 1)
                if q := at(LN):
                    dve.wait_ge(s_x[q.ring], (q.turn + 1) * DMA)
                    norm.front(dve, xb[:, q.ring], q)

            sweep(dve, body, LP)


class Unit:

    def __init__(self, b, i):
        self.i, self.gi, self.hq = i, i // UPG, i % UPG
        self.n = b * UPB + i
        self.g = b * GB + self.gi
        self.batch = b
        self.gpar = self.gi % 2
        self.ghalf = b * (GB // 2) + self.gi // 2
        self.upar = i % 2
        self.uhalf = b * (UPB // 2) + i // 2


def march(eng, body, lags):
    def step(b, i):
        def at(lag):
            j = i - lag
            if j >= 0:
                return Unit(b, j) if not isinstance(b, int) or b < B else None
            if isinstance(b, int) and b == 0:
                return None
            return Unit(b - 1, j + UPB)
        return at

    for i in range(UPB):
        body(step(0, i))
    with eng.Fori(1, B) as b:
        for i in range(UPB):
            body(step(b, i))
    for i in range(lags):
        body(step(B, i))


SCORE_TILES = ((0, 0, 1, 0, 3), (0, 3, -1, 0, 1),
               (1, 0, 0, 0, 2), (1, 2, 3, 2, 2),
               (2, 0, 4, 3, 1), (2, 1, 2, 1, 3))
HEAD_COLS = 3 * GT
CUT_LOW = ((0, 1), (6, 1), (8, 2))
CUT_HIGH = ((2, 2), (5, 1), (11, 1))
SUM_ORDER = (1, 2, 0, 3, -1, 4)
CHUNK = 2 * GT
CHUNKS = NQ * HEAD_COLS // CHUNK
TILES = NQ * TB
TURN_OF_M, TURN_OF_S, TURN_BANKS = 3, 7, 3
TURN_OF_TILE = tuple(j if j < 3 else j + 1 if j < 6 else j + 2 for j in range(TILES))
TILE_OF_TURN = {k: j for j, k in enumerate(TURN_OF_TILE)}
TURNS = TILES + 2
assert TURNS % TURN_BANKS == 0

L_KEY0, L_MAX, L_SHIFT, L_SCORE, L_SUM, L_OUT = 2, 3, 4, 5, 6, 7


AFTER_TILE = (
    (("score", 0), ("score", 1)), (("score", 2), ("score", 3)), (("M", 0),), (("score", 4), ("score", 5)),
    (("sum", 0),), (("S", 0), ("score", 6)), (("score", 7),), (("sum", 1),),
    (("score", 8), ("score", 9)), (("sum", 2),), (("score", 10), ("score", 11)), (("sum", 3),),
    (), (("sum", 4),), (), (("sum", 5),))


def in_group(gi, kb):
    return not (gi == 0 and kb == -1) and not (gi == GB - 1 and kb == TB)


def stage_attend(nc, qk_dram, va_dram, o_dram):
    with ExitStack() as ctx:
        def sb(name, shape, dt=F32):
            return ctx.enter_context(nc.sbuf_tensor(f"a_{name}", shape, dt))

        def sem(name):
            return ctx.enter_context(nc.semaphore(f"a_{name}"))

        rows = SLOT_ROWS + SHIFT_ROWS
        kw = [[sb(f"k{g}{q}", [P, NQ, WIN], BF16) for q in range(UPG)] for g in range(2)]
        qw = [[sb(f"q{g}{q}", [P, NQ, GT], BF16) for q in range(UPG)] for g in range(2)]
        vw = sb("v", [P, 2, TB + 2, VROW])
        v0 = sb("v0", [P, VROW])
        k0 = sb("k0", [P, H], BF16)
        ident = sb("ident", [P, P])
        band = sb("band", [P, 3 * P + 1], BF16)
        gate0 = sb("gate0", [P, NQ, TB])
        masked = sb("masked", [P, TILES, 3 * P + 1])
        mx = sb("max", [P, UPG, P])
        d0 = sb("d0", [P, 2, TILES])
        p0 = sb("p0", [P, UPG, NQ, TB])
        neg = sb("neg", [TILES, P])
        rest = sb("neg_rest", [TILES, P])
        shift = sb("shift", [TILES, 2, SHIFT_ROWS, P], BF16)
        pe_w = sb("weights", [P, 2, NQ * HEAD_COLS])
        sums = sb("sums", [P, 2, GT])
        t0 = sb("key0_part", [P, UPG, TB, NQ, HD])
        den = sb("den", [P, 2, TB, NQ])
        rden = sb("rden", [P, 2, TB, NQ])
        num = sb("num", [P, 2, TB, NQ, HD])
        ob = sb("o", [P, 2, TB, D])
        score = [ctx.enter_context(nc.psum_tensor(f"a_score{i}", [P, CHUNK], F32)) for i in range(2)]
        sum_bank = ctx.enter_context(nc.psum_tensor("a_sum", [P, GT], F32))
        turn = [ctx.enter_context(nc.psum_tensor(f"a_turn{i}", [P, GT], F32)) for i in range(TURN_BANKS)]

        s_init, s_pool, s_ones = sem("init"), sem("pool_init"), sem("ones")
        s_load = [[sem(f"qk_in{g}{q}") for q in range(UPG)] for g in range(2)]
        s_v, s_v0 = [sem("v_in0"), sem("v_in1")], sem("v0_in")
        s_row = [sem("row0"), sem("row1")]
        s_k0 = sem("k0")
        s_tile, s_tile_read = sem("tile"), sem("tile_read")
        s_m, s_m_read, s_s, s_s_read = sem("m"), sem("m_read"), sem("s"), sem("s_read")
        s_den = sem("den")
        s_d0, s_p0 = sem("d0"), sem("p0")
        s_shift = sem("shift")
        s_score, s_exp, s_cut = sem("score"), sem("exp"), sem("cut")
        s_sum, s_sumout = sem("sum"), sem("sum_out")
        s_t0, s_gate = sem("t0"), sem("gate")
        s_num, s_o = sem("num"), sem("o")
        s_out = [sem("out0"), sem("out1")]
        LOADS = 2 * (1 + len(SINGLES[0]))
        block = ctx.enter_context(nc.Block())

        def window(gi):
            return (1 if gi == 0 else 0), (TB + 1 if gi == GB - 1 else TB + 2)

        @block.sync
        def _(sp):
            def body(at):
                if u := at(0):
                    wait(sp, s_score, (u.n - 2 * UPG) * CHUNKS + CHUNKS)
                    lo, hi = window(u.gi)
                    h0 = u.hq * NQ
                    keys = bass.ds(u.g * GT + (lo - 1) * P, (hi - lo) * P)
                    queries = bass.ds(u.g * GT, GT)
                    for which, buf, cols, tokens in ((1, kw[u.gpar][u.hq], slice(lo * P, hi * P), keys),
                                                     (0, qw[u.gpar][u.hq], slice(0, GT), queries)):
                        rows_of = qk_dram[which, h0 * HD:(h0 + NQ) * HD, :, tokens]
                        sp.dma_start(buf[0:3 * HD, :, cols], rows_of.rearrange("(h d) s t -> (d s) h t", d=HD)
                                     ).then_inc(s_load[u.gpar][u.hq], DMA)
                        for n, part in enumerate(SINGLES[which]):
                            sp.dma_start(buf[(3 + n) * HD:(4 + n) * HD, :, cols],
                                         rows_of[:, PLACE[which][part], :].rearrange("(h d) t -> d h t", d=HD)
                                         ).then_inc(s_load[u.gpar][u.hq], DMA)
                if (u := at(L_MAX)) and u.hq == 0:
                    wait(sp, s_sum, (u.n - UPG * 2) + UPG)
                    lo, hi = window(u.gi)
                    sp.dma_start(vw[:, u.gpar, lo:hi, :],
                                 va_dram[bass.ds(u.g * GT + (lo - 1) * P, (hi - lo) * P), :]
                                 .rearrange("(w p) n -> p w n", p=P)).then_inc(s_v[u.gpar], DMA)
                if (u := at(L_SCORE)) and u.i == 0:
                    wait(sp, s_t0, u.n)
                    sp.dma_start(v0[:], va_dram[bass.ds(u.batch * T, 1), :].to_broadcast((P, VROW))
                                 ).then_inc(s_v0, DMA)
                if u := at(L_SHIFT):
                    sp.wait_ge(s_shift, u.n * 3 + 3)
                    for part in range(SHIFT_ROWS):
                        row = qw[u.gpar][u.hq][SLOT_ROWS + part:SLOT_ROWS + part + 1, :, :]
                        sp.dma_start(row.rearrange("s h (t q) -> s (h t) q", q=P),
                                     shift[:, u.upar, part, :]).then_inc(s_row[u.upar], DMA)
                if (u := at(L_OUT)) and u.hq == UPG - 1:
                    sp.wait_ge(s_o, u.n + 1)
                    sp.dma_start(o_dram[bass.ds(u.g * GT, GT), :].rearrange("(t p) d -> p t d", p=P),
                                 ob[:, u.gpar]).then_inc(s_out[u.gpar], DMA)

            march(sp, body, L_OUT)
            for par in range(2):
                sp.wait_ge(s_out[par], DMA * (G // 2))

        @block.gpsimd
        def _(pool):
            identity(pool, ident[:], s_pool)
            pool.memset(band[:], 0.0).then_inc(s_pool, 1)
            pool.wait_ge(s_pool, 3)
            pool.affine_select(out=band[:, 0:P], in_=band[:, 0:P], compare_op=ALU.is_ge, fill=NEG, base=0,
                               pattern=[[1, P]], channel_multiplier=-1)
            pool.affine_select(out=band[:, 2 * P:3 * P], in_=band[:, 2 * P:3 * P], compare_op=ALU.is_ge,
                               fill=NEG, base=0, pattern=[[-1, P]], channel_multiplier=1)
            pool.memset(gate0[:], 1.0).then_inc(s_pool, 1)
            pool.wait_ge(s_pool, 4)
            pool.affine_select(out=gate0[:], in_=gate0[:], compare_op=ALU.is_gt, fill=0.0, base=-P,
                               pattern=[[0, NQ], [P, TB]], channel_multiplier=1).then_inc(s_pool, 1)

            pool.wait_ge(s_pool, 5)
            for g in range(2):
                for q in range(UPG):
                    pool.memset(kw[g][q][SLOT_ROWS:rows, :, :], 1.0).then_inc(s_ones, 1)
                    pool.wait_ge(s_ones, g * UPG + q + 1)
            exp_turn = Turn(pool, s_exp, "exp_turn", CHUNKS // 2, CHUNKS // 2)

            def cut_half(u, half):
                exp_turn.wait(u.n * CHUNKS + (half + 1) * CHUNKS // 2)
                w = pe_w[:, u.upar].rearrange("p (h c q) -> p h c q", h=NQ, q=P)
                for runs, sign in ((CUT_LOW, 1), (CUT_HIGH, -1)):
                    for c, m in runs:
                        cut = w[:, half * NQ // 2:(half + 1) * NQ // 2, c:c + m, :]
                        ins = pool.affine_select(out=cut, in_=cut, compare_op=ALU.is_ge, fill=0.0, base=0,
                                                 pattern=[[0, NQ // 2], [0, m], [sign, P]],
                                                 channel_multiplier=-sign)
                ins.then_inc(s_cut, 1)

            def body(at):
                if u := at(L_SCORE):
                    pool.wait_ge(s_p0, u.n + 1)
                    if u.gi == 0:
                        pool.tensor_tensor(p0[:, u.hq], p0[:, u.hq], gate0[:], ALU.mult).then_inc(s_gate, 1)
                        pool.wait_ge(s_gate, u.batch * UPG + u.hq + 1)
                    if u.i == 0:
                        pool.wait_ge(s_v0, (u.batch + 1) * DMA)
                    wait(pool, s_num, u.n - 3)
                    values = v0[:, u.hq * NQ * VW:(u.hq + 1) * NQ * VW].rearrange("p (h e) -> p h e", h=NQ)
                    pool.tensor_tensor(
                        t0[:, u.hq], values[:, :, 0:HD].unsqueeze(1).broadcast_to([P, TB, NQ, HD]),
                        p0[:, u.hq].rearrange("p h t -> p t h").unsqueeze(3).broadcast_to([P, TB, NQ, HD]),
                        ALU.mult).then_inc(s_t0, 1)
                    cut_half(u, 0)
                if u := at(L_OUT):
                    pool.wait_ge(s_num, u.n + 1)
                    if u.hq == 0:
                        wait(pool, s_out[u.gpar], u.ghalf * DMA)
                    o = ob[:, u.gpar].rearrange("p t (h e) -> p t h e", e=HD)[:, :, u.hq * NQ:(u.hq + 1) * NQ, :]
                    pool.tensor_tensor(o, num[:, u.upar], rden[:, u.upar].unsqueeze(3).broadcast_to([P, TB, NQ, HD]),
                                       ALU.mult).then_inc(s_o, 1)
                if u := at(L_SCORE):
                    cut_half(u, 1)

            march(pool, body, L_OUT)

        @block.tensor
        def _(pe):
            pe.wait_ge(s_init, 4)
            pe.wait_ge(s_pool, 2)

            def body(at):
                um, ux, us, up, uo = at(L_SHIFT), at(L_MAX), at(L_SCORE), at(L_SUM), at(L_OUT)

                def bank_read(k):
                    before = k - TURN_BANKS
                    if before < 0:
                        if ux:
                            wait(pe, s_tile_read, (ux.n - 1) * TILES + TILE_OF_TURN[before + TURNS] + 1)
                    elif before == TURN_OF_M and um:
                        pe.wait_ge(s_m_read, um.n + 1)
                    elif before == TURN_OF_S and uo:
                        pe.wait_ge(s_s_read, uo.n + 1)
                    elif ux:
                        tile = TILE_OF_TURN.get(before, TILE_OF_TURN.get(before - TURN_BANKS))
                        pe.wait_ge(s_tile_read, ux.n * TILES + tile + 1)
                    else:
                        pe.wait_ge(s_tile_read, UNITS * TILES)
                        if k == TURN_OF_S:
                            pe.wait_ge(s_s_read, uo.n)

                def maxima_turned():
                    if um:
                        pe.wait_ge(s_d0, um.n + 1)
                        bank_read(TURN_OF_M)
                        pe.transpose(turn[TURN_OF_M % TURN_BANKS][:, 0:P], mx[:, um.hq, :], ident[:]
                                     ).then_inc(s_m, 1)

                def sums_turned():
                    if uo:
                        pe.wait_ge(s_sumout, uo.n + 1)
                        bank_read(TURN_OF_S)
                        for t in range(TB):
                            ins = pe.transpose(turn[TURN_OF_S % TURN_BANKS][:, t * P:t * P + P],
                                               sums[:, uo.upar, t * P:t * P + P], ident[:])
                        ins.then_inc(s_s, 1)

                def max_tile(j):
                    if not ux:
                        return
                    k = TURN_OF_TILE[j]
                    h, t = j // TB, j % TB
                    if j == 0:
                        pe.wait_ge(s_load[ux.gpar][ux.hq], (ux.ghalf + 1) * LOADS * DMA)
                        if ux.gi == 0:
                            pe.wait_ge(s_k0, ux.batch * UPG + ux.hq + 1)
                    bank_read(k)
                    lo = P if ux.gi == 0 and t == 0 else 0
                    hi = 2 * P if ux.gi == GB - 1 and t == TB - 1 else 3 * P
                    q, kk = qw[ux.gpar][ux.hq], kw[ux.gpar][ux.hq]
                    lhs = q[0:SLOT_ROWS, h, t * P:t * P + P]
                    pe.matmul(turn[k % TURN_BANKS][:, lo:hi], lhs, kk[0:SLOT_ROWS, h, t * P + lo:t * P + hi],
                              start=True, stop=True)
                    key = ux.hq * NQ + h
                    pe.matmul(turn[k % TURN_BANKS][:, hi:hi + 1], lhs, k0[0:SLOT_ROWS, key:key + 1],
                              start=True, stop=True).then_inc(s_tile, 1)

                def score_bank(n):
                    if not us:
                        return
                    c = n // 2
                    if n == 0:
                        if isinstance(us.n, int) and us.n < 2 * UPG:
                            pe.wait_ge(s_ones, us.n + 1)
                        pe.wait_ge(s_row[us.upar], (us.uhalf + 1) * DMA * SHIFT_ROWS)
                    if n % 2 == 0:
                        wait(pe, s_exp, us.n * CHUNKS + c - 1)
                    j, third = n // 3, n % 3
                    q, kk = qw[us.gpar][us.hq], kw[us.gpar][us.hq]
                    tiles = [x for x in SCORE_TILES if x[0] == third and in_group(us.gi, x[2])]
                    for _, col, kb, qb, m in tiles:
                        ins = pe.matmul(
                            score[c % 2][:, (n % 2) * GT + col * P:(n % 2) * GT + (col + m) * P],
                            kk[0:rows, j, (kb + 1) * P:(kb + 2) * P], q[0:rows, j, qb * P:(qb + m) * P],
                            start=True, stop=True)
                    if n % 2 == 1:
                        ins.then_inc(s_score, 1)

                def sum_block(o):
                    if not up:
                        return
                    kb = SUM_ORDER[o]
                    if o == 0:
                        pe.wait_ge(s_cut, up.n * 2 + 2)
                        wait(pe, s_sumout, up.n)
                        if up.hq == 0:
                            pe.wait_ge(s_v[up.gpar], (up.ghalf + 1) * DMA)
                    last = [x for x in SUM_ORDER if in_group(up.gi, x)][-1]
                    if in_group(up.gi, kb):
                        third, col, _, qb, m = [x for x in SCORE_TILES if x[2] == kb][0]
                        for j in range(NQ):
                            c0 = j * HEAD_COLS + third * GT + col * P
                            h = up.hq * NQ + j
                            ins = pe.matmul(sum_bank[32 * j:32 * j + VW, qb * P:(qb + m) * P],
                                            vw[:, up.gpar, kb + 1, h * VW:h * VW + VW],
                                            pe_w[:, up.upar, c0:c0 + m * P], start=(o == 0), stop=(kb == last),
                                            skip_group_check=True)
                        if kb == last:
                            ins.then_inc(s_sum, 1)

                for j in range(TILES):
                    max_tile(j)
                    for kind, n in AFTER_TILE[j]:
                        if kind == "score":
                            score_bank(n)
                        elif kind == "sum":
                            sum_block(n)
                        elif kind == "M":
                            maxima_turned()
                        else:
                            sums_turned()

            march(pe, body, L_OUT)

        @block.scalar
        def _(act):
            def body(at):
                if u := at(L_OUT):
                    act.wait_ge(s_sum, u.n + 1)
                    wait(act, s_s, u.n - 1)
                    act.activation(sums[:, u.upar, :], sum_bank[:], ACT.Copy).then_inc(s_sumout, 1)
                us, ud = at(L_SCORE), at(L_SHIFT)
                for c in range(CHUNKS):
                    if us:
                        act.wait_ge(s_score, us.n * CHUNKS + c + 1)
                        if c == 0:
                            wait(act, s_sum, us.n - 1)
                        act.activation(pe_w[:, us.upar, c * CHUNK:(c + 1) * CHUNK], score[c % 2][:], ACT.Exp
                                       ).then_inc(s_exp, 1)
                    if ud and c == 0:
                        act.wait_ge(s_d0, ud.n + 1)
                        wait(act, s_num, ud.n - 3)
                        act.activation(p0[:, ud.hq].rearrange("p h t -> p (h t)"), d0[:, ud.upar, :], ACT.Exp
                                       ).then_inc(s_p0, 1)
                    if ud and c == 1:
                        t_in = turn[TURN_OF_M % TURN_BANKS][0:TILES, 0:P]
                        wait(act, s_row[ud.upar], ud.uhalf * DMA * SHIFT_ROWS)
                        wait(act, s_shift, ud.n * 3)
                        act.wait_ge(s_m, ud.n + 1)
                        act.activation(shift[:, ud.upar, HIGH, :], t_in, ACT.Copy, scale=-1.0)
                        act.activation(neg[:], t_in, ACT.Copy, scale=-1.0).then_inc(s_m_read, 1)

            march(act, body, L_OUT)

        @block.vector
        def _(dve):
            dve.memset(score[0][:], 0.0).then_inc(s_init, 1)
            dve.memset(score[1][:], 0.0).then_inc(s_init, 1)
            dve.memset(sum_bank[:], 0.0).then_inc(s_init, 1)
            dve.memset(mx[:], 0.0).then_inc(s_init, 1)
            dve.wait_ge(s_init, 4)
            dve.wait_ge(s_pool, 5)
            tile_turn = Turn(dve, s_tile, "tile_turn", 1)

            def body(at):
                um, ux, uo = at(L_SHIFT), at(L_MAX), at(L_OUT)
                if (u := at(L_KEY0)) and u.gi == 0:
                    wait(dve, s_tile_read, (u.n - UPG) * TILES + TILES)
                    dve.wait_ge(s_load[0][u.hq], (u.ghalf + 1) * LOADS * DMA)
                    dve.tensor_copy(k0[0:SLOT_ROWS, u.hq * NQ:u.hq * NQ + NQ],
                                    kw[0][u.hq][0:SLOT_ROWS, :, P]).then_inc(s_k0, 1)
                for j in range(TILES):
                    if ux:
                        bank = turn[TURN_OF_TILE[j] % TURN_BANKS]
                        h, t = j // TB, j % TB
                        lo = P if ux.gi == 0 and t == 0 else 0
                        hi = 2 * P if ux.gi == GB - 1 and t == TB - 1 else 3 * P
                        first = 3 * P - (hi - lo)
                        if j == 0:
                            wait(dve, s_d0, ux.n)
                        tile_turn.wait(ux.n * TILES + j + 1)
                        dve.tensor_tensor_reduce(
                            out=masked[:, j, first:3 * P + 1], in0=bank[:, lo:hi + 1],
                            in1=band[:, lo:hi + 1], scale=1.0, scalar=NEG, op0=ALU.add, op1=ALU.max,
                            accum_out=mx[:, ux.hq, j:j + 1]).then_inc(s_tile_read, 1)
                    if um:
                        high, mid, low = (shift[:, um.upar, part, :] for part in (HIGH, MID, LOW))
                        if j == 3:
                            dve.wait_ge(s_m_read, um.n + 1)
                            dve.tensor_tensor(rest[:], neg[:], high, ALU.subtract).then_inc(s_shift, 1)
                        if j == 4:
                            dve.wait_ge(s_shift, um.n * 3 + 1)
                            dve.tensor_copy(mid, rest[:]).then_inc(s_shift, 1)
                        if j == 5:
                            dve.wait_ge(s_shift, um.n * 3 + 2)
                            dve.tensor_tensor(low, rest[:], mid, ALU.subtract).then_inc(s_shift, 1)
                    if j == 6 and uo:
                        turned = turn[TURN_OF_S % TURN_BANKS][:].rearrange("p (t h e) -> p t h e", t=TB, h=NQ)
                        dve.wait_ge(s_s, uo.n + 1)
                        dve.wait_ge(s_t0, uo.n + 1)
                        wait(dve, s_o, uo.n - 1)
                        dve.tensor_tensor(den[:, uo.upar], turned[:, :, :, HD],
                                          p0[:, uo.hq].rearrange("p h t -> p t h"), ALU.add).then_inc(s_den, 1)
                        dve.tensor_tensor(num[:, uo.upar], turned[:, :, :, 0:HD], t0[:, uo.hq], ALU.add
                                          ).then_inc(s_s_read, 1)
                        dve.wait_ge(s_den, uo.n + 1)
                        dve.reciprocal(rden[:, uo.upar], den[:, uo.upar]).then_inc(s_num, 1)
                if ux:
                    dve.wait_ge(s_tile_read, ux.n * TILES + TILES)
                    wait(dve, s_p0, ux.n - 1)
                    dve.tensor_tensor(d0[:, ux.upar, :], masked[:, :, 3 * P], mx[:, ux.hq, 0:TILES], ALU.subtract
                                      ).then_inc(s_d0, 1)

            march(dve, body, L_OUT)


def block_mask(pool, tile, groups, size, base, sem):
    start = sem[1]
    pool.memset(tile, 1.0).then_inc(sem[0], 1)
    pool.wait_ge(sem[0], start + 1)
    pool.affine_select(out=tile, in_=tile, compare_op=ALU.is_ge, fill=0.0, base=base,
                       pattern=[[-size, groups]], channel_multiplier=1).then_inc(sem[0], 1)
    pool.wait_ge(sem[0], start + 2)
    pool.affine_select(out=tile, in_=tile, compare_op=ALU.is_ge, fill=0.0, base=size - 1 - base,
                       pattern=[[size, groups]], channel_multiplier=-1).then_inc(sem[0], 1)
    sem[1] = start + 3


def stage_row_zero(nc, qk_dram, kf_dram, va_dram, o_dram):
    CH = T // GT
    NB = T // P
    QR = 32
    RUN = 32
    with ExitStack() as ctx:
        def sb(name, shape, dt=F32):
            return ctx.enter_context(nc.sbuf_tensor(f"z_{name}", shape, dt))

        def sem(name):
            return ctx.enter_context(nc.semaphore(f"z_{name}"))

        qp_run = sb("q_parts", [P, KT, B, 3, RUN], BF16)
        qp = [qp_run[:, :, :, place, 0] for place in range(3)]
        q0 = sb("q", [P, KT, B])
        head_of = sb("head_of", [P, KT, H])
        qd = sb("q_diag", [P, KT, B, QR])
        kf = sb("k", [P, B, KT, T])
        va = sb("v", [P, B, NB, VROW])
        ident = sb("ident", [P, P])
        own = sb("own", [P, H, VW])
        seq_of = sb("seq_of", [P, B])
        nmax = sb("nmax", [P, 1])
        den = sb("den", [P, 1])
        rden = sb("rden", [P, 1])
        w = sb("w", [P, T])
        wt = sb("wt", [P, NB, P])
        picked = sb("picked", [P, H, VW])
        row = sb("row", [B, H, HD])
        scores = ctx.enter_context(nc.psum_tensor("z_scores", [P, T], F32))
        turned = ctx.enter_context(nc.psum_tensor("z_turned", [P, 2, GT], F32))
        sums = ctx.enter_context(nc.psum_tensor("z_sums", [P, GT], F32))
        total = ctx.enter_context(nc.psum_tensor("z_total", [P, GT], F32))
        s_q, s_k, s_v, s_pool = sem("q"), sem("k"), sem("v"), sem("pool")
        s_qd, s_sc, s_max, s_exp = sem("qd"), sem("sc"), sem("max"), sem("exp")
        s_turn, s_wt, s_sum, s_pick, s_tot, s_row, s_out = (
            sem("turn"), sem("wt"), sem("sum"), sem("pick"), sem("tot"), sem("row"), sem("out"))
        block = ctx.enter_context(nc.Block())

        @block.sync
        def _(sp):
            for k in range(KT):
                for b in range(B):
                    sp.dma_start(qp_run[:, k, b], qk_dram[0, k * P:(k + 1) * P, :, b * T:b * T + RUN]
                                 ).then_inc(s_q, DMA)
            for b in range(B):
                sp.dma_start(kf[:, b], kf_dram[:, b * T:(b + 1) * T].rearrange("(k p) t -> p k t", p=P)
                             ).then_inc(s_k, DMA)
            for b in range(B):
                sp.dma_start(va[:, b], va_dram[b * T:(b + 1) * T, :].rearrange("(n p) e -> p n e", p=P)
                             ).then_inc(s_v, DMA)
            sp.wait_ge(s_row, 1)
            sp.dma_start(o_dram[0:N:T, :], row[:].rearrange("b h e -> b (h e)")).then_inc(s_out, DMA)
            sp.wait_ge(s_out, DMA)

        @block.gpsimd
        def _(pool):
            count = [s_pool, 0]
            for k in range(KT):
                block_mask(pool, head_of[:, k, :], H, HD, k * P, count)
            block_mask(pool, seq_of[:], B, QR, 0, count)
            pool.memset(own[:], 0.0).then_inc(s_pool, 1)
            pool.wait_ge(s_pool, count[1] + 1)
            for b in range(B):
                pool.affine_select(out=own[:], in_=own[:], compare_op=ALU.not_equal, fill=1.0, base=-QR * b,
                                   pattern=[[-1, H], [0, VW]], channel_multiplier=1).then_inc(s_pool, 1)
                pool.wait_ge(s_pool, count[1] + 2 + b)
            pool.memset(ident[:], 1.0).then_inc(s_pool, 1)
            pool.wait_ge(s_pool, count[1] + 6)
            pool.affine_select(out=ident[:], in_=ident[:], compare_op=ALU.is_equal, fill=0.0, base=0,
                               pattern=[[-1, P]], channel_multiplier=1).then_inc(s_pool, 1)
            assert count[1] + 7 == 3 * (KT + 1) + 7

        POOL_DONE = 3 * (KT + 1) + 7

        @block.vector
        def _(dve):
            dve.memset(qd[:], 0.0).then_inc(s_qd, 1)
            dve.wait_ge(s_q, KT * B * DMA)
            dve.wait_ge(s_pool, POOL_DONE)
            dve.tensor_tensor(q0[:], qp[0], qp[1], ALU.add).then_inc(s_qd, 1)
            dve.wait_ge(s_qd, 2)
            dve.tensor_tensor(q0[:], q0[:], qp[2], ALU.add).then_inc(s_qd, 1)
            dve.wait_ge(s_qd, 3)
            for k in range(KT):
                for b in range(B):
                    dve.tensor_scalar(qd[:, k, b, 0:H], head_of[:, k, :], q0[:, k, b:b + 1], None, ALU.mult
                                      ).then_inc(s_qd, 1)
            dve.wait_ge(s_sc, 1)
            dve.tensor_reduce(nmax[:], scores[:], AX.X, ALU.max, negate=True).then_inc(s_max, 1)
            dve.wait_ge(s_exp, 1)
            dve.reciprocal(rden[:], den[:]).then_inc(s_max, 1)
            for n in range(NB // TB):
                dve.wait_ge(s_turn, n + 1)
                dve.tensor_copy(wt[:, n * TB:(n + 1) * TB, :].rearrange("p a b -> p (a b)"), turned[:, n % 2, :]
                                ).then_inc(s_wt, 1)
            dve.wait_ge(s_sum, 1)
            dve.wait_ge(s_max, 2)
            dve.scalar_tensor_tensor(out=picked[:].rearrange("p h e -> p (h e)"), in0=sums[:, 0:VROW],
                                     scalar=rden[:, 0:1], in1=own[:].rearrange("p h e -> p (h e)"),
                                     op0=ALU.mult, op1=ALU.mult).then_inc(s_pick, 1)
            dve.wait_ge(s_tot, 1)
            dve.tensor_copy(row[:], total[0:B, 0:VROW].rearrange("b (h e) -> b h e", h=H)[:, :, 0:HD]
                            ).then_inc(s_row, 1)

        @block.scalar
        def _(act):
            act.wait_ge(s_max, 1)
            act.activation(w[:], scores[:], ACT.Exp, bias=nmax[:, 0:1], accum_out=den[:, 0:1]).then_inc(s_exp, 1)

        @block.tensor
        def _(pe):
            pe.wait_ge(s_qd, 3 + KT * B)
            pe.wait_ge(s_k, B * DMA)
            for c in range(CH):
                for k in range(KT):
                    for b in range(B):
                        ins = pe.matmul(scores[QR * b:QR * b + QR, c * GT:(c + 1) * GT], qd[:, k, b, :],
                                        kf[:, b, k, c * GT:(c + 1) * GT], start=(k == 0), stop=(k == KT - 1))
            ins.then_inc(s_sc, 1)
            pe.wait_ge(s_exp, 1)
            for n in range(NB // TB):
                wait(pe, s_wt, n - 1)
                for i in range(TB):
                    c = (n * TB + i) * P
                    ins = pe.transpose(turned[:, n % 2, i * P:(i + 1) * P], w[:, c:c + P], ident[:])
                ins.then_inc(s_turn, 1)
            pe.wait_ge(s_v, B * DMA)
            pe.wait_ge(s_wt, NB // TB)
            for n in range(NB):
                for b in range(B):
                    ins = pe.matmul(sums[QR * b:QR * b + QR, 0:VROW], wt[:, n, QR * b:QR * b + QR], va[:, b, n, :],
                                    start=(n == 0), stop=(n == NB - 1))
            ins.then_inc(s_sum, 1)
            pe.wait_ge(s_pick, 1)
            pe.matmul(total[0:B, 0:VROW], seq_of[:], picked[:].rearrange("p h e -> p (h e)"),
                      start=True, stop=True).then_inc(s_tot, 1)


def stage_feed(nc, x, o_dram, wo, fast_b, w_fc, w_proj, u, v, gate, out):
    MH = HID // P
    with ExitStack() as ctx:
        def sb(name, shape, dt=F32):
            return ctx.enter_context(nc.sbuf_tensor(f"f_{name}", shape, dt))

        def sem(name):
            return ctx.enter_context(nc.semaphore(f"f_{name}"))

        ident = sb("ident", [P, P])
        wo_in = sb("wo_in", [P, KT, D])
        wo_hi, wo_lo = sb("wo_hi", [P, KT, D], F32R), sb("wo_lo", [P, KT, D], F32R)
        w1_in = sb("w1_in", [P, MH, D])
        w1_low = sb("w1_low", [P, MH, D])
        w1_hi, w1_lo = sb("w1_hi", [P, KT, HID], F32R), sb("w1_lo", [P, KT, HID], F32R)
        w2_in = sb("w2_in", [P, KT, HID])
        w2_tern = sb("w2_tern", [P, KT, HID])
        w2_t = sb("w2_t", [P, MH, D], F32R)
        mag1, half1, nhalf1 = sb("mag1", [P, MH]), sb("half1", [P, MH]), sb("nhalf1", [P, MH])
        mag2, half2, nhalf2 = sb("mag2", [P, KT]), sb("half2", [P, KT]), sb("nhalf2", [P, KT])
        u_in, u_t = sb("u_in", [P, MH, RANK]), sb("u_t", [P, P])
        u_m = sb("u_m", [P, MH, P])
        tile_of = sb("tile_of", [P, MH])
        fb_t = sb("fb_t", [RANK, RANK])
        fb_rep = sb("fb_rep", [RANK, MH, RANK])
        v_in = sb("v_in", [RANK, D])
        gate_c = sb("gate", [P, 1])
        low_v = sb("low_v", [P, D])
        ob = sb("o", [P, 2, TB, D])
        ot_hi, ot_lo = sb("o_t_hi", [P, KT, GT], F32R), sb("o_t_lo", [P, KT, GT], F32R)
        xb = sb("x", [P, 4, TB, D])
        xn = sb("xn", [P, TB, D])
        xt_hi, xt_lo = sb("xt_hi", [P, 2, KT, GT], F32R), sb("xt_lo", [P, 2, KT, GT], F32R)
        r = sb("relu", [P, 4, GT])
        r2 = sb("square", [P, 4, GT])
        r2_hi, r2_lo = sb("square_hi", [P, 4, GT], F32R), sb("square_lo", [P, 4, GT], F32R)
        yt = sb("y_t", [P, KT, GT])
        banks = [ctx.enter_context(nc.psum_tensor(f"f_bank{i}", [P, GT], F32)) for i in range(8)]
        t_bank, a_bank, h_bank, y_bank = banks[0:2], banks[2:4], banks[4:6], banks[6:8]
        norm = Norm(nc, ctx, "n2")

        s_in, s_pool = sem("weights_in"), sem("pool")
        s_prep, s_wolo, s_pt, s_pc = sem("prep"), sem("wo_lo"), sem("prep_turned"), sem("prep_copied")
        s_m1, s_low, s_w1, s_w1hi = sem("low_v"), sem("low"), sem("w1"), sem("w1_hi")
        s_scale, s_tern = sem("scale"), sem("ternary")
        s_o, s_x = [sem("o_in0"), sem("o_in1")], [sem(f"x_in{i}") for i in range(4)]
        s_ot, s_oth, s_otc, s_a, s_x1 = sem("o_turned"), sem("o_high"), sem("o_low"), sem("attn"), sem("x1")
        s_xt, s_hi, s_lo = sem("xn_turned"), sem("xt_hi"), sem("xt_lo")
        s_h, s_r, s_sq, s_r2hi, s_r2lo = sem("hidden"), sem("relu"), sem("square"), sem("square_hi"), sem("square_lo")
        s_y, s_yc, s_back, s_fin = sem("y"), sem("y_copied"), sem("y_back"), sem("final")
        s_out = [sem(f"out{i}") for i in range(4)]
        x_v = x.rearrange("b (g t p) d -> (b g) p t d", t=TB, p=P)
        out_v = out.rearrange("b (g t p) d -> (b g) p t d", t=TB, p=P)
        WEIGHTS = 7
        block = ctx.enter_context(nc.Block())
        LA, LX, LF, LB = 1, 2, 3, 4

        @block.sync
        def _(sp):
            for dst, src in (
                    (wo_in[:], wo.rearrange("(m p) k -> p m k", p=P)),
                    (w1_in[:], w_fc.rearrange("(m p) k -> p m k", p=P)),
                    (w2_in[:], w_proj.rearrange("(m p) k -> p m k", p=P)),
                    (u_in[:], u.rearrange("(m p) r -> p m r", p=P)),
                                        (v_in[:], v),
                    (gate_c[:], gate.rearrange("(a b) -> a b", a=1).to_broadcast((P, 1)))):
                sp.dma_start(dst, src).then_inc(s_in, DMA)
            with nc.allow_non_contiguous_dma(reason="16 by 16, turned"):
                sp.dma_start(fb_t[:], fast_b.rearrange("a b -> b a")).then_inc(s_in, DMA)

            def body(at):
                if q := at(LB):
                    sp.wait_ge(s_fin, q.g * KT + KT)
                    sp.dma_start(out_v[bass.ds(q.g, 1)].rearrange("a p t d -> (a p) t d"), xb[:, q.ring]
                                 ).then_inc(s_out[q.ring], DMA)
                if q := at(0):
                    wait(sp, s_ot, (q.g - 2) * KT + KT)
                    sp.dma_start(ob[:, q.par], o_dram[bass.ds(q.g * GT, GT), :]
                                 .rearrange("(t p) d -> p t d", p=P)).then_inc(s_o[q.par], DMA)
                    wait(sp, s_out[q.ring], q.turn * DMA)
                    sp.dma_start(xb[:, q.ring], x_v[bass.ds(q.g, 1)].rearrange("a p t d -> (a p) t d")
                                 ).then_inc(s_x[q.ring], DMA)

            sweep(sp, body, LB)
            for i in range(4):
                sp.wait_ge(s_out[i], DMA * (G // 4))

        @block.gpsimd
        def _(pool):
            identity(pool, ident[:], s_pool)
            block_mask(pool, tile_of[:], MH, RANK, 0, [s_pool, 2])

            def body(at):
                if q := at(LF):
                    for j in range(MH):
                        pool.wait_ge(s_r, q.g * MH + j + 1)
                        wait(pool, s_r2lo, q.g * MH + j + 1 - 4)
                        pool.tensor_tensor(r2[:, j % 4, :], r[:, j % 4, :], r[:, j % 4, :], ALU.mult
                                           ).then_inc(s_sq, 1)

            sweep(pool, body, LB)

        @block.tensor
        def _(pe):
            pe.wait_ge(s_pool, 5)
            pe.wait_ge(s_in, WEIGHTS * DMA)
            for k in range(KT):
                for m in range(KT):
                    ins = pe.transpose(banks[0][:, k * D + m * P:k * D + m * P + P], wo_in[:, m, k * P:k * P + P],
                                       ident[:])
            ins.then_inc(s_pt, 1)
            pe.transpose(banks[1][:, 0:P], u_in[:].rearrange("p m r -> p (m r)"), ident[:]).then_inc(s_pt, 1)
            pe.wait_ge(s_prep, 1)
            pe.matmul(banks[2][:, 0:D], fb_rep[:].rearrange("a m b -> a (m b)"), v_in[:],
                      start=True, stop=True).then_inc(s_m1, 1)
            pe.wait_ge(s_m1, 2)
            pe.wait_ge(s_pc, 2 + MH)
            for m in range(MH):
                if m % 2 == 0:
                    wait(pe, s_w1, m - 2)
                ins = pe.matmul(banks[4 + m // 2 % 2][:, m % 2 * D:(m % 2 + 1) * D], u_m[:, m, :], low_v[:],
                                start=True, stop=True)
                if m % 2 == 1:
                    ins.then_inc(s_low, 1)
            pe.wait_ge(s_w1, MH)
            pe.wait_ge(s_wolo, 1)
            for n in range(4):
                k, c = n // 2, n % 2 * GT
                for m in range(TB):
                    ins = pe.transpose(banks[n % 2][:, m * P:m * P + P], w1_low[:, n % 2 * TB + m, k * P:k * P + P],
                                       ident[:])
                ins.then_inc(s_pt, 1)
                pe.wait_ge(s_pc, 2 + MH + n + 1)
            pe.wait_ge(s_tern, 2 * (MH + KT))
            for n in range(4):
                for i in range(2):
                    for m in range(KT):
                        ins = pe.transpose(banks[n % 2][:, i * D + m * P:i * D + m * P + P],
                                           w2_tern[:, m, (2 * n + i) * P:(2 * n + i + 1) * P], ident[:])
                ins.then_inc(s_pt, 1)
                pe.wait_ge(s_pc, 2 + MH + 4 + n + 1)

            def body(at):
                qa, qx, qf, qb = at(LA), at(LX), at(LF), at(LB)

                def back():
                    if not qb:
                        return
                    pe.wait_ge(s_yc, qb.g * KT + KT)
                    for c in range(2):
                        if qf:
                            pe.wait_ge(s_lo, qf.g * KT + c + 1)
                        wait(pe, s_fin, qb.g * KT)
                        for t in range(2):
                            for m in range(KT):
                                ins = pe.transpose(t_bank[c][:, t * D + m * P:t * D + m * P + P],
                                                   yt[:, m, (2 * c + t) * P:(2 * c + t + 1) * P], ident[:])
                        ins.then_inc(s_back, 1)

                def turn_o():
                    if not qa:
                        return
                    pe.wait_ge(s_o[qa.par], (qa.half + 1) * DMA)
                    for k in range(KT):
                        if qb:
                            pe.wait_ge(s_fin, qb.g * KT + k + 1)
                        else:
                            wait(pe, s_lo, (qa.g - 2) * KT + k + 1)
                            wait(pe, s_otc, (qa.g - 1) * KT + k + 1)
                        for t in range(TB):
                            ins = pe.transpose(t_bank[k][:, t * P:t * P + P], ob[:, qa.par, t, k * P:k * P + P],
                                               ident[:])
                        ins.then_inc(s_ot, 1)

                def turn_norm():
                    if not qx:
                        return
                    pe.wait_ge(norm.s_back, norm.done(qx))
                    for k in range(KT):
                        if qa:
                            pe.wait_ge(s_otc, qa.g * KT + k + 1)
                        elif qb:
                            pe.wait_ge(s_fin, qb.g * KT + k + 1)
                        for t in range(TB):
                            ins = pe.transpose(t_bank[k][:, t * P:t * P + P], xn[:, t, k * P:k * P + P], ident[:])
                        ins.then_inc(s_xt, 1)

                def attention_product():
                    if not qa:
                        return
                    pe.wait_ge(s_otc, qa.g * KT + KT)
                    for c in range(2):
                        wait(pe, s_x1, (qa.g - 1) * 2 + c + 1)
                        for t in range(2):
                            cut = slice((2 * c + t) * P, (2 * c + t + 1) * P)
                            ins = three_pass(pe, a_bank[c][:, t * D:t * D + D],
                                             [ot_hi[:, k, cut] for k in range(KT)],
                                             [ot_lo[:, k, cut] for k in range(KT)],
                                             [wo_hi[:, k, :] for k in range(KT)], [wo_lo[:, k, :] for k in range(KT)])
                        ins.then_inc(s_a, 1)

                def hidden(j):
                    if not qf:
                        return
                    if j == 0:
                        pe.wait_ge(s_lo, qf.g * KT + KT)
                    wait(pe, s_r, qf.g * MH + j - 1)
                    three_pass(pe, h_bank[j % 2][:], [w1_hi[:, k, j * P:j * P + P] for k in range(KT)],
                               [w1_lo[:, k, j * P:j * P + P] for k in range(KT)],
                               [xt_hi[:, qf.par, k, :] for k in range(KT)],
                               [xt_lo[:, qf.par, k, :] for k in range(KT)]).then_inc(s_h, 1)

                def output(j):
                    if not qf:
                        return
                    pe.wait_ge(s_r2lo, qf.g * MH + j + 1)
                    for m in range(KT):
                        if j == 0:
                            wait(pe, s_yc, (qf.g - 1) * KT + m + 1)
                        wt = w2_t[:, j, m * P:m * P + P]
                        pe.matmul(y_bank[m][:], wt, r2_hi[:, j % 4, :], start=(j == 0), stop=False)
                        ins = pe.matmul(y_bank[m][:], wt, r2_lo[:, j % 4, :], start=False, stop=(j == MH - 1))
                    ins.then_inc(s_y, 1)

                hidden(0)
                hidden(1)
                back()
                hidden(2)
                turn_o()
                for j in range(2, MH):
                    if j > 2:
                        hidden(j)
                    output(j - 2)
                turn_norm()
                output(MH - 2)
                attention_product()
                output(MH - 1)

            sweep(pe, body, LB)

        @block.scalar
        def _(act):
            act.wait_ge(s_pt, 1)
            act.activation(wo_hi[:].rearrange("p k n -> p (k n)"), banks[0][:], ACT.Copy).then_inc(s_pc, 1)
            act.wait_ge(s_pt, 2)
            act.activation(u_t[:], banks[1][:, 0:P], ACT.Copy).then_inc(s_pc, 1)
            act.wait_ge(s_pc, 2)
            for m in range(MH):
                act.activation(u_m[:, m, :], u_t[:], ACT.Copy, scale=tile_of[:, m:m + 1]).then_inc(s_pc, 1)
            for n in range(4):
                act.wait_ge(s_pt, 2 + n + 1)
                k, c = n // 2, n % 2 * GT
                act.activation(w1_hi[:, k, c:c + GT], banks[n % 2][:], ACT.Copy).then_inc(s_w1hi, 1)
            for n in range(4):
                act.wait_ge(s_pt, 6 + n + 1)
                act.activation(w2_t[:, 2 * n:2 * n + 2, :].rearrange("p a b -> p (a b)"), banks[n % 2][:], ACT.Copy
                               ).then_inc(s_pc, 1)

            def squares(q, j):
                wait(act, s_y, q.g * MH + j + 1 - 4)
                act.activation(r[:, j % 4, :], h_bank[j % 2][:], ACT.Relu).then_inc(s_r, 1)
                act.wait_ge(s_r, q.g * MH + j + 1)
                act.activation(r2_hi[:, j % 4, :], r[:, j % 4, :], ACT.Square).then_inc(s_r2hi, 1)

            def body(at):
                qa, qx, qf, qb = at(LA), at(LX), at(LF), at(LB)
                for j in range(MH):
                    if qf:
                        act.wait_ge(s_h, qf.g * MH + j + 1)
                        wait(act, s_sq, qf.g * MH + j + 1 - 4)
                        squares(qf, j)
                    if j == 1 and qa:
                        for k in range(KT):
                            act.wait_ge(s_ot, qa.g * KT + k + 1)
                            wait(act, s_a, (qa.g - 1) * 2 + 2)
                            act.activation(ot_hi[:, k, :], t_bank[k][:], ACT.Copy).then_inc(s_oth, 1)
                    if j == 3 and qx:
                        norm.root(act, qx)
                if qx:
                    for k in range(KT):
                        act.wait_ge(s_xt, qx.g * KT + k + 1)
                        wait(act, s_h, (qx.g - 2) * MH + MH)
                        act.activation(xt_hi[:, qx.par, k, :], t_bank[k][:], ACT.Copy).then_inc(s_hi, 1)
                if qf:
                    act.wait_ge(s_y, qf.g * MH + MH)
                    wait(act, s_back, (qf.g - 1) * KT + KT)
                    for m in range(KT):
                        act.activation(yt[:, m, :], y_bank[m][:], ACT.Copy, scale=mag2[:, m:m + 1]).then_inc(s_yc, 1)

            sweep(act, body, LB)

        @block.vector
        def _(dve):
            norm.begin(dve)
            dve.wait_ge(s_in, WEIGHTS * DMA)
            dve.tensor_copy(fb_rep[:], fb_t[:].unsqueeze(1).broadcast_to([RANK, MH, RANK])).then_inc(s_prep, 1)
            steps = 0
            for w, mag, half, nhalf, width in ((w1_in, mag1, half1, nhalf1, D), (w2_in, mag2, half2, nhalf2, HID)):
                dve.tensor_reduce(mag[:], w[:], AX.X, ALU.add, apply_absolute_value=True).then_inc(s_scale, 1)
                dve.wait_ge(s_scale, steps + 1)
                dve.tensor_scalar(mag[:], mag[:], 1.0 / width, 1e-5, ALU.mult, ALU.max).then_inc(s_scale, 1)
                dve.wait_ge(s_scale, steps + 2)
                dve.tensor_scalar(half[:], mag[:], 0.5, None, ALU.mult)
                dve.tensor_scalar(nhalf[:], mag[:], -0.5, None, ALU.mult).then_inc(s_scale, 1)
                dve.wait_ge(s_scale, steps + 3)
                steps += 3
            for w, tern, half, nhalf, n in ((w1_in, w1_low, half1, nhalf1, MH), (w2_in, w2_tern, half2, nhalf2, KT)):
                for m in range(n):
                    dve.tensor_scalar(tern[:, m, :], w[:, m, :], nhalf[:, m:m + 1], None, ALU.is_lt).then_inc(s_tern, 1)
            dve.wait_ge(s_tern, MH + KT)
            for w, tern, half, nhalf, n in ((w1_in, w1_low, half1, nhalf1, MH), (w2_in, w2_tern, half2, nhalf2, KT)):
                for m in range(n):
                    ins = dve.scalar_tensor_tensor(out=tern[:, m, :], in0=w[:, m, :], scalar=half[:, m:m + 1],
                                                   in1=tern[:, m, :], op0=ALU.is_gt, op1=ALU.subtract)
                    ins.then_inc(s_tern, 1)
            dve.wait_ge(s_pc, 1)
            dve.tensor_tensor(wo_lo[:].rearrange("p k n -> p (k n)"), banks[0][:],
                              wo_hi[:].bitcast(F32).rearrange("p k n -> p (k n)"), ALU.subtract).then_inc(s_wolo, 1)
            dve.wait_ge(s_m1, 1)
            dve.tensor_scalar(low_v[:], banks[2][:, 0:D], gate_c[:, 0:1], None, ALU.mult).then_inc(s_m1, 1)
            dve.wait_ge(s_tern, 2 * (MH + KT))
            for m in range(MH):
                if m % 2 == 0:
                    dve.wait_ge(s_low, m // 2 + 1)
                dve.scalar_tensor_tensor(out=w1_low[:, m, :], in0=w1_low[:, m, :], scalar=mag1[:, m:m + 1],
                                         in1=banks[4 + m // 2 % 2][:, m % 2 * D:(m % 2 + 1) * D],
                                         op0=ALU.mult, op1=ALU.add).then_inc(s_w1, 1)
            for n in range(4):
                k, c = n // 2, n % 2 * GT
                dve.wait_ge(s_w1hi, n + 1)
                dve.tensor_tensor(w1_lo[:, k, c:c + GT], banks[n % 2][:], w1_hi[:, k, c:c + GT].bitcast(F32),
                                  ALU.subtract).then_inc(s_pc, 1)

            def low_of_squares(q, j):
                dve.wait_ge(s_r2hi, q.g * MH + j + 1)
                dve.wait_ge(s_sq, q.g * MH + j + 1)
                dve.tensor_tensor(r2_lo[:, j % 4, :], r2[:, j % 4, :], r2_hi[:, j % 4, :].bitcast(F32), ALU.subtract
                                  ).then_inc(s_r2lo, 1)

            def body(at):
                qa, qx, qf, qb = at(LA), at(LX), at(LF), at(LB)
                for j in range(MH):
                    if qf:
                        low_of_squares(qf, j)
                    if j == 0 and qb:
                        for c in range(2):
                            dve.wait_ge(s_back, qb.g * KT + c + 1)
                            rows = xb[:, qb.ring, 2 * c:2 * c + 2, :].rearrange("p t d -> p (t d)")
                            dve.tensor_tensor(rows, t_bank[c][:], rows, ALU.add).then_inc(s_fin, 1)
                    if j == 0 and qa:
                        for k in range(KT):
                            dve.wait_ge(s_oth, qa.g * KT + k + 1)
                            dve.tensor_tensor(ot_lo[:, k, :], t_bank[k][:], ot_hi[:, k, :].bitcast(F32),
                                              ALU.subtract).then_inc(s_otc, 1)
                    if j == 1 and qx:
                        dve.wait_ge(s_x1, qx.g * 2 + 2)
                        norm.front(dve, xb[:, qx.ring], qx)
                    if j == 3 and qx:
                        wait(dve, s_xt, (qx.g - 1) * KT + KT)
                        norm.back(dve, xb[:, qx.ring], xn[:], qx)
                if qx:
                    for k in range(KT):
                        dve.wait_ge(s_hi, qx.g * KT + k + 1)
                        dve.tensor_tensor(xt_lo[:, qx.par, k, :], t_bank[k][:],
                                          xt_hi[:, qx.par, k, :].bitcast(F32), ALU.subtract).then_inc(s_lo, 1)
                if qa:
                    dve.wait_ge(s_x[qa.ring], (qa.turn + 1) * DMA)
                    for c in range(2):
                        dve.wait_ge(s_a, qa.g * 2 + c + 1)
                        rows = xb[:, qa.ring, 2 * c:2 * c + 2, :].rearrange("p t d -> p (t d)")
                        dve.tensor_tensor(rows, a_bank[c][:], rows, ALU.add).then_inc(s_x1, 1)

            sweep(dve, body, LB)


def layer(nc, x, wq, wk, wv, wo, fast_b, w_fc, w_proj, u, v, gate, out):
    qk_dram = nc.dram_tensor("qk_parts", [2, D, 3, N], BF16, kind="Internal").ap()
    kf_dram = nc.dram_tensor("k_whole", [D, N], F32, kind="Internal").ap()
    va_dram = nc.dram_tensor("v_ones", [N, VROW], F32, kind="Internal").ap()
    o_dram = nc.dram_tensor("attention", [N, D], F32, kind="Internal").ap()
    stage_project(nc, x, (wq, wk, wv), qk_dram, kf_dram, va_dram)
    stage_attend(nc, qk_dram, va_dram, o_dram)
    stage_row_zero(nc, qk_dram, kf_dram, va_dram, o_dram)
    stage_feed(nc, x, o_dram, wo, fast_b, w_fc, w_proj, u, v, gate, out)


_INS = ["x", "Wq", "Wk", "Wv", "Wo", "fast_b", "w_fc", "w_proj", "u", "v", "gate"]


def kernel(**inputs):
    import concourse.bacc as bacc
    from concourse.bass_utils import run_bass_kernel_spmd

    nc = bacc.Bacc("TRN2", target_bir_lowering=False, num_devices=1)
    arrays, args = {}, []
    for name in _INS:
        key = ("L0_attn_" if name[0] == "W" or name == "x" else "L0_ffn_") + name
        a = np.ascontiguousarray(inputs[key])
        if a.ndim == 0:
            a = a.reshape(1)
        arrays[f"in_{name}"] = a
        args.append(nc.dram_tensor(f"in_{name}", a.shape, mybir.dt.from_np(a.dtype), kind="ExternalInput").ap())
    out = nc.dram_tensor("out", (B, T, D), F32, kind="ExternalOutput").ap()
    layer(nc, *args, out)
    r = run_bass_kernel_spmd(nc, [arrays], core_ids=[0])
    return r.results[0]["out"]
```

```python
from contextlib import ExitStack

import numpy as np

import concourse.bass as bass
from concourse import mybir

ACT = mybir.ActivationFunctionType
ALU = mybir.AluOpType
AX = mybir.AxisListType
F32 = mybir.dt.float32
F32R = mybir.dt.float32r
BF16 = mybir.dt.bfloat16

P = 128
B, T, D = 4, 2048, 256
H, HD = 16, 16
HID = 1024
RANK = 16
MH = HID // P
N = B * T
KT = D // P
GT = 512
TB = GT // P
G = N // GT
GB = T // GT
VW = HD + 1
VROW = H * VW
EPS = 1e-5
QSCALE = 1.0 / float(np.sqrt(HD))
NEG = -3.0e38
ROUND = 4
DMA = 16
HIGH, MID, LOW = 0, 1, 2
PLACE = ({LOW: 0, MID: 1, HIGH: 2}, {HIGH: 0, MID: 1, LOW: 2})
SLOTS = 6
SINGLES = ((MID, HIGH, HIGH), (HIGH, MID, HIGH))
SLOT_ROWS = SLOTS * HD
SHIFT_ROWS = 3
NQ = 4
UPG = H // NQ
UNITS = G * UPG
UPB = GB * UPG
P0_BUFS = 2 * UPG
WIN = GT + 2 * P


class Group:

    def __init__(self, i, k):
        self.g = i * ROUND + k
        self.par, self.half = k % 2, i * (ROUND // 2) + k // 2
        self.ring, self.turn = k % 4, i * (ROUND // 4) + k // 4


def wait(eng, sem, value):
    if isinstance(value, int) and value <= 0:
        return
    eng.wait_ge(sem, value)


class Turn:

    def __init__(self, eng, sem, name, start, step=1):
        self.eng, self.sem, self.step = eng, sem, step
        self.value = eng.alloc_register(name)
        self.looped = False
        eng.reg_mov(self.value, start)

    def wait(self, value):
        self.looped = self.looped or not isinstance(value, int)
        if self.looped and isinstance(value, int):
            self.eng.wait_ge(self.sem, value)
        else:
            self.eng.wait_ge(self.sem, self.value)
            self.eng.reg_add(self.value, self.value, self.step)


def sweep(eng, body, lags):
    def fixed(it):
        return lambda lag: Group(0, it - lag) if 0 <= it - lag < G else None

    first = -(-lags // ROUND)
    for it in range(first * ROUND):
        body(fixed(it))
    with eng.Fori(first, G // ROUND) as i:
        for p in range(ROUND):
            body(lambda lag, p=p: Group(i, p - lag))
    for it in range(G, G + lags):
        body(fixed(it))


def identity(pool, tile, sem):
    pool.memset(tile, 1.0).then_inc(sem, 1)
    pool.wait_ge(sem, 1)
    pool.affine_select(out=tile, in_=tile, compare_op=ALU.is_equal, fill=0.0, base=0,
                       pattern=[[-1, P]], channel_multiplier=1).then_inc(sem, 1)


class Norm:

    def __init__(self, nc, ctx, name):
        def sb(n, shape):
            return ctx.enter_context(nc.sbuf_tensor(f"{name}_{n}", shape, F32))
        self.name = name
        self.stats = sb("stats", [P, TB, 6])
        self.mv = sb("meanvar", [P, 2, TB, 2])
        self.ve = sb("var_eps", [P, 2, TB])
        self.sd = sb("stddev", [P, 2, TB])
        self.r0 = sb("rstd_first", [P, TB])
        self.t0 = sb("newton", [P, TB])
        self.rs = sb("rstd", [P, TB])
        self.s_step = ctx.enter_context(nc.semaphore(f"{name}_step"))
        self.s_sd = ctx.enter_context(nc.semaphore(f"{name}_sd"))
        self.s_back = ctx.enter_context(nc.semaphore(f"{name}_back"))

    def begin(self, v):
        self.stats_turn = Turn(v, self.s_step, f"{self.name}_stats_turn", 1, 3)

    def front(self, v, x, q):
        par, base = q.par, q.g * 3
        for t in range(TB):
            ins = v.bn_stats(self.stats[:, t, :], x[:, t, :])
        ins.then_inc(self.s_step, 1)
        self.stats_turn.wait(base + 1)
        for t in range(TB):
            ins = v.bn_aggr(self.mv[:, par, t, :], self.stats[:, t, :])
        ins.then_inc(self.s_step, 1)
        v.wait_ge(self.s_step, base + 2)
        v.tensor_scalar(self.ve[:, par, :], self.mv[:, par, :, 1], EPS, None, ALU.add).then_inc(self.s_step, 1)

    def root(self, a, q):
        a.wait_ge(self.s_step, q.g * 3 + 3)
        a.activation(self.sd[:, q.par, :], self.ve[:, q.par, :], ACT.Sqrt).then_inc(self.s_sd, 1)

    def back(self, v, x, xn, q):
        par, base = q.par, q.g * 6
        v.wait_ge(self.s_sd, q.g + 1)
        v.reciprocal(self.r0[:], self.sd[:, par, :]).then_inc(self.s_back, 1)
        v.wait_ge(self.s_back, base + 1)
        v.tensor_tensor(self.t0[:], self.ve[:, par, :], self.r0[:], ALU.mult).then_inc(self.s_back, 1)
        v.wait_ge(self.s_back, base + 2)
        v.tensor_tensor(self.t0[:], self.t0[:], self.r0[:], ALU.mult).then_inc(self.s_back, 1)
        v.wait_ge(self.s_back, base + 3)
        v.tensor_scalar(self.t0[:], self.t0[:], -0.5, 1.5, ALU.mult, ALU.add).then_inc(self.s_back, 1)
        v.wait_ge(self.s_back, base + 4)
        v.tensor_tensor(self.rs[:], self.t0[:], self.r0[:], ALU.mult).then_inc(self.s_back, 1)
        v.wait_ge(self.s_back, base + 5)
        for t in range(TB):
            ins = v.tensor_scalar(xn[:, t, :], x[:, t, :], self.mv[:, par, t, 0:1], self.rs[:, t:t + 1],
                                  ALU.subtract, ALU.mult)
        ins.then_inc(self.s_back, 1)

    def done(self, q):
        return q.g * 6 + 6


def three_pass(pe, out, lhs_hi, lhs_lo, rhs_hi, rhs_lo):
    n = len(lhs_hi)
    for k in range(n):
        pe.matmul(out, lhs_hi[k], rhs_hi[k], start=(k == 0), stop=False)
        pe.matmul(out, lhs_hi[k], rhs_lo[k], start=False, stop=False)
        ins = pe.matmul(out, lhs_lo[k], rhs_hi[k], start=False, stop=(k == n - 1))
    return ins


def stage_project(nc, x, weights, qk_dram, kf_dram, va_dram):
    with ExitStack() as ctx:
        def sb(name, shape, dt=F32):
            return ctx.enter_context(nc.sbuf_tensor(f"p_{name}", shape, dt))

        def sem(name):
            return ctx.enter_context(nc.semaphore(f"p_{name}"))

        ident = sb("ident", [P, P])
        w_in = sb("w_in", [P, 3, KT, D])
        wt_hi = sb("wt_hi", [P, 3, KT, D], F32R)
        wt_lo = sb("wt_lo", [P, 3, KT, D], F32R)
        xb = sb("x", [P, 4, TB, D])
        xn = sb("xn", [P, 2, TB, D])
        xt_hi = sb("xt_hi", [P, 2, KT, GT], F32R)
        xt_lo = sb("xt_lo", [P, 2, KT, GT], F32R)
        parts = sb("parts", [P, 2, 2 * KT, 3, GT], BF16)
        rest = sb("rest", [P, 2 * KT, GT])
        kf = sb("kf", [P, 2, KT, GT])
        va = sb("va", [P, 2, TB, H, VW])
        banks = [ctx.enter_context(nc.psum_tensor(f"p_bank{i}", [P, GT], F32)) for i in range(8)]
        t_bank, qk_bank, v_bank = banks[0:2], banks[2:6], banks[6:8]
        norm = Norm(nc, ctx, "n1")

        s_w, s_id, s_ones = sem("weights_in"), sem("ident"), sem("ones")
        s_wt, s_whi, s_wlo = sem("w_turned"), sem("w_hi"), sem("w_lo")
        s_x = [sem(f"x_in{i}") for i in range(4)]
        s_t, s_hi, s_lo = sem("turned"), sem("xt_hi"), sem("xt_lo")
        s_qk, s_v = sem("qk"), sem("v")
        s_high, s_rest, s_mid, s_low, s_vout = (
            sem("high"), sem("rest"), sem("mid"), sem("low"), sem("v_out"))
        s_out = [sem("out0"), sem("out1")]
        STORES = 2 * KT + 2

        x_v = x.rearrange("b (g t p) d -> (b g) p t d", t=TB, p=P)
        LN, LT, LP = 1, 2, 3
        block = ctx.enter_context(nc.Block())

        @block.sync
        def _(sp):
            for w in range(3):
                sp.dma_start(w_in[:, w], weights[w].rearrange("(m p) k -> p m k", p=P)).then_inc(s_w, DMA)

            def body(at):
                if q := at(0):
                    wait(sp, norm.s_back, (q.g - 4) * 6 + 6)
                    sp.dma_start(xb[:, q.ring], x_v[bass.ds(q.g, 1)].rearrange("a p t d -> (a p) t d")
                                 ).then_inc(s_x[q.ring], DMA)
                if q := at(LP):
                    cols = bass.ds(q.g * GT, GT)
                    for u in range(2 * KT):
                        k = u % KT * P
                        sp.wait_ge(s_low, q.g * 4 + u + 1)
                        sp.dma_start(qk_dram[u // KT, k:k + P, :, cols], parts[:, q.par, u]
                                     ).then_inc(s_out[q.par], DMA)
                    sp.dma_start(kf_dram[:, cols].rearrange("(m p) t -> p m t", p=P),
                                 kf[:, q.par]).then_inc(s_out[q.par], DMA)
                    sp.wait_ge(s_vout, q.g * 2 + 2)
                    sp.dma_start(va_dram[cols, :].rearrange("(t p) n -> p t n", p=P),
                                 va[:, q.par].rearrange("p t h e -> p t (h e)")).then_inc(s_out[q.par], DMA)

            sweep(sp, body, LP)
            for par in range(2):
                sp.wait_ge(s_out[par], DMA * STORES * (G // 2))

        @block.gpsimd
        def _(pool):
            pool.memset(va[:, :, :, :, HD:VW], 1.0).then_inc(s_ones, 1)
            identity(pool, ident[:], s_id)

            def body(at):
                if q := at(LP):
                    for u in range(2 * KT):
                        pool.wait_ge(s_mid, q.g * 4 + u + 1)
                        pool.tensor_tensor(parts[:, q.par, u, PLACE[u // KT][LOW], :], rest[:, u, :],
                                           parts[:, q.par, u, PLACE[u // KT][MID], :], ALU.subtract).then_inc(s_low, 1)

            sweep(pool, body, LP)

        @block.tensor
        def _(pe):
            pe.wait_ge(s_id, 2)
            for w in range(3):
                pe.wait_ge(s_w, 3 * DMA)
                for k in range(KT):
                    for m in range(KT):
                        ins = pe.transpose(banks[w][:, k * D + m * P:k * D + m * P + P],
                                           w_in[:, w, m, k * P:k * P + P], ident[:])
                ins.then_inc(s_wt, 1)
            pe.wait_ge(s_wlo, 3)

            def body(at):
                def turn():
                    if q := at(LT):
                        pe.wait_ge(norm.s_back, norm.done(q))
                        for k in range(KT):
                            wait(pe, s_lo, (q.g - 1) * KT + k + 1)
                            for t in range(TB):
                                ins = pe.transpose(t_bank[k][:, t * P:t * P + P],
                                                   xn[:, q.par, t, k * P:k * P + P], ident[:])
                            ins.then_inc(s_t, 1)

                q = at(LP)
                if q:
                    pe.wait_ge(s_lo, q.g * KT + KT)
                    xh = [xt_hi[:, q.par, k, :] for k in range(KT)]
                    xl = [xt_lo[:, q.par, k, :] for k in range(KT)]
                for u in range(2 * KT):
                    if u == KT + 1:
                        turn()
                    if q:
                        w, m = u // KT, (u % KT) * P
                        wait(pe, s_rest, (q.g - 1) * 4 + u + 1)
                        three_pass(pe, qk_bank[u][:], [wt_hi[:, w, k, m:m + P] for k in range(KT)],
                                   [wt_lo[:, w, k, m:m + P] for k in range(KT)], xh, xl).then_inc(s_qk, 1)
                if q:
                    for c in range(2):
                        wait(pe, s_vout, (q.g - 1) * 2 + c + 1)
                        for t in range(2):
                            cut = slice((2 * c + t) * P, (2 * c + t + 1) * P)
                            ins = three_pass(pe, v_bank[c][:, t * D:t * D + D], [a[:, cut] for a in xh],
                                             [a[:, cut] for a in xl], [wt_hi[:, 2, k, :] for k in range(KT)],
                                             [wt_lo[:, 2, k, :] for k in range(KT)])
                        ins.then_inc(s_v, 1)

            sweep(pe, body, LP)

        @block.scalar
        def _(act):
            for w in range(3):
                act.wait_ge(s_wt, w + 1)
                act.activation(wt_hi[:, w].rearrange("p k n -> p (k n)"), banks[w][:], ACT.Copy).then_inc(s_whi, 1)

            def mid(q, u):
                act.wait_ge(s_rest, q.g * 4 + u + 1)
                act.activation(parts[:, q.par, u, PLACE[u // KT][MID], :], rest[:, u, :], ACT.Copy).then_inc(s_mid, 1)

            def body(at):
                q = at(LP)
                if q:
                    wait(act, s_out[q.par], q.half * DMA * STORES)
                for u in range(2 * KT):
                    if q:
                        act.wait_ge(s_qk, q.g * 4 + u + 1)
                        if u >= KT:
                            act.activation(kf[:, q.par, u - KT, :], qk_bank[u][:], ACT.Copy)
                        act.activation(parts[:, q.par, u, PLACE[u // KT][HIGH], :], qk_bank[u][:], ACT.Copy,
                                       scale=QSCALE if u < KT else 1.0).then_inc(s_high, 1)
                    if u == KT and (t := at(LT)):
                        wait(act, s_v, (t.g - 2) * 2 + 2)
                        for k in range(KT):
                            act.wait_ge(s_t, t.g * KT + k + 1)
                            act.activation(xt_hi[:, t.par, k, :], t_bank[k][:], ACT.Copy).then_inc(s_hi, 1)
                    if q and u:
                        mid(q, u - 1)
                    if u == 2 and (t := at(LN)):
                        norm.root(act, t)
                if q:
                    mid(q, 2 * KT - 1)
                    if isinstance(q.g, int) and q.g == 0:
                        act.wait_ge(s_ones, 1)
                    for c in range(2):
                        act.wait_ge(s_v, q.g * 2 + c + 1)
                        for t in range(2):
                            ins = act.activation(va[:, q.par, 2 * c + t, :, 0:HD],
                                                 v_bank[c][:, t * D:t * D + D].rearrange("p (h e) -> p h e", h=H),
                                                 ACT.Copy)
                        ins.then_inc(s_vout, 1)

            sweep(act, body, LP)

        @block.vector
        def _(dve):
            norm.begin(dve)
            for w in range(3):
                dve.wait_ge(s_whi, w + 1)
                dve.tensor_tensor(wt_lo[:, w].rearrange("p k n -> p (k n)"), banks[w][:],
                                  wt_hi[:, w].bitcast(F32).rearrange("p k n -> p (k n)"),
                                  ALU.subtract).then_inc(s_wlo, 1)

            def body(at):
                q = at(LP)
                for u in range(2 * KT):
                    if q:
                        dve.wait_ge(s_high, q.g * 4 + u + 1)
                        wait(dve, s_low, (q.g - 1) * 4 + u + 1)
                        dve.scalar_tensor_tensor(out=rest[:, u, :], in0=qk_bank[u][:],
                                                 scalar=QSCALE if u < KT else 1.0,
                                                 in1=parts[:, q.par, u, PLACE[u // KT][HIGH], :],
                                                 op0=ALU.mult, op1=ALU.subtract).then_inc(s_rest, 1)
                    if u == KT and (t := at(LT)):
                        for k in range(KT):
                            dve.wait_ge(s_hi, t.g * KT + k + 1)
                            dve.tensor_tensor(xt_lo[:, t.par, k, :], t_bank[k][:],
                                              xt_hi[:, t.par, k, :].bitcast(F32), ALU.subtract).then_inc(s_lo, 1)
                    if u == 1 and (t := at(LN)):
                        dve.wait_ge(s_x[t.ring], (t.turn + 1) * DMA)
                        norm.front(dve, xb[:, t.ring], t)
                if q := at(LN):
                    wait(dve, s_t, (q.g - 2) * KT + KT)
                    norm.back(dve, xb[:, q.ring], xn[:, q.par], q)

            sweep(dve, body, LP)


class Unit:

    def __init__(self, b, i):
        self.i, self.gi, self.hq = i, i // UPG, i % UPG
        self.n = b * UPB + i
        self.g = b * GB + self.gi
        self.batch = b
        self.gpar = self.gi % 2
        self.ghalf = b * (GB // 2) + self.gi // 2
        self.p0 = i % P0_BUFS
        self.upar = i % 2
        self.uhalf = b * (UPB // 2) + i // 2


def march(eng, body, lags):
    def step(b, i):
        def at(lag):
            j = i - lag
            if j >= 0:
                return Unit(b, j) if not isinstance(b, int) or b < B else None
            if isinstance(b, int) and b == 0:
                return None
            return Unit(b - 1, j + UPB)
        return at

    for i in range(UPB):
        body(step(0, i))
    with eng.Fori(1, B) as b:
        for i in range(UPB):
            body(step(b, i))
    for i in range(lags):
        body(step(B, i))


SCORE_TILES = ((0, 0, 1, 0, 3), (0, 3, -1, 0, 1),
               (1, 0, 0, 0, 2), (1, 2, 3, 2, 2),
               (2, 0, 4, 3, 1), (2, 1, 2, 1, 3))
HEAD_COLS = 3 * GT
CUT_LOW = ((0, 1), (6, 1), (8, 2))
CUT_HIGH = ((2, 2), (5, 1), (11, 1))
SUM_ORDER = (1, 2, 0, 3, -1, 4)
CHUNK = 2 * GT
CHUNKS = NQ * HEAD_COLS // CHUNK
TILES = NQ * TB
TURN_OF_M, TURN_OF_S, TURN_BANKS = 3, TILES + 1, 3
TURN_OF_TILE = tuple(j if j < TURN_OF_M else j + 1 for j in range(TILES))
TILE_OF_TURN = {k: j for j, k in enumerate(TURN_OF_TILE)}
TURNS = TILES + 2
assert TURNS % TURN_BANKS == 0

L_KEY0, L_MAX, L_SHIFT, L_SCORE, L_SUM, L_OUT, L_STORE = 2, 3, 4, 6, 7, 8, 9


AFTER_TILE = (
    (("score", 0), ("score", 1)), (("score", 2),), (("score", 3), ("M", 0)), (("score", 4), ("score", 5)),
    (("sum", 0),), (("score", 6),), (("score", 7),), (("sum", 1),),
    (("score", 8),), (("score", 9),), (("sum", 2),), (("score", 10),),
    (("score", 11),), (("sum", 3),), (("sum", 4),), (("sum", 5), ("S", 0)))


def in_group(gi, kb):
    return not (gi == 0 and kb == -1) and not (gi == GB - 1 and kb == TB)


class Ahead:

    SEQS = 2

    def __init__(self, nc, ctx, kf_dram, wo, fast_b, w_fc, u, v, gate):
        def sb(name, shape, dt=F32):
            return ctx.enter_context(nc.sbuf_tensor(f"e_{name}", shape, dt))

        def sem(name):
            return ctx.enter_context(nc.semaphore(f"e_{name}"))

        self.nc, self.kf_dram = nc, kf_dram
        k_all = sb("k", [P, self.SEQS * KT * T])
        self.k = k_all[:].rearrange("p (b k t) -> p b k t", b=self.SEQS, k=KT)
        shared, kn, qn = k_all[:].bitcast(BF16), NQ * WIN, NQ * GT
        self.Q_SHARED = (2 * self.SEQS * KT * T - UPG * kn) // qn
        self.kw = [shared[:, i * kn:(i + 1) * kn].rearrange("p (h t) -> p h t", h=NQ) for i in range(UPG)]
        self.qw = [shared[:, UPG * kn + i * qn:UPG * kn + (i + 1) * qn].rearrange("p (h t) -> p h t", h=NQ)
                   for i in range(self.Q_SHARED)]
        self.w1_in = sb("w1_in", [P, MH, D])
        self.wo_in = sb("wo_in", [P, KT, D])
        self.u_in = sb("u_in", [P, MH, RANK])
        self.v_in = sb("v_in", [RANK, D])
        self.fb_t = sb("fb_t", [RANK, RANK])
        self.gate_c = sb("gate", [P, 1])
        self.s_k, self.s_in, self.s_w1in = sem("k"), sem("weights_in"), sem("w1_in")
        self.sources = (
            (self.w1_in[:], w_fc.rearrange("(m p) k -> p m k", p=P), self.s_w1in),
            (self.u_in[:], u.rearrange("(m p) r -> p m r", p=P), self.s_in),
            (self.v_in[:], v, self.s_in),
            (self.gate_c[:], gate.rearrange("(a b) -> a b", a=1).to_broadcast((P, 1)), self.s_in),
            (self.wo_in[:], wo.rearrange("(m p) k -> p m k", p=P), self.s_in),
            (self.fb_t[:], fast_b.rearrange("a b -> b a"), self.s_in))
        self.WEIGHTS = len(self.sources) - 1

    def load_weights(self, sp):
        with self.nc.allow_non_contiguous_dma(reason="16 by 16, turned"):
            for dst, src, sem_in in self.sources:
                sp.dma_start(dst, src).then_inc(sem_in, DMA)

    def load_k(self, sp, b):
        sp.dma_start(self.k[:, b], self.kf_dram[:, b * T:(b + 1) * T].rearrange("(k p) t -> p k t", p=P)
                     ).then_inc(self.s_k, DMA)


def stage_attend(nc, qk_dram, va_dram, o_dram, ahead):
    with ExitStack() as ctx:
        def sb(name, shape, dt=F32):
            return ctx.enter_context(nc.sbuf_tensor(f"a_{name}", shape, dt))

        def sem(name):
            return ctx.enter_context(nc.semaphore(f"a_{name}"))

        rows = SLOT_ROWS + SHIFT_ROWS
        kw = [ahead.kw, [sb(f"k1{q}", [P, NQ, WIN], BF16) for q in range(UPG)]]
        qw = [ahead.qw + [sb(f"q0{q}", [P, NQ, GT], BF16) for q in range(ahead.Q_SHARED, UPG)],
              [sb(f"q1{q}", [P, NQ, GT], BF16) for q in range(UPG)]]
        vw = sb("v", [P, 2, TB + 2, VROW])
        v0 = sb("v0", [P, VROW])
        k0 = sb("k0", [P, H], BF16)
        ident = sb("ident", [P, P])
        band = sb("band", [P, 3 * P + 1], BF16)
        gate0 = sb("gate0", [P, NQ, TB])
        masked = sb("masked", [P, TILES, 3 * P + 1])
        mx = sb("max", [P, UPG, P])
        d0 = sb("d0", [P, 2, TILES])
        p0 = sb("p0", [P, P0_BUFS, NQ, TB])
        neg = sb("neg", [TILES, P])
        rest = sb("neg_rest", [TILES, P])
        shift = sb("shift", [TILES, 2, SHIFT_ROWS, P], BF16)
        pe_w = sb("weights", [P, 2, NQ * HEAD_COLS])
        sums = sb("sums", [P, 2, GT])
        turned = sb("turned", [P, 2, TB, NQ, VW])
        t0 = sb("key0_part", [P, UPG, TB, NQ, HD])
        den = sb("den", [P, 2, TB, NQ])
        rden = sb("rden", [P, 2, TB, NQ])
        num = sb("num", [P, 2, TB, NQ, HD])
        ob = sb("o", [P, 2, TB, D])
        score = [ctx.enter_context(nc.psum_tensor(f"a_score{i}", [P, CHUNK], F32)) for i in range(2)]
        sum_bank = ctx.enter_context(nc.psum_tensor("a_sum", [P, GT], F32))
        turn = [ctx.enter_context(nc.psum_tensor(f"a_turn{i}", [P, GT], F32)) for i in range(TURN_BANKS)]

        s_init, s_pool, s_ones = sem("init"), sem("pool_init"), sem("ones")
        s_load = [[sem(f"qk_in{g}{q}") for q in range(UPG)] for g in range(2)]
        s_v, s_v0 = [sem("v_in0"), sem("v_in1")], [sem(f"v0_in{q}") for q in range(UPG)]
        s_row = [sem("row0"), sem("row1")]
        s_k0 = sem("k0")
        s_tile, s_tile_read = sem("tile"), sem("tile_read")
        s_m, s_m_read, s_s, s_s_read = sem("m"), sem("m_read"), sem("s"), sem("s_read")
        s_den = sem("den")
        s_d0, s_p0 = sem("d0"), sem("p0")
        s_shift = sem("shift")
        s_score, s_exp, s_cut = sem("score"), sem("exp"), sem("cut")
        s_sum, s_sumout = sem("sum"), sem("sum_out")
        s_t0, s_gate = sem("t0"), sem("gate")
        s_rden, s_num, s_o = sem("rden"), sem("num"), sem("o")
        s_out = [sem("out0"), sem("out1")]
        LOADS = 2 * (1 + len(SINGLES[0]))
        block = ctx.enter_context(nc.Block())

        def window(gi):
            return (1 if gi == 0 else 0), (TB + 1 if gi == GB - 1 else TB + 2)

        @block.sync
        def _(sp):
            def body(at):
                if u := at(0):
                    wait(sp, s_score, (u.n - 2 * UPG) * CHUNKS + CHUNKS)
                    lo, hi = window(u.gi)
                    h0 = u.hq * NQ
                    keys = bass.ds(u.g * GT + (lo - 1) * P, (hi - lo) * P)
                    queries = bass.ds(u.g * GT, GT)
                    for which, buf, cols, tokens in ((1, kw[u.gpar][u.hq], slice(lo * P, hi * P), keys),
                                                     (0, qw[u.gpar][u.hq], slice(0, GT), queries)):
                        rows_of = qk_dram[which, h0 * HD:(h0 + NQ) * HD, :, tokens]
                        sp.dma_start(buf[0:3 * HD, :, cols], rows_of.rearrange("(h d) s t -> (d s) h t", d=HD)
                                     ).then_inc(s_load[u.gpar][u.hq], DMA)
                        for n, part in enumerate(SINGLES[which]):
                            sp.dma_start(buf[(3 + n) * HD:(4 + n) * HD, :, cols],
                                         rows_of[:, PLACE[which][part], :].rearrange("(h d) t -> d h t", d=HD)
                                         ).then_inc(s_load[u.gpar][u.hq], DMA)
                if (u := at(L_MAX)) and u.hq == 0:
                    wait(sp, s_sum, (u.n - UPG * 2) + UPG)
                    lo, hi = window(u.gi)
                    sp.dma_start(vw[:, u.gpar, lo:hi, :],
                                 va_dram[bass.ds(u.g * GT + (lo - 1) * P, (hi - lo) * P), :]
                                 .rearrange("(w p) n -> p w n", p=P)).then_inc(s_v[u.gpar], DMA)
                if (u := at(L_SHIFT)) and u.gi == 0:
                    wait(sp, s_t0, u.n - UPG + 1)
                    cols = slice(u.hq * NQ * VW, (u.hq + 1) * NQ * VW)
                    sp.dma_start(v0[:, cols], va_dram[bass.ds(u.batch * T, 1), cols].to_broadcast((P, NQ * VW))
                                 ).then_inc(s_v0[u.hq], DMA)
                if u := at(L_SHIFT):
                    sp.wait_ge(s_shift, u.n * 3 + 3)
                    for part in range(SHIFT_ROWS):
                        row = qw[u.gpar][u.hq][SLOT_ROWS + part:SLOT_ROWS + part + 1, :, :]
                        sp.dma_start(row.rearrange("s h (t q) -> s (h t) q", q=P),
                                     shift[:, u.upar, part, :]).then_inc(s_row[u.upar], DMA)
                last = (G - 1) * UPG
                if (u := at(L_SHIFT)) and isinstance(u.n, int) and u.n == last:
                    ahead.load_weights(sp)
                if (u := at(L_SUM)) and isinstance(u.n, int) and u.n == last:
                    sp.wait_ge(s_score, last * CHUNKS)
                    for b in range(ahead.SEQS):
                        ahead.load_k(sp, b)
                if (u := at(L_STORE)) and u.hq == UPG - 1:
                    sp.wait_ge(s_o, u.n + 1)
                    sp.dma_start(o_dram[bass.ds(u.g * GT, GT), :].rearrange("(t p) d -> p t d", p=P),
                                 ob[:, u.gpar]).then_inc(s_out[u.gpar], DMA)

            march(sp, body, L_STORE)
            for par in range(2):
                sp.wait_ge(s_out[par], DMA * (G // 2))

        @block.gpsimd
        def _(pool):
            identity(pool, ident[:], s_pool)
            pool.memset(band[:], 0.0).then_inc(s_pool, 1)
            pool.wait_ge(s_pool, 3)
            pool.affine_select(out=band[:, 0:P], in_=band[:, 0:P], compare_op=ALU.is_ge, fill=NEG, base=0,
                               pattern=[[1, P]], channel_multiplier=-1)
            pool.affine_select(out=band[:, 2 * P:3 * P], in_=band[:, 2 * P:3 * P], compare_op=ALU.is_ge,
                               fill=NEG, base=0, pattern=[[-1, P]], channel_multiplier=1)
            pool.memset(gate0[:], 1.0).then_inc(s_pool, 1)
            pool.wait_ge(s_pool, 4)
            pool.affine_select(out=gate0[:], in_=gate0[:], compare_op=ALU.is_gt, fill=0.0, base=-P,
                               pattern=[[0, NQ], [P, TB]], channel_multiplier=1).then_inc(s_pool, 1)

            pool.wait_ge(s_pool, 5)
            for g in range(2):
                for q in range(UPG):
                    pool.memset(kw[g][q][SLOT_ROWS:rows, :, :], 1.0).then_inc(s_ones, 1)
                    pool.wait_ge(s_ones, g * UPG + q + 1)
            exp_turn = Turn(pool, s_exp, "exp_turn", CHUNKS // 2, CHUNKS // 2)

            def cut_half(u, half):
                exp_turn.wait(u.n * CHUNKS + (half + 1) * CHUNKS // 2)
                w = pe_w[:, u.upar].rearrange("p (h c q) -> p h c q", h=NQ, q=P)
                for runs, sign in ((CUT_LOW, 1), (CUT_HIGH, -1)):
                    for c, m in runs:
                        cut = w[:, half * NQ // 2:(half + 1) * NQ // 2, c:c + m, :]
                        ins = pool.affine_select(out=cut, in_=cut, compare_op=ALU.is_ge, fill=0.0, base=0,
                                                 pattern=[[0, NQ // 2], [0, m], [sign, P]],
                                                 channel_multiplier=-sign)
                ins.then_inc(s_cut, 1)

            def body(at):
                if u := at(L_SCORE):
                    pool.wait_ge(s_p0, u.n + 1)
                    if u.gi == 0:
                        pool.tensor_tensor(p0[:, u.p0], p0[:, u.p0], gate0[:], ALU.mult).then_inc(s_gate, 1)
                        pool.wait_ge(s_gate, u.batch * UPG + u.hq + 1)
                        pool.wait_ge(s_v0[u.hq], (u.batch + 1) * DMA)
                    wait(pool, s_num, u.n - 3)
                    values = v0[:, u.hq * NQ * VW:(u.hq + 1) * NQ * VW].rearrange("p (h e) -> p h e", h=NQ)
                    pool.tensor_tensor(
                        t0[:, u.hq], values[:, :, 0:HD].unsqueeze(1).broadcast_to([P, TB, NQ, HD]),
                        p0[:, u.p0].rearrange("p h t -> p t h").unsqueeze(3).broadcast_to([P, TB, NQ, HD]),
                        ALU.mult).then_inc(s_t0, 1)
                if u := at(L_SHIFT):
                    pool.wait_ge(s_m_read, u.n + 1)
                    pool.tensor_tensor(rest[:], neg[:], shift[:, u.upar, HIGH, :], ALU.subtract).then_inc(s_shift, 1)
                if u := at(L_SCORE):
                    cut_half(u, 0)
                if u := at(L_SHIFT):
                    pool.wait_ge(s_shift, u.n * 3 + 2)
                    pool.tensor_tensor(shift[:, u.upar, LOW, :], rest[:], shift[:, u.upar, MID, :], ALU.subtract
                                       ).then_inc(s_shift, 1)
                if u := at(L_STORE):
                    pool.wait_ge(s_s_read, u.n + 1)
                    pool.tensor_tensor(num[:, u.upar], turned[:, u.upar, :, :, 0:HD], t0[:, u.hq], ALU.add
                                       ).then_inc(s_num, 1)
                if u := at(L_SCORE):
                    cut_half(u, 1)
                if u := at(L_STORE):
                    pool.wait_ge(s_num, u.n + 1)
                    pool.wait_ge(s_rden, u.n + 1)
                    if u.hq == 0:
                        wait(pool, s_out[u.gpar], u.ghalf * DMA)
                    o = ob[:, u.gpar].rearrange("p t (h e) -> p t h e", e=HD)[:, :, u.hq * NQ:(u.hq + 1) * NQ, :]
                    pool.tensor_tensor(o, num[:, u.upar], rden[:, u.upar].unsqueeze(3).broadcast_to([P, TB, NQ, HD]),
                                       ALU.mult).then_inc(s_o, 1)

            march(pool, body, L_STORE)

        @block.tensor
        def _(pe):
            pe.wait_ge(s_init, 4)
            pe.wait_ge(s_pool, 2)

            def body(at):
                um, ux, us, up, uo = at(L_SHIFT), at(L_MAX), at(L_SCORE), at(L_SUM), at(L_OUT)

                def bank_read(k):
                    before = k - TURN_BANKS
                    if before + TURNS == TURN_OF_S:
                        if uo:
                            wait(pe, s_s_read, uo.n)
                    elif before < 0:
                        if ux:
                            wait(pe, s_tile_read, (ux.n - 1) * TILES + TILE_OF_TURN[before + TURNS] + 1)
                    elif before == TURN_OF_M and um:
                        pe.wait_ge(s_m_read, um.n + 1)
                    elif ux:
                        tile = TILE_OF_TURN.get(before, TILE_OF_TURN.get(before - TURN_BANKS))
                        pe.wait_ge(s_tile_read, ux.n * TILES + tile + 1)
                    else:
                        pe.wait_ge(s_tile_read, UNITS * TILES)
                        if k == TURN_OF_S:
                            pe.wait_ge(s_s_read, uo.n)

                def maxima_turned():
                    if um:
                        pe.wait_ge(s_d0, um.n + 1)
                        bank_read(TURN_OF_M)
                        pe.transpose(turn[TURN_OF_M % TURN_BANKS][:, 0:P], mx[:, um.hq, :], ident[:]
                                     ).then_inc(s_m, 1)

                def sums_turned():
                    if uo:
                        pe.wait_ge(s_sumout, uo.n + 1)
                        bank_read(TURN_OF_S)
                        for t in range(TB):
                            ins = pe.transpose(turn[TURN_OF_S % TURN_BANKS][:, t * P:t * P + P],
                                               sums[:, uo.upar, t * P:t * P + P], ident[:])
                        ins.then_inc(s_s, 1)

                def max_tile(j):
                    if not ux:
                        return
                    k = TURN_OF_TILE[j]
                    h, t = j // TB, j % TB
                    if j == 0:
                        pe.wait_ge(s_load[ux.gpar][ux.hq], (ux.ghalf + 1) * LOADS * DMA)
                        if ux.gi == 0:
                            pe.wait_ge(s_k0, ux.batch * UPG + ux.hq + 1)
                    bank_read(k)
                    lo = P if ux.gi == 0 and t == 0 else 0
                    hi = 2 * P if ux.gi == GB - 1 and t == TB - 1 else 3 * P
                    q, kk = qw[ux.gpar][ux.hq], kw[ux.gpar][ux.hq]
                    lhs = q[0:SLOT_ROWS, h, t * P:t * P + P]
                    pe.matmul(turn[k % TURN_BANKS][:, lo:hi], lhs, kk[0:SLOT_ROWS, h, t * P + lo:t * P + hi],
                              start=True, stop=True)
                    key = ux.hq * NQ + h
                    pe.matmul(turn[k % TURN_BANKS][:, hi:hi + 1], lhs, k0[0:SLOT_ROWS, key:key + 1],
                              start=True, stop=True).then_inc(s_tile, 1)

                def score_bank(n):
                    if not us:
                        return
                    c = n // 2
                    if n == 0:
                        if isinstance(us.n, int) and us.n < 2 * UPG:
                            pe.wait_ge(s_ones, us.n + 1)
                        pe.wait_ge(s_row[us.upar], (us.uhalf + 1) * DMA * SHIFT_ROWS)
                    if n % 2 == 0:
                        wait(pe, s_exp, us.n * CHUNKS + c - 1)
                    j, third = n // 3, n % 3
                    q, kk = qw[us.gpar][us.hq], kw[us.gpar][us.hq]
                    tiles = [x for x in SCORE_TILES if x[0] == third and in_group(us.gi, x[2])]
                    for _, col, kb, qb, m in tiles:
                        ins = pe.matmul(
                            score[c % 2][:, (n % 2) * GT + col * P:(n % 2) * GT + (col + m) * P],
                            kk[0:rows, j, (kb + 1) * P:(kb + 2) * P], q[0:rows, j, qb * P:(qb + m) * P],
                            start=True, stop=True)
                    if n % 2 == 1:
                        ins.then_inc(s_score, 1)

                def sum_block(o):
                    if not up:
                        return
                    kb = SUM_ORDER[o]
                    if o == 0:
                        pe.wait_ge(s_cut, up.n * 2 + 2)
                        wait(pe, s_sumout, up.n)
                        if up.hq == 0:
                            pe.wait_ge(s_v[up.gpar], (up.ghalf + 1) * DMA)
                    last = [x for x in SUM_ORDER if in_group(up.gi, x)][-1]
                    if in_group(up.gi, kb):
                        third, col, _, qb, m = [x for x in SCORE_TILES if x[2] == kb][0]
                        for j in range(NQ):
                            c0 = j * HEAD_COLS + third * GT + col * P
                            h = up.hq * NQ + j
                            ins = pe.matmul(sum_bank[32 * j:32 * j + VW, qb * P:(qb + m) * P],
                                            vw[:, up.gpar, kb + 1, h * VW:h * VW + VW],
                                            pe_w[:, up.upar, c0:c0 + m * P], start=(o == 0), stop=(kb == last),
                                            skip_group_check=True)
                        if kb == last:
                            ins.then_inc(s_sum, 1)

                for j in range(TILES):
                    max_tile(j)
                    for kind, n in AFTER_TILE[j]:
                        if kind == "score":
                            score_bank(n)
                        elif kind == "sum":
                            sum_block(n)
                        elif kind == "M":
                            maxima_turned()
                        else:
                            sums_turned()

            march(pe, body, L_STORE)

        @block.scalar
        def _(act):
            def body(at):
                if u := at(L_STORE):
                    act.wait_ge(s_s, u.n + 1)
                    wait(act, s_den, u.n - 1)
                    wait(act, s_num, u.n - 1)
                    act.activation(turned[:, u.upar],
                                   turn[TURN_OF_S % TURN_BANKS][:].rearrange("p (t h e) -> p t h e", t=TB, h=NQ)
                                   [:, :, :, 0:VW], ACT.Copy).then_inc(s_s_read, 1)
                if u := at(L_OUT):
                    act.wait_ge(s_sum, u.n + 1)
                    wait(act, s_s, u.n - 1)
                    act.activation(sums[:, u.upar, :], sum_bank[:], ACT.Copy).then_inc(s_sumout, 1)
                us, ud = at(L_SCORE), at(L_SHIFT)
                for c in range(CHUNKS):
                    if us:
                        act.wait_ge(s_score, us.n * CHUNKS + c + 1)
                        if c == 0:
                            wait(act, s_sum, us.n - 1)
                        act.activation(pe_w[:, us.upar, c * CHUNK:(c + 1) * CHUNK], score[c % 2][:], ACT.Exp
                                       ).then_inc(s_exp, 1)
                    if ud and c == 0:
                        act.wait_ge(s_d0, ud.n + 1)
                        wait(act, s_den, ud.n + 1 - P0_BUFS)
                        act.activation(p0[:, ud.p0].rearrange("p h t -> p (h t)"), d0[:, ud.upar, :], ACT.Exp
                                       ).then_inc(s_p0, 1)
                    if ud and c == 3:
                        act.wait_ge(s_shift, ud.n * 3 + 1)
                        act.activation(shift[:, ud.upar, MID, :], rest[:], ACT.Copy).then_inc(s_shift, 1)
                    if ud and c == 1:
                        t_in = turn[TURN_OF_M % TURN_BANKS][0:TILES, 0:P]
                        wait(act, s_row[ud.upar], ud.uhalf * DMA * SHIFT_ROWS)
                        wait(act, s_shift, ud.n * 3)
                        act.wait_ge(s_m, ud.n + 1)
                        act.activation(shift[:, ud.upar, HIGH, :], t_in, ACT.Copy, scale=-1.0)
                        act.activation(neg[:], t_in, ACT.Copy, scale=-1.0).then_inc(s_m_read, 1)

            march(act, body, L_STORE)

        @block.vector
        def _(dve):
            dve.memset(score[0][:], 0.0).then_inc(s_init, 1)
            dve.memset(score[1][:], 0.0).then_inc(s_init, 1)
            dve.memset(sum_bank[:], 0.0).then_inc(s_init, 1)
            dve.memset(mx[:], 0.0).then_inc(s_init, 1)
            dve.wait_ge(s_init, 4)
            dve.wait_ge(s_pool, 5)
            tile_turn = Turn(dve, s_tile, "tile_turn", 1)

            def body(at):
                ux, uo = at(L_MAX), at(L_STORE)
                if (u := at(L_KEY0)) and u.gi == 0:
                    wait(dve, s_tile_read, (u.n - UPG) * TILES + TILES)
                    dve.wait_ge(s_load[0][u.hq], (u.ghalf + 1) * LOADS * DMA)
                    dve.tensor_copy(k0[0:SLOT_ROWS, u.hq * NQ:u.hq * NQ + NQ],
                                    kw[0][u.hq][0:SLOT_ROWS, :, P]).then_inc(s_k0, 1)
                for j in range(TILES):
                    if ux:
                        bank = turn[TURN_OF_TILE[j] % TURN_BANKS]
                        h, t = j // TB, j % TB
                        lo = P if ux.gi == 0 and t == 0 else 0
                        hi = 2 * P if ux.gi == GB - 1 and t == TB - 1 else 3 * P
                        first = 3 * P - (hi - lo)
                        if j == 0:
                            wait(dve, s_d0, ux.n)
                        tile_turn.wait(ux.n * TILES + j + 1)
                        dve.tensor_tensor_reduce(
                            out=masked[:, j, first:3 * P + 1], in0=bank[:, lo:hi + 1],
                            in1=band[:, lo:hi + 1], scale=1.0, scalar=NEG, op0=ALU.add, op1=ALU.max,
                            accum_out=mx[:, ux.hq, j:j + 1]).then_inc(s_tile_read, 1)
                if uo:
                    wait(dve, s_o, uo.n - 1)
                    dve.wait_ge(s_s_read, uo.n + 1)
                    dve.tensor_tensor(den[:, uo.upar], turned[:, uo.upar, :, :, HD],
                                      p0[:, uo.p0].rearrange("p h t -> p t h"), ALU.add).then_inc(s_den, 1)
                if ux:
                    dve.wait_ge(s_tile_read, ux.n * TILES + TILES)
                    wait(dve, s_p0, ux.n - 1)
                    dve.tensor_tensor(d0[:, ux.upar, :], masked[:, :, 3 * P], mx[:, ux.hq, 0:TILES], ALU.subtract
                                      ).then_inc(s_d0, 1)
                if uo:
                    dve.wait_ge(s_den, uo.n + 1)
                    dve.reciprocal(rden[:, uo.upar], den[:, uo.upar]).then_inc(s_rden, 1)

            march(dve, body, L_STORE)


def block_mask(pool, tile, groups, size, base, sem):
    start = sem[1]
    pool.memset(tile, 1.0).then_inc(sem[0], 1)
    pool.wait_ge(sem[0], start + 1)
    pool.affine_select(out=tile, in_=tile, compare_op=ALU.is_ge, fill=0.0, base=base,
                       pattern=[[-size, groups]], channel_multiplier=1).then_inc(sem[0], 1)
    pool.wait_ge(sem[0], start + 2)
    pool.affine_select(out=tile, in_=tile, compare_op=ALU.is_ge, fill=0.0, base=size - 1 - base,
                       pattern=[[size, groups]], channel_multiplier=-1).then_inc(sem[0], 1)
    sem[1] = start + 3


class Weights:

    def __init__(self, nc, ctx):
        def sb(name, shape, dt=F32):
            return ctx.enter_context(nc.sbuf_tensor(f"w_{name}", shape, dt))

        self.ident = sb("ident", [P, P])
        self.wo_hi, self.wo_lo = sb("wo_hi", [P, KT, D], F32R), sb("wo_lo", [P, KT, D], F32R)
        self.w1_hi, self.w1_lo = sb("w1_hi", [P, KT, HID], F32R), sb("w1_lo", [P, KT, HID], F32R)
        self.w2_t = sb("w2_t", [P, MH, D], F32R)
        self.mag_row = sb("mag_row", [P, 2 * D])


def stage_row_zero(nc, qk_dram, kf_dram, va_dram, o_dram, w_proj, ahead, weights):
    CH = T // GT
    NB = T // P
    QR = 32
    RUN = 32
    with ExitStack() as ctx:
        def sb(name, shape, dt=F32):
            return ctx.enter_context(nc.sbuf_tensor(f"z_{name}", shape, dt))

        def sem(name):
            return ctx.enter_context(nc.semaphore(f"z_{name}"))

        qp_run = sb("q_parts", [P, KT, B, 3, RUN], BF16)
        qp = [qp_run[:, :, :, place, 0] for place in range(3)]
        q0 = sb("q", [P, KT, B])
        head_of = sb("head_of", [P, KT, H])
        qd = sb("q_diag", [P, KT, B, QR])
        kf_flat = sb("k", [P, (B - ahead.SEQS) * KT * T])
        kf_late = kf_flat[:].rearrange("p (b k t) -> p b k t", b=B - ahead.SEQS, k=KT)
        kf = [ahead.k[:, b] if b < ahead.SEQS else kf_late[:, b - ahead.SEQS] for b in range(B)]
        EARLY = B - 1
        va_early = sb("v", [P, EARLY, NB, VROW])
        va = [va_early[:, b] for b in range(EARLY)]
        va += [kf_flat[:, 0:NB * VROW].rearrange("p (n e) -> p n e", n=NB)]
        own = sb("own", [P, H, VW])
        seq_of = sb("seq_of", [P, B])
        nmax = sb("nmax", [P, 1])
        den = sb("den", [P, 1])
        rden = sb("rden", [P, 1])
        w = sb("w", [P, T])
        wt = sb("wt", [P, NB, P])
        picked = sb("picked", [P, H, VW])
        row = sb("row", [B, H, HD])
        wo_in, w1_in, u_in, fb_t, v_in, gate_c = (
            ahead.wo_in, ahead.w1_in, ahead.u_in, ahead.fb_t, ahead.v_in, ahead.gate_c)
        s_in, s_w1in, WEIGHTS = ahead.s_in, ahead.s_w1in, ahead.WEIGHTS
        w1_low = sb("w1_low", [P, MH, D])
        w2_in = sb("w2_in", [P, KT, HID])
        w2_tern = sb("w2_tern", [P, KT, HID])
        mag1, half1, nhalf1 = sb("mag1", [P, MH]), sb("half1", [P, MH]), sb("nhalf1", [P, MH])
        mag2, half2, nhalf2 = sb("mag2", [P, KT]), sb("half2", [P, KT]), sb("nhalf2", [P, KT])
        mag_diag = sb("mag_diag", [P, KT, P])
        ones = sb("ones", [P, P])
        u_t = sb("u_t", [P, P])
        u_m = w[:, 0:MH * P].rearrange("p (m q) -> p m q", m=MH)
        tile_of = sb("tile_of", [P, MH])
        fb_rep = sb("fb_rep", [RANK, MH, RANK])
        low_v = sb("low_v", [P, D])
        ident, wo_hi, wo_lo, w1_hi, w1_lo, w2_t, mag_row = (
            weights.ident, weights.wo_hi, weights.wo_lo, weights.w1_hi, weights.w1_lo, weights.w2_t, weights.mag_row)
        psum = ctx.enter_context(nc.psum_tensor("z_psum", [P, 8, GT], F32))
        banks = [psum[:, i, :] for i in range(8)]
        scores, turned, sums, total = psum[:, 4:8, :].rearrange("p a n -> p (a n)"), psum[:, 0:2, :], banks[2], banks[3]
        s_q, s_k, s_v, s_pool = sem("q"), sem("k"), sem("v"), sem("pool")
        s_qd, s_sc, s_max, s_exp = sem("qd"), sem("sc"), sem("max"), sem("exp")
        s_turn, s_wt, s_sum, s_pick, s_tot, s_row, s_out = (
            sem("turn"), sem("wt"), sem("sum"), sem("pick"), sem("tot"), sem("row"), sem("out"))
        s_w2in, s_wpool = sem("w2_in"), sem("weights_pool")
        s_prep, s_wolo, s_pt, s_pc = sem("prep"), sem("wo_lo"), sem("prep_turned"), sem("prep_copied")
        s_m1, s_low, s_w1, s_w1hi = sem("low_v"), sem("low"), sem("w1"), sem("w1_hi")
        s_scale, s_tern, s_mag = sem("scale"), sem("ternary"), sem("mag_row")
        block = ctx.enter_context(nc.Block())

        @block.sync
        def _(sp):
            sp.dma_start(w2_in[:], w_proj.rearrange("(m p) k -> p m k", p=P)).then_inc(s_w2in, DMA)
            for k in range(KT):
                for b in range(B):
                    sp.dma_start(qp_run[:, k, b], qk_dram[0, k * P:(k + 1) * P, :, b * T:b * T + RUN]
                                 ).then_inc(s_q, DMA)
            for b in range(ahead.SEQS, B):
                sp.dma_start(kf[b], kf_dram[:, b * T:(b + 1) * T].rearrange("(k p) t -> p k t", p=P)
                             ).then_inc(s_k, DMA)
            for b in range(B):
                if b == EARLY:
                    sp.wait_ge(s_sc, 1)
                sp.dma_start(va[b], va_dram[b * T:(b + 1) * T, :].rearrange("(n p) e -> p n e", p=P)
                             ).then_inc(s_v, DMA)
            sp.wait_ge(s_row, 1)
            sp.dma_start(o_dram[0:N:T, :], row[:].rearrange("b h e -> b (h e)")).then_inc(s_out, DMA)
            sp.wait_ge(s_out, DMA)

        @block.gpsimd
        def _(pool):
            identity(pool, ident[:], s_wpool)
            block_mask(pool, tile_of[:], MH, RANK, 0, [s_wpool, 2])
            pool.wait_ge(s_wpool, 5)
            count = [s_pool, 0]
            for k in range(KT):
                block_mask(pool, head_of[:, k, :], H, HD, k * P, count)
            block_mask(pool, seq_of[:], B, QR, 0, count)
            pool.memset(own[:], 0.0).then_inc(s_pool, 1)
            pool.wait_ge(s_pool, count[1] + 1)
            for b in range(B):
                pool.affine_select(out=own[:], in_=own[:], compare_op=ALU.not_equal, fill=1.0, base=-QR * b,
                                   pattern=[[-1, H], [0, VW]], channel_multiplier=1).then_inc(s_pool, 1)
                pool.wait_ge(s_pool, count[1] + 2 + b)

        POOL_DONE = 3 * (KT + 1) + 5

        @block.vector
        def _(dve):
            def ternary(w, tern, mag, half, nhalf, width, n, steps, terns):
                dve.tensor_reduce(mag[:], w[:], AX.X, ALU.add, apply_absolute_value=True).then_inc(s_scale, 1)
                dve.wait_ge(s_scale, steps + 1)
                dve.tensor_scalar(mag[:], mag[:], 1.0 / width, 1e-5, ALU.mult, ALU.max).then_inc(s_scale, 1)
                dve.wait_ge(s_scale, steps + 2)
                dve.tensor_scalar(half[:], mag[:], 0.5, None, ALU.mult)
                dve.tensor_scalar(nhalf[:], mag[:], -0.5, None, ALU.mult).then_inc(s_scale, 1)
                dve.wait_ge(s_scale, steps + 3)
                for m in range(n):
                    dve.tensor_scalar(tern[:, m, :], w[:, m, :], nhalf[:, m:m + 1], None, ALU.is_lt).then_inc(s_tern, 1)
                dve.wait_ge(s_tern, terns + n)
                for m in range(n):
                    ins = dve.scalar_tensor_tensor(out=tern[:, m, :], in0=w[:, m, :], scalar=half[:, m:m + 1],
                                                   in1=tern[:, m, :], op0=ALU.is_gt, op1=ALU.subtract)
                    ins.then_inc(s_tern, 1)
                dve.wait_ge(s_tern, terns + 2 * n)

            dve.memset(ones[:], 1.0)
            dve.wait_ge(s_wpool, 2)
            dve.wait_ge(s_w1in, DMA)
            ternary(w1_in, w1_low, mag1, half1, nhalf1, D, MH, 0, 0)
            dve.memset(qd[:], 0.0).then_inc(s_qd, 1)
            dve.wait_ge(s_q, KT * B * DMA)
            dve.wait_ge(s_pool, POOL_DONE)
            dve.tensor_tensor(q0[:], qp[0], qp[1], ALU.add).then_inc(s_qd, 1)
            dve.wait_ge(s_qd, 2)
            dve.tensor_tensor(q0[:], q0[:], qp[2], ALU.add).then_inc(s_qd, 1)
            dve.wait_ge(s_qd, 3)
            for k in range(KT):
                for b in range(B):
                    dve.tensor_scalar(qd[:, k, b, 0:H], head_of[:, k, :], q0[:, k, b:b + 1], None, ALU.mult
                                      ).then_inc(s_qd, 1)
            dve.wait_ge(s_in, WEIGHTS * DMA)
            dve.tensor_copy(fb_rep[:], fb_t[:].unsqueeze(1).broadcast_to([RANK, MH, RANK])).then_inc(s_prep, 1)
            dve.wait_ge(s_m1, 1)
            dve.tensor_scalar(low_v[:], banks[2][:, 0:D], gate_c[:, 0:1], None, ALU.mult).then_inc(s_m1, 1)
            dve.wait_ge(s_pc, 1)
            dve.tensor_tensor(wo_lo[:].rearrange("p k n -> p (k n)"), banks[0][:],
                              wo_hi[:].bitcast(F32).rearrange("p k n -> p (k n)"), ALU.subtract).then_inc(s_wolo, 1)
            for m in range(MH):
                if m % 2 == 0:
                    dve.wait_ge(s_low, m // 2 + 1)
                dve.scalar_tensor_tensor(out=w1_low[:, m, :], in0=w1_low[:, m, :], scalar=mag1[:, m:m + 1],
                                         in1=banks[4 + m // 2][:, m % 2 * D:(m % 2 + 1) * D],
                                         op0=ALU.mult, op1=ALU.add).then_inc(s_w1, 1)
            dve.wait_ge(s_w2in, DMA)
            ternary(w2_in, w2_tern, mag2, half2, nhalf2, HID, KT, 3, 2 * MH)
            for m in range(KT):
                ins = dve.tensor_scalar(mag_diag[:, m, :], ident[:], mag2[:, m:m + 1], None, ALU.mult)
            ins.then_inc(s_mag, 1)
            for n in range(4):
                k, c = n // 2, n % 2 * GT
                dve.wait_ge(s_w1hi, n + 1)
                dve.tensor_tensor(w1_lo[:, k, c:c + GT], banks[n][:], w1_hi[:, k, c:c + GT].bitcast(F32),
                                  ALU.subtract).then_inc(s_pc, 1)

            dve.wait_ge(s_sc, 1)
            dve.tensor_reduce(nmax[:], scores[:], AX.X, ALU.max, negate=True).then_inc(s_max, 1)
            dve.wait_ge(s_exp, 1)
            dve.reciprocal(rden[:], den[:]).then_inc(s_max, 1)
            for n in range(NB // TB):
                dve.wait_ge(s_turn, n + 1)
                dve.tensor_copy(wt[:, n * TB:(n + 1) * TB, :].rearrange("p a b -> p (a b)"), turned[:, n % 2, :]
                                ).then_inc(s_wt, 1)
            dve.wait_ge(s_sum, 1)
            dve.wait_ge(s_max, 2)
            dve.scalar_tensor_tensor(out=picked[:].rearrange("p h e -> p (h e)"), in0=sums[:, 0:VROW],
                                     scalar=rden[:, 0:1], in1=own[:].rearrange("p h e -> p (h e)"),
                                     op0=ALU.mult, op1=ALU.mult).then_inc(s_pick, 1)
            dve.wait_ge(s_tot, 1)
            dve.tensor_copy(row[:], total[0:B, 0:VROW].rearrange("b (h e) -> b h e", h=H)[:, :, 0:HD]
                            ).then_inc(s_row, 1)

        @block.scalar
        def _(act):
            act.wait_ge(s_pt, 1)
            act.activation(wo_hi[:].rearrange("p k n -> p (k n)"), banks[0][:], ACT.Copy).then_inc(s_pc, 1)
            act.wait_ge(s_pt, 2)
            act.activation(u_t[:], banks[1][:, 0:P], ACT.Copy).then_inc(s_pc, 1)
            act.wait_ge(s_pc, 2)
            for m in range(MH):
                act.activation(u_m[:, m, :], u_t[:], ACT.Copy, scale=tile_of[:, m:m + 1]).then_inc(s_pc, 1)
            for n in range(4):
                act.wait_ge(s_pt, 2 + n + 1)
                k, c = n // 2, n % 2 * GT
                act.activation(w1_hi[:, k, c:c + GT], banks[n][:], ACT.Copy).then_inc(s_w1hi, 1)
            for n in range(4):
                act.wait_ge(s_pt, 6 + n + 1)
                act.activation(w2_t[:, 2 * n:2 * n + 2, :].rearrange("p a b -> p (a b)"), banks[n][:], ACT.Copy
                               ).then_inc(s_pc, 1)
            act.wait_ge(s_mag, 2)
            act.activation(mag_row[:], banks[3][:], ACT.Copy).then_inc(s_mag, 1)

            act.wait_ge(s_max, 1)
            act.activation(w[:], scores[:], ACT.Exp, bias=nmax[:, 0:1], accum_out=den[:, 0:1]).then_inc(s_exp, 1)

        @block.tensor
        def _(pe):
            pe.wait_ge(s_wpool, 5)
            pe.wait_ge(s_in, WEIGHTS * DMA)
            for k in range(KT):
                for m in range(KT):
                    ins = pe.transpose(banks[0][:, k * D + m * P:k * D + m * P + P], wo_in[:, m, k * P:k * P + P],
                                       ident[:])
            ins.then_inc(s_pt, 1)
            pe.transpose(banks[1][:, 0:P], u_in[:].rearrange("p m r -> p (m r)"), ident[:]).then_inc(s_pt, 1)
            pe.wait_ge(s_prep, 1)
            pe.matmul(banks[2][:, 0:D], fb_rep[:].rearrange("a m b -> a (m b)"), v_in[:],
                      start=True, stop=True).then_inc(s_m1, 1)
            pe.wait_ge(s_m1, 2)
            pe.wait_ge(s_pc, 2 + MH)
            for m in range(MH):
                ins = pe.matmul(banks[4 + m // 2][:, m % 2 * D:(m % 2 + 1) * D], u_m[:, m, :], low_v[:],
                                start=True, stop=True)
                if m % 2 == 1:
                    ins.then_inc(s_low, 1)
            pe.wait_ge(s_wolo, 1)
            for n in range(4):
                k, c = n // 2, n % 2 * GT
                if n < 2:
                    pe.wait_ge(s_w1, (n + 1) * TB)
                for m in range(TB):
                    ins = pe.transpose(banks[n][:, m * P:m * P + P], w1_low[:, n % 2 * TB + m, k * P:k * P + P],
                                       ident[:])
                ins.then_inc(s_pt, 1)
            pe.wait_ge(s_qd, 3 + KT * B)
            pe.wait_ge(ahead.s_k, ahead.SEQS * DMA)
            pe.wait_ge(s_k, (B - ahead.SEQS) * DMA)
            for c in range(CH):
                for k in range(KT):
                    for b in range(B):
                        ins = pe.matmul(scores[QR * b:QR * b + QR, c * GT:(c + 1) * GT], qd[:, k, b, :],
                                        kf[b][:, k, c * GT:(c + 1) * GT], start=(k == 0), stop=(k == KT - 1))
            ins.then_inc(s_sc, 1)
            pe.wait_ge(s_tern, 2 * (MH + KT))
            pe.wait_ge(s_pc, 2 + MH + 4)
            for n in range(4):
                for i in range(2):
                    for m in range(KT):
                        ins = pe.transpose(banks[n][:, i * D + m * P:i * D + m * P + P],
                                           w2_tern[:, m, (2 * n + i) * P:(2 * n + i + 1) * P], ident[:])
                ins.then_inc(s_pt, 1)
            pe.wait_ge(s_pc, 2 + MH + 4 + 4)
            pe.wait_ge(s_mag, 1)
            for c in range(2):
                for m in range(KT):
                    ins = pe.matmul(banks[3][:, c * D + m * P:c * D + m * P + P], ones[:], mag_diag[:, m, :],
                                    start=True, stop=True)
            ins.then_inc(s_mag, 1)

            def sums_of(n):
                pe.wait_ge(s_wt, n + 1)
                for i in range(n * TB, (n + 1) * TB):
                    for b in range(B):
                        ins = pe.matmul(sums[QR * b:QR * b + QR, 0:VROW], wt[:, i, QR * b:QR * b + QR],
                                        va[b][:, i, :], start=(i == 0), stop=(i == NB - 1))
                return ins

            pe.wait_ge(s_exp, 1)
            for n in range(NB // TB):
                wait(pe, s_wt, n - 1)
                for i in range(TB):
                    c = (n * TB + i) * P
                    ins = pe.transpose(turned[:, n % 2, i * P:(i + 1) * P], w[:, c:c + P], ident[:])
                ins.then_inc(s_turn, 1)
                if n == 0:
                    pe.wait_ge(s_v, B * DMA)
                else:
                    sums_of(n - 1)
            ins = sums_of(NB // TB - 1)
            ins.then_inc(s_sum, 1)
            pe.wait_ge(s_mag, 3)
            pe.wait_ge(s_pick, 1)
            pe.matmul(total[0:B, 0:VROW], seq_of[:], picked[:].rearrange("p h e -> p (h e)"),
                      start=True, stop=True).then_inc(s_tot, 1)


def stage_feed(nc, x, o_dram, weights, out):
    with ExitStack() as ctx:
        def sb(name, shape, dt=F32):
            return ctx.enter_context(nc.sbuf_tensor(f"f_{name}", shape, dt))

        def sem(name):
            return ctx.enter_context(nc.semaphore(f"f_{name}"))

        ident, wo_hi, wo_lo, w1_hi, w1_lo, w2_t, mag_row = (
            weights.ident, weights.wo_hi, weights.wo_lo, weights.w1_hi, weights.w1_lo, weights.w2_t, weights.mag_row)
        ob = sb("o", [P, 2, TB, D])
        ot_hi, ot_lo = sb("o_t_hi", [P, KT, GT], F32R), sb("o_t_lo", [P, KT, GT], F32R)
        xb = sb("x", [P, 4, TB, D])
        xn = sb("xn", [P, TB, D])
        xt_hi, xt_lo = sb("xt_hi", [P, 2, KT, GT], F32R), sb("xt_lo", [P, 2, KT, GT], F32R)
        r = sb("relu", [P, 4, GT])
        r2 = sb("square", [P, 4, GT])
        r2_hi, r2_lo = sb("square_hi", [P, 4, GT], F32R), sb("square_lo", [P, 4, GT], F32R)
        scaled = sb("scaled", [P, 2, 2 * D])
        banks = [ctx.enter_context(nc.psum_tensor(f"f_bank{i}", [P, GT], F32)) for i in range(8)]
        t_bank, a_bank, h_bank, y_bank = banks[0:2], banks[2:4], banks[4:6], banks[6:8]
        norm = Norm(nc, ctx, "n2")

        s_o, s_x = [sem("o_in0"), sem("o_in1")], [sem(f"x_in{i}") for i in range(4)]
        s_ot, s_oth, s_otc, s_a, s_x1 = sem("o_turned"), sem("o_high"), sem("o_low"), sem("attn"), sem("x1")
        s_xt, s_hi, s_lo = sem("xn_turned"), sem("xt_hi"), sem("xt_lo")
        s_h, s_r, s_sq, s_r2hi, s_r2lo = sem("hidden"), sem("relu"), sem("square"), sem("square_hi"), sem("square_lo")
        s_y, s_yc, s_fin = sem("y"), sem("y_scaled"), sem("final")
        s_out = [sem(f"out{i}") for i in range(4)]
        x_v = x.rearrange("b (g t p) d -> (b g) p t d", t=TB, p=P)
        out_v = out.rearrange("b (g t p) d -> (b g) p t d", t=TB, p=P)
        block = ctx.enter_context(nc.Block())
        LA, LX, LF, LB = 1, 2, 3, 4
        TURN_O, ACT_O, DVE_O = 2, 2, 2

        @block.sync
        def _(sp):
            def body(at):
                if q := at(LB):
                    sp.wait_ge(s_fin, q.g * KT + KT)
                    sp.dma_start(out_v[bass.ds(q.g, 1)].rearrange("a p t d -> (a p) t d"), xb[:, q.ring]
                                 ).then_inc(s_out[q.ring], DMA)
                if q := at(0):
                    wait(sp, s_ot, (q.g - 2) * KT + KT)
                    sp.dma_start(ob[:, q.par], o_dram[bass.ds(q.g * GT, GT), :]
                                 .rearrange("(t p) d -> p t d", p=P)).then_inc(s_o[q.par], DMA)
                    wait(sp, s_out[q.ring], q.turn * DMA)
                    sp.dma_start(xb[:, q.ring], x_v[bass.ds(q.g, 1)].rearrange("a p t d -> (a p) t d")
                                 ).then_inc(s_x[q.ring], DMA)

            sweep(sp, body, LB)
            for i in range(4):
                sp.wait_ge(s_out[i], DMA * (G // 4))

        @block.gpsimd
        def _(pool):
            def body(at):
                if q := at(LF):
                    for j in range(MH):
                        pool.wait_ge(s_r, q.g * MH + j + 1)
                        wait(pool, s_r2lo, q.g * MH + j + 1 - 4)
                        pool.tensor_tensor(r2[:, j % 4, :], r[:, j % 4, :], r[:, j % 4, :], ALU.mult
                                           ).then_inc(s_sq, 1)

            sweep(pool, body, LB)

        @block.tensor
        def _(pe):
            def body(at):
                qa, qx, qf, qb = at(LA), at(LX), at(LF), at(LB)

                def turn_o():
                    if not qa:
                        return
                    pe.wait_ge(s_o[qa.par], (qa.half + 1) * DMA)
                    for k in range(KT):
                        if isinstance(qa.g, int) and qa.g < 2:
                            wait(pe, s_otc, (qa.g - 1) * KT + k + 1)
                        wait(pe, s_lo, (qa.g - 2) * KT + k + 1)
                        for t in range(TB):
                            ins = pe.transpose(t_bank[k][:, t * P:t * P + P], ob[:, qa.par, t, k * P:k * P + P],
                                               ident[:])
                        ins.then_inc(s_ot, 1)

                def turn_norm():
                    if not qx:
                        return
                    pe.wait_ge(norm.s_back, norm.done(qx))
                    for k in range(KT):
                        if qa:
                            pe.wait_ge(s_otc, qa.g * KT + k + 1)
                        else:
                            wait(pe, s_lo, (qx.g - 1) * KT + k + 1)
                        for t in range(TB):
                            ins = pe.transpose(t_bank[k][:, t * P:t * P + P], xn[:, t, k * P:k * P + P], ident[:])
                        ins.then_inc(s_xt, 1)

                def attention_product():
                    if not qa:
                        return
                    pe.wait_ge(s_otc, qa.g * KT + KT)
                    for c in range(2):
                        wait(pe, s_x1, (qa.g - 1) * 2 + c + 1)
                        for t in range(2):
                            cut = slice((2 * c + t) * P, (2 * c + t + 1) * P)
                            ins = three_pass(pe, a_bank[c][:, t * D:t * D + D],
                                             [ot_hi[:, k, cut] for k in range(KT)],
                                             [ot_lo[:, k, cut] for k in range(KT)],
                                             [wo_hi[:, k, :] for k in range(KT)], [wo_lo[:, k, :] for k in range(KT)])
                        ins.then_inc(s_a, 1)

                def hidden(j):
                    if not qf:
                        return
                    if j == 0:
                        pe.wait_ge(s_lo, qf.g * KT + KT)
                    wait(pe, s_r, qf.g * MH + j - 1)
                    three_pass(pe, h_bank[j % 2][:], [w1_hi[:, k, j * P:j * P + P] for k in range(KT)],
                               [w1_lo[:, k, j * P:j * P + P] for k in range(KT)],
                               [xt_hi[:, qf.par, k, :] for k in range(KT)],
                               [xt_lo[:, qf.par, k, :] for k in range(KT)]).then_inc(s_h, 1)

                def output(j):
                    if not qf:
                        return
                    pe.wait_ge(s_r2lo, qf.g * MH + j + 1)
                    for c in range(2):
                        if j == 0:
                            wait(pe, s_yc, (qf.g - 1) * 2 + c + 1)
                        for t in range(2):
                            cut, y = slice((2 * c + t) * P, (2 * c + t + 1) * P), y_bank[c][:, t * D:t * D + D]
                            pe.matmul(y, r2_hi[:, j % 4, cut], w2_t[:, j, :], start=(j == 0 and t == 0), stop=False,
                                      skip_group_check=True)
                            ins = pe.matmul(y, r2_lo[:, j % 4, cut], w2_t[:, j, :], start=False, stop=(j == MH - 1),
                                            skip_group_check=True)
                    ins.then_inc(s_y, 1)

                hidden(0)
                hidden(1)
                for j in range(2, MH):
                    hidden(j)
                    if j == TURN_O:
                        turn_o()
                    output(j - 2)
                turn_norm()
                output(MH - 2)
                attention_product()
                output(MH - 1)

            sweep(pe, body, LB)

        @block.scalar
        def _(act):
            def squares(q, j):
                wait(act, s_y, q.g * MH + j + 1 - 4)
                act.activation(r[:, j % 4, :], h_bank[j % 2][:], ACT.Relu).then_inc(s_r, 1)
                act.wait_ge(s_r, q.g * MH + j + 1)
                act.activation(r2_hi[:, j % 4, :], r[:, j % 4, :], ACT.Square).then_inc(s_r2hi, 1)

            def body(at):
                qa, qx, qf, qb = at(LA), at(LX), at(LF), at(LB)
                for j in range(MH):
                    if qf:
                        act.wait_ge(s_h, qf.g * MH + j + 1)
                        wait(act, s_sq, qf.g * MH + j + 1 - 4)
                        squares(qf, j)
                    if j == ACT_O and qa:
                        for k in range(KT):
                            act.wait_ge(s_ot, qa.g * KT + k + 1)
                            wait(act, s_a, (qa.g - 1) * 2 + 2)
                            act.activation(ot_hi[:, k, :], t_bank[k][:], ACT.Copy).then_inc(s_oth, 1)
                    if j == 3 and qx:
                        norm.root(act, qx)
                if qx:
                    for k in range(KT):
                        act.wait_ge(s_xt, qx.g * KT + k + 1)
                        wait(act, s_h, (qx.g - 2) * MH + MH)
                        act.activation(xt_hi[:, qx.par, k, :], t_bank[k][:], ACT.Copy).then_inc(s_hi, 1)

            sweep(act, body, LB)

        @block.vector
        def _(dve):
            norm.begin(dve)
            def low_of_squares(q, j):
                dve.wait_ge(s_r2hi, q.g * MH + j + 1)
                dve.wait_ge(s_sq, q.g * MH + j + 1)
                dve.tensor_tensor(r2_lo[:, j % 4, :], r2[:, j % 4, :], r2_hi[:, j % 4, :].bitcast(F32), ALU.subtract
                                  ).then_inc(s_r2lo, 1)

            def body(at):
                qa, qx, qf, qb = at(LA), at(LX), at(LF), at(LB)
                if qb:
                    dve.wait_ge(s_y, qb.g * MH + MH)
                    for c in range(2):
                        dve.tensor_tensor(scaled[:, c], y_bank[c][:], mag_row[:], ALU.mult).then_inc(s_yc, 1)
                    for c in range(2):
                        dve.wait_ge(s_yc, qb.g * 2 + c + 1)
                        rows = xb[:, qb.ring, 2 * c:2 * c + 2, :].rearrange("p t d -> p (t d)")
                        dve.tensor_tensor(rows, scaled[:, c], rows, ALU.add).then_inc(s_fin, 1)
                for j in range(MH):
                    if qf:
                        low_of_squares(qf, j)
                    if j == DVE_O and qa:
                        for k in range(KT):
                            dve.wait_ge(s_oth, qa.g * KT + k + 1)
                            dve.tensor_tensor(ot_lo[:, k, :], t_bank[k][:], ot_hi[:, k, :].bitcast(F32),
                                              ALU.subtract).then_inc(s_otc, 1)
                    if j == 1 and qx:
                        dve.wait_ge(s_x1, qx.g * 2 + 2)
                        norm.front(dve, xb[:, qx.ring], qx)
                    if j == 3 and qx:
                        wait(dve, s_xt, (qx.g - 1) * KT + KT)
                        norm.back(dve, xb[:, qx.ring], xn[:], qx)
                if qx:
                    for k in range(KT):
                        dve.wait_ge(s_hi, qx.g * KT + k + 1)
                        dve.tensor_tensor(xt_lo[:, qx.par, k, :], t_bank[k][:],
                                          xt_hi[:, qx.par, k, :].bitcast(F32), ALU.subtract).then_inc(s_lo, 1)
                if qa:
                    dve.wait_ge(s_x[qa.ring], (qa.turn + 1) * DMA)
                    for c in range(2):
                        dve.wait_ge(s_a, qa.g * 2 + c + 1)
                        rows = xb[:, qa.ring, 2 * c:2 * c + 2, :].rearrange("p t d -> p (t d)")
                        dve.tensor_tensor(rows, a_bank[c][:], rows, ALU.add).then_inc(s_x1, 1)

            sweep(dve, body, LB)


def layer(nc, x, wq, wk, wv, wo, fast_b, w_fc, w_proj, u, v, gate, out):
    qk_dram = nc.dram_tensor("qk_parts", [2, D, 3, N], BF16, kind="Internal").ap()
    kf_dram = nc.dram_tensor("k_whole", [D, N], F32, kind="Internal").ap()
    va_dram = nc.dram_tensor("v_ones", [N, VROW], F32, kind="Internal").ap()
    o_dram = nc.dram_tensor("attention", [N, D], F32, kind="Internal").ap()
    stage_project(nc, x, (wq, wk, wv), qk_dram, kf_dram, va_dram)
    with ExitStack() as ctx:
        ahead = Ahead(nc, ctx, kf_dram, wo, fast_b, w_fc, u, v, gate)
        stage_attend(nc, qk_dram, va_dram, o_dram, ahead)
        weights = Weights(nc, ctx)
        stage_row_zero(nc, qk_dram, kf_dram, va_dram, o_dram, w_proj, ahead, weights)
        stage_feed(nc, x, o_dram, weights, out)


_INS = ["x", "Wq", "Wk", "Wv", "Wo", "fast_b", "w_fc", "w_proj", "u", "v", "gate"]


def kernel(**inputs):
    import concourse.bacc as bacc
    from concourse.bass_utils import run_bass_kernel_spmd

    nc = bacc.Bacc("TRN2", target_bir_lowering=False, num_devices=1)
    arrays, args = {}, []
    for name in _INS:
        key = ("L0_attn_" if name[0] == "W" or name == "x" else "L0_ffn_") + name
        a = np.ascontiguousarray(inputs[key])
        if a.ndim == 0:
            a = a.reshape(1)
        arrays[f"in_{name}"] = a
        args.append(nc.dram_tensor(f"in_{name}", a.shape, mybir.dt.from_np(a.dtype), kind="ExternalInput").ap())
    out = nc.dram_tensor("out", (B, T, D), F32, kind="ExternalOutput").ap()
    layer(nc, *args, out)
    r = run_bass_kernel_spmd(nc, [arrays], core_ids=[0])
    return r.results[0]["out"]
```
